# Optimizing a Trainium2 kernel written in Bass

```python
import numpy as np
import jax
import jax.numpy as jnp

def _softmax(x, axis=-1):
    return jax.nn.softmax(x, axis=axis)

def _gelu(x):
    return jax.nn.gelu(x, approximate=True)

def _silu(x):
    return jax.nn.silu(x)

def _sigmoid(x):
    return jax.nn.sigmoid(x)

def _layernorm(x, axis=-1, eps=1e-05):
    m = jnp.mean(x, axis=axis, keepdims=True)
    v = jnp.var(x, axis=axis, keepdims=True)
    return (x - m) / jnp.sqrt(v + eps)

def _scatter_add(tgt, idx, src, axis=0):
    return tgt.at[idx].add(src)

def _segment_sum(src, seg, n):
    return jax.ops.segment_sum(src, seg, n)
kernel_name = 'mk_xattn_ffn_d4_seqx_r8_f6e894'

def setup_inputs(seed: int=0):
    np.random.seed(seed)
    _w = jnp.asarray

    def _rec_inputs():
        import jax
        import jax.numpy as jnp
        _rk = jax.random.key(seed)
        x = -9.806e-05 + 1 * jax.random.normal(jax.random.fold_in(_rk, 1), (128, 64, 128), jnp.float32)
        _lenS = 64 - jax.random.randint(jax.random.fold_in(_rk, 7), (128,), 0, max(1, 64 // 4) + 1, jnp.int32)
        _lenS2 = 64 - jax.random.randint(jax.random.fold_in(_rk, 8), (128,), 0, max(1, 64 // 4) + 1, jnp.int32)
        _ctx_1024P = jax.random.normal(jax.random.fold_in(_rk, 11), (128, 16, 128), jnp.float32)
        _ctx_1024c = jax.random.dirichlet(jax.random.fold_in(_rk, 511), 0.3 * jnp.ones((16,), jnp.float32), (128, 64))
        _ctx_1024t = jnp.einsum('bsk,bkd->bsd', _ctx_1024c, _ctx_1024P)
        _ctx_1024t = _ctx_1024t * jax.lax.rsqrt(jnp.mean(jnp.square(_ctx_1024t)) + 1e-12) * 0.953939
        ctx_1024 = -1.52775e-05 + 0.999936 * (_ctx_1024t + 0.3 * jax.random.normal(jax.random.fold_in(_rk, 611), (128, 64, 128), jnp.float32))
        _validS = jnp.arange(64)[None, :] < _lenS[:, None]
        _validS2 = jnp.arange(64)[None, :] < _lenS2[:, None]
        _causal = jnp.tril(jnp.ones((64, 64), dtype=bool))
        mask_SxS2_bk1 = jnp.broadcast_to(_validS2[0:1, :], (64, 64))
        return (x, ctx_1024, mask_SxS2_bk1)
    x, ctx_1024, mask_SxS2_bk1 = _rec_inputs()

    def _L0_xattn_setup():
        import jax, jax.numpy as jnp
        import numpy as np
        D = 128
        NUM_ITERS = 3
        EPS = 1e-06
        SCALE = D ** (-0.5)

        def rmsnorm(x, w, eps=EPS):
            return x * jax.lax.rsqrt(jnp.mean(x * x, axis=-1, keepdims=True) + eps) * w

        def gru_cell(x, h, wih, whh, bih, bhh):
            gx = x @ wih.T + bih
            gh = h @ whh.T + bhh
            xr, xz, xn = jnp.split(gx, 3, axis=-1)
            hr, hz, hn = jnp.split(gh, 3, axis=-1)
            r = jax.nn.sigmoid(xr + hr)
            z = jax.nn.sigmoid(xz + hz)
            n = jnp.tanh(xn + r * hn)
            return (1.0 - z) * n + z * h
        key = jax.random.key(seed)
        ks = jax.random.split(key, 8)
        B, K, M, d = (8, 64, 512, D)
        w_std = d ** (-0.5)
        return {'slots': jax.random.normal(ks[0], (B, K, d), jnp.float32), 'P': jax.random.normal(ks[1], (B, M, d), jnp.float32), 'Wq': jax.random.normal(ks[2], (d, d), jnp.float32) * w_std, 'Wk': jax.random.normal(ks[3], (d, d), jnp.float32) * w_std, 'Wv': jax.random.normal(ks[4], (d, d), jnp.float32) * w_std, 'gru_wih': jax.random.normal(ks[5], (3 * d, d), jnp.float32) * w_std, 'gru_whh': jax.random.normal(ks[6], (3 * d, d), jnp.float32) * w_std, 'gru_bih': jnp.zeros((3 * d,), jnp.float32), 'gru_bhh': jnp.zeros((3 * d,), jnp.float32), 'slot_norm_w': jnp.ones((d,), jnp.float32), 'input_norm_w': jnp.ones((d,), jnp.float32)}
    _L0_xattn_all = _L0_xattn_setup()
    _L0_xattn_in = {k: v for k, v in _L0_xattn_all.items() if k in ('Wq', 'Wk', 'Wv', 'gru_wih', 'gru_whh', 'gru_bih', 'gru_bhh', 'slot_norm_w', 'input_norm_w')}
    del _L0_xattn_all

    def _L0_ffn_setup():
        import jax, jax.numpy as jnp
        import numpy as np
        E, D, F, GATE_DIM = (8, 128, 512, 16)
        B, T = (2, 256)
        key = jax.random.key(seed)
        ks = jax.random.split(key, 7)
        s = 0.02
        return {'hidden_states': jax.random.normal(ks[0], (B, T, D), dtype=jnp.float32), 'w_red': jax.random.normal(ks[1], (D, GATE_DIM), dtype=jnp.float32) * s, 'wg': jax.random.normal(ks[2], (E, GATE_DIM), dtype=jnp.float32), 'w1': jax.random.normal(ks[3], (E, D, F), dtype=jnp.float32) * s, 'b1': jax.random.normal(ks[4], (E, F), dtype=jnp.float32) * s, 'w2': jax.random.normal(ks[5], (E, F, D), dtype=jnp.float32) * s, 'b2': jax.random.normal(ks[6], (E, D), dtype=jnp.float32) * s}
    _L0_ffn_all = _L0_ffn_setup()
    _L0_ffn_in = {k: v for k, v in _L0_ffn_all.items() if k in ('w_red', 'wg', 'w1', 'b1', 'w2', 'b2')}
    del _L0_ffn_all

    def _L1_xattn_setup():
        import jax, jax.numpy as jnp
        import numpy as np
        DIM = 128
        N_HEADS = 16
        HEAD_DIM = DIM // N_HEADS
        EPS = 1e-06
        Q_THETA = 32.0
        K_THETA = 1000.0

        def precompute_freqs_1d(dim, seq_len, theta):
            freqs = theta ** (-jnp.arange(0, dim, 2, dtype=jnp.float32) / dim)
            t = jnp.arange(seq_len, dtype=jnp.float32)
            ang = t[:, None] * freqs[None, :]
            return (jnp.cos(ang), jnp.sin(ang))

        def rms_norm(x, w):
            var = jnp.mean(x * x, axis=-1, keepdims=True)
            return x * jax.lax.rsqrt(var + EPS) * w

        def apply_rope(t, cos, sin):
            cos = cos[None, None, :, :]
            sin = sin[None, None, :, :]
            t1, t2 = jnp.split(t, 2, axis=-1)
            return jnp.concatenate([t1 * cos - t2 * sin, t2 * cos + t1 * sin], axis=-1)
        key = jax.random.key(seed)
        ks = jax.random.split(key, 8)
        B, T, S = (128, 64, 48)
        s = 1.0 / np.sqrt(DIM)
        return {'x': jax.random.normal(ks[0], (B, T, DIM), jnp.float32), 'context': jax.random.normal(ks[1], (B, S, DIM), jnp.float32), 'Wq': jax.random.normal(ks[2], (DIM, DIM), jnp.float32) * s, 'Wk': jax.random.normal(ks[3], (DIM, DIM), jnp.float32) * s, 'Wv': jax.random.normal(ks[4], (DIM, DIM), jnp.float32) * s, 'Wo': jax.random.normal(ks[5], (DIM, DIM), jnp.float32) * s, 'q_norm_w': jnp.ones((HEAD_DIM,), jnp.float32), 'k_norm_w': jnp.ones((HEAD_DIM,), jnp.float32)}
    _L1_xattn_all = _L1_xattn_setup()
    _L1_xattn_in = {k: v for k, v in _L1_xattn_all.items() if k in ('Wq', 'Wk', 'Wv', 'Wo', 'q_norm_w', 'k_norm_w')}
    del _L1_xattn_all

    def _L1_ffn_setup():
        import jax, jax.numpy as jnp
        import numpy as np
        LN_EPS = 1e-05

        def _layernorm(x, g, b):
            m = jnp.mean(x, axis=-1, keepdims=True)
            v = jnp.mean(jnp.square(x - m), axis=-1, keepdims=True)
            return (x - m) * jax.lax.rsqrt(v + LN_EPS) * g + b
        K_TOP = 2
        key = jax.random.key(seed)
        ks = jax.random.split(key, 4)
        B, N, D, E = (8, 256, 128, 4)
        s = 0.02
        return {'x': jax.random.normal(ks[0], (B, N, D), dtype=jnp.float32), 'gate_W': jax.random.normal(ks[1], (D, E), dtype=jnp.float32) * s, 'gate_b': jnp.zeros((E,), jnp.float32), 'W1': jax.random.normal(ks[2], (E, D, D), dtype=jnp.float32) * s, 'b1': jnp.zeros((E, D), jnp.float32), 'g1': jnp.ones((E, D), jnp.float32), 'be1': jnp.zeros((E, D), jnp.float32), 'W2': jax.random.normal(ks[3], (E, D, D), dtype=jnp.float32) * s, 'b2': jnp.zeros((E, D), jnp.float32), 'g2': jnp.ones((E, D), jnp.float32), 'be2': jnp.zeros((E, D), jnp.float32)}
    _L1_ffn_all = _L1_ffn_setup()
    _L1_ffn_in = {k: v for k, v in _L1_ffn_all.items() if k in ('gate_W', 'gate_b', 'W1', 'b1', 'g1', 'be1', 'W2', 'b2', 'g2', 'be2')}
    del _L1_ffn_all

    def _L2_xattn_setup():
        import jax, jax.numpy as jnp
        import numpy as np
        B, S, D, H = (2, 256, 128, 16)
        HD = D // H

        def _split_heads(x):
            b, s, _ = x.shape
            return x.reshape(b, s, H, HD).transpose(0, 2, 1, 3)
        key = jax.random.key(seed)
        ks = jax.random.split(key, 12)
        s = 1.0 / np.sqrt(D)
        inp = {'queries': jax.random.normal(ks[0], (B, S, D), jnp.float32), 'keys': jax.random.normal(ks[1], (B, S, D), jnp.float32), 'values': jax.random.normal(ks[2], (B, S, D), jnp.float32), 'attn_mask': jnp.triu(jnp.ones((S, S), bool), k=1), 'W_q': jax.random.normal(ks[3], (D, D), jnp.float32) * s, 'b_q': jnp.zeros((D,), jnp.float32), 'W_k': jax.random.normal(ks[4], (D, D), jnp.float32) * s, 'b_k': jnp.zeros((D,), jnp.float32), 'W_v': jax.random.normal(ks[5], (D, D), jnp.float32) * s, 'b_v': jnp.zeros((D,), jnp.float32), 'W_o': jax.random.normal(ks[6], (D, D), jnp.float32) * s, 'b_o': jnp.zeros((D,), jnp.float32)}
        return inp
    _L2_xattn_all = _L2_xattn_setup()
    _L2_xattn_in = {k: v for k, v in _L2_xattn_all.items() if k in ('W_q', 'b_q', 'W_k', 'b_k', 'W_v', 'b_v', 'W_o', 'b_o')}
    del _L2_xattn_all

    def _L2_ffn_setup():
        import jax, jax.numpy as jnp
        import numpy as np
        D_MODEL = 128
        D_FF = 512
        N_EXPERTS = 8
        INIT_SCALE = 0.1

        def _trunc_normal(key, shape, std):
            return std * jax.random.truncated_normal(key, -2.0, 2.0, shape, dtype=jnp.float32)
        key = jax.random.key(seed)
        ks = jax.random.split(key, 5)
        x = jax.random.normal(ks[0], (4, 128, D_MODEL), dtype=jnp.float32)
        router_W = _trunc_normal(ks[1], (D_MODEL, N_EXPERTS), INIT_SCALE / np.sqrt(D_MODEL))
        router_b = jnp.zeros((N_EXPERTS,), dtype=jnp.float32)
        W1 = _trunc_normal(ks[2], (N_EXPERTS, D_MODEL, D_FF), INIT_SCALE / np.sqrt(D_MODEL))
        b1 = jnp.zeros((N_EXPERTS, D_FF), dtype=jnp.float32)
        W2 = _trunc_normal(ks[3], (N_EXPERTS, D_FF, D_MODEL), INIT_SCALE / np.sqrt(D_FF))
        b2 = jnp.zeros((N_EXPERTS, D_MODEL), dtype=jnp.float32)
        return {'x': x, 'router_W': router_W, 'router_b': router_b, 'W1': W1, 'b1': b1, 'W2': W2, 'b2': b2}
    _L2_ffn_all = _L2_ffn_setup()
    _L2_ffn_in = {k: v for k, v in _L2_ffn_all.items() if k in ('router_W', 'router_b', 'W1', 'b1', 'W2', 'b2')}
    del _L2_ffn_all

    def _L3_xattn_setup():
        import jax, jax.numpy as jnp
        import numpy as np
        import math
        H = 16

        def _split_heads(x):
            b, n, hd = x.shape
            return x.reshape(b, n, H, hd // H).transpose(0, 2, 1, 3)
        key = jax.random.key(seed)
        ks = jax.random.split(key, 5)
        D = 128
        s = 1.0 / math.sqrt(D)
        return {'hidden_states': jax.random.normal(ks[0], (8, 128, D), dtype=jnp.float32), 'context_states': jax.random.normal(ks[1], (8, 32, D), dtype=jnp.float32), 'Wq': jax.random.normal(ks[2], (D, D), dtype=jnp.float32) * s, 'bq': jnp.zeros((D,), dtype=jnp.float32), 'Wk': jax.random.normal(ks[3], (D, D), dtype=jnp.float32) * s, 'bk': jnp.zeros((D,), dtype=jnp.float32), 'Wv': jax.random.normal(ks[4], (D, D), dtype=jnp.float32) * s, 'bv': jnp.zeros((D,), dtype=jnp.float32)}
    _L3_xattn_all = _L3_xattn_setup()
    _L3_xattn_in = {k: v for k, v in _L3_xattn_all.items() if k in ('Wq', 'bq', 'Wk', 'bk', 'Wv', 'bv')}
    del _L3_xattn_all

    def _L3_ffn_setup():
        import jax, jax.numpy as jnp
        import numpy as np
        B, S, D, H, E = (4, 256, 128, 512, 8)
        key = jax.random.key(seed)
        ks = jax.random.split(key, 8)
        s_d = 1.0 / np.sqrt(D)
        s_h = 1.0 / np.sqrt(H)
        return {'x': jax.random.normal(ks[0], (B, S, D), dtype=jnp.float32), 'gate_w': jax.random.uniform(ks[1], (E, D), jnp.float32, -s_d, s_d), 'gate_b': jax.random.uniform(ks[2], (E,), jnp.float32, -s_d, s_d), 'w1': jax.random.uniform(ks[3], (E, H, D), jnp.float32, -s_d, s_d), 'b1': jax.random.uniform(ks[4], (E, H), jnp.float32, -s_d, s_d), 'w2': jax.random.uniform(ks[5], (E, D, H), jnp.float32, -s_h, s_h), 'b2': jax.random.uniform(ks[6], (E, D), jnp.float32, -s_h, s_h)}
    _L3_ffn_all = _L3_ffn_setup()
    _L3_ffn_in = {k: v for k, v in _L3_ffn_all.items() if k in ('gate_w', 'gate_b', 'w1', 'b1', 'w2', 'b2')}
    del _L3_ffn_all
    return {'x': x, 'ctx_1024': ctx_1024, 'mask_SxS2_bk1': mask_SxS2_bk1, 'L0_xattn_Wq': _L0_xattn_in['Wq'], 'L0_xattn_Wk': _L0_xattn_in['Wk'], 'L0_xattn_Wv': _L0_xattn_in['Wv'], 'L0_xattn_gru_wih': _L0_xattn_in['gru_wih'], 'L0_xattn_gru_whh': _L0_xattn_in['gru_whh'], 'L0_xattn_gru_bih': _L0_xattn_in['gru_bih'], 'L0_xattn_gru_bhh': _L0_xattn_in['gru_bhh'], 'L0_xattn_slot_norm_w': _L0_xattn_in['slot_norm_w'], 'L0_xattn_input_norm_w': _L0_xattn_in['input_norm_w'], 'L0_ffn_w_red': _L0_ffn_in['w_red'], 'L0_ffn_wg': _L0_ffn_in['wg'], 'L0_ffn_w1': _L0_ffn_in['w1'], 'L0_ffn_b1': _L0_ffn_in['b1'], 'L0_ffn_w2': _L0_ffn_in['w2'], 'L0_ffn_b2': _L0_ffn_in['b2'], 'L1_xattn_Wq': _L1_xattn_in['Wq'], 'L1_xattn_Wk': _L1_xattn_in['Wk'], 'L1_xattn_Wv': _L1_xattn_in['Wv'], 'L1_xattn_Wo': _L1_xattn_in['Wo'], 'L1_xattn_q_norm_w': _L1_xattn_in['q_norm_w'], 'L1_xattn_k_norm_w': _L1_xattn_in['k_norm_w'], 'L1_ffn_gate_W': _L1_ffn_in['gate_W'], 'L1_ffn_gate_b': _L1_ffn_in['gate_b'], 'L1_ffn_W1': _L1_ffn_in['W1'], 'L1_ffn_b1': _L1_ffn_in['b1'], 'L1_ffn_g1': _L1_ffn_in['g1'], 'L1_ffn_be1': _L1_ffn_in['be1'], 'L1_ffn_W2': _L1_ffn_in['W2'], 'L1_ffn_b2': _L1_ffn_in['b2'], 'L1_ffn_g2': _L1_ffn_in['g2'], 'L1_ffn_be2': _L1_ffn_in['be2'], 'L2_xattn_W_q': _L2_xattn_in['W_q'], 'L2_xattn_b_q': _L2_xattn_in['b_q'], 'L2_xattn_W_k': _L2_xattn_in['W_k'], 'L2_xattn_b_k': _L2_xattn_in['b_k'], 'L2_xattn_W_v': _L2_xattn_in['W_v'], 'L2_xattn_b_v': _L2_xattn_in['b_v'], 'L2_xattn_W_o': _L2_xattn_in['W_o'], 'L2_xattn_b_o': _L2_xattn_in['b_o'], 'L2_ffn_router_W': _L2_ffn_in['router_W'], 'L2_ffn_router_b': _L2_ffn_in['router_b'], 'L2_ffn_W1': _L2_ffn_in['W1'], 'L2_ffn_b1': _L2_ffn_in['b1'], 'L2_ffn_W2': _L2_ffn_in['W2'], 'L2_ffn_b2': _L2_ffn_in['b2'], 'L3_xattn_Wq': _L3_xattn_in['Wq'], 'L3_xattn_bq': _L3_xattn_in['bq'], 'L3_xattn_Wk': _L3_xattn_in['Wk'], 'L3_xattn_bk': _L3_xattn_in['bk'], 'L3_xattn_Wv': _L3_xattn_in['Wv'], 'L3_xattn_bv': _L3_xattn_in['bv'], 'L3_ffn_gate_w': _L3_ffn_in['gate_w'], 'L3_ffn_gate_b': _L3_ffn_in['gate_b'], 'L3_ffn_w1': _L3_ffn_in['w1'], 'L3_ffn_b1': _L3_ffn_in['b1'], 'L3_ffn_w2': _L3_ffn_in['w2'], 'L3_ffn_b2': _L3_ffn_in['b2']}

def reference(x, ctx_1024, mask_SxS2_bk1, L0_xattn_Wq, L0_xattn_Wk, L0_xattn_Wv, L0_xattn_gru_wih, L0_xattn_gru_whh, L0_xattn_gru_bih, L0_xattn_gru_bhh, L0_xattn_slot_norm_w, L0_xattn_input_norm_w, L0_ffn_w_red, L0_ffn_wg, L0_ffn_w1, L0_ffn_b1, L0_ffn_w2, L0_ffn_b2, L1_xattn_Wq, L1_xattn_Wk, L1_xattn_Wv, L1_xattn_Wo, L1_xattn_q_norm_w, L1_xattn_k_norm_w, L1_ffn_gate_W, L1_ffn_gate_b, L1_ffn_W1, L1_ffn_b1, L1_ffn_g1, L1_ffn_be1, L1_ffn_W2, L1_ffn_b2, L1_ffn_g2, L1_ffn_be2, L2_xattn_W_q, L2_xattn_b_q, L2_xattn_W_k, L2_xattn_b_k, L2_xattn_W_v, L2_xattn_b_v, L2_xattn_W_o, L2_xattn_b_o, L2_ffn_router_W, L2_ffn_router_b, L2_ffn_W1, L2_ffn_b1, L2_ffn_W2, L2_ffn_b2, L3_xattn_Wq, L3_xattn_bq, L3_xattn_Wk, L3_xattn_bk, L3_xattn_Wv, L3_xattn_bv, L3_ffn_gate_w, L3_ffn_gate_b, L3_ffn_w1, L3_ffn_b1, L3_ffn_w2, L3_ffn_b2):
    import jax
    import jax.numpy as jnp

    def _L0_xattn_ref(slots, P, Wq, Wk, Wv, gru_wih, gru_whh, gru_bih, gru_bhh, slot_norm_w, input_norm_w):
        import jax, jax.numpy as jnp
        import numpy as np
        D = 128
        NUM_ITERS = 3
        EPS = 1e-06
        SCALE = D ** (-0.5)

        def rmsnorm(x, w, eps=EPS):
            return x * jax.lax.rsqrt(jnp.mean(x * x, axis=-1, keepdims=True) + eps) * w

        def gru_cell(x, h, wih, whh, bih, bhh):
            gx = x @ wih.T + bih
            gh = h @ whh.T + bhh
            xr, xz, xn = jnp.split(gx, 3, axis=-1)
            hr, hz, hn = jnp.split(gh, 3, axis=-1)
            r = jax.nn.sigmoid(xr + hr)
            z = jax.nn.sigmoid(xz + hz)
            n = jnp.tanh(xn + r * hn)
            return (1.0 - z) * n + z * h
        Pn = rmsnorm(P, input_norm_w)
        k_proj = Pn @ Wk.T
        v_proj = Pn @ Wv.T
        for _ in range(NUM_ITERS):
            sn = rmsnorm(slots, slot_norm_w)
            q_proj = sn @ Wq.T
            scores = jnp.einsum('bkd,bmd->bkm', q_proj, k_proj) * SCALE
            attn = jax.nn.softmax(scores, axis=-2)
            attn = attn / (jnp.sum(attn, axis=-1, keepdims=True) + EPS)
            updates = jnp.einsum('bkm,bmd->bkd', attn, v_proj)
            slots = gru_cell(updates, slots, gru_wih, gru_whh, gru_bih, gru_bhh)
        return slots

    def _L0_ffn_ref(hidden_states, w_red, wg, w1, b1, w2, b2):
        import jax, jax.numpy as jnp
        import numpy as np
        E, D, F, GATE_DIM = (8, 128, 512, 16)
        B, T = (2, 256)
        b, t, c = hidden_states.shape
        x = hidden_states.reshape(-1, c)
        red = x @ w_red
        wg_n = wg / jnp.maximum(jnp.linalg.norm(wg, axis=1, keepdims=True), 0.0001)
        logits = red @ wg_n.T
        gates = jax.nn.softmax(logits, axis=1)
        idx = jnp.argmax(gates, axis=1)
        scores = jnp.take_along_axis(gates, idx[:, None], axis=1)
        h = jax.nn.gelu(jnp.einsum('td,edf->etf', x, w1) + b1[:, None, :], approximate=False)
        y = jnp.einsum('etf,efd->etd', h, w2) + b2[:, None, :]
        out = jnp.take_along_axis(y, idx[None, :, None], axis=0)[0]
        out = out * scores
        return out.reshape(b, t, c)

    def _L1_xattn_ref(x, context, Wq, Wk, Wv, Wo, q_norm_w, k_norm_w):
        import jax, jax.numpy as jnp
        import numpy as np
        DIM = 128
        N_HEADS = 16
        HEAD_DIM = DIM // N_HEADS
        EPS = 1e-06
        Q_THETA = 32.0
        K_THETA = 1000.0

        def precompute_freqs_1d(dim, seq_len, theta):
            freqs = theta ** (-jnp.arange(0, dim, 2, dtype=jnp.float32) / dim)
            t = jnp.arange(seq_len, dtype=jnp.float32)
            ang = t[:, None] * freqs[None, :]
            return (jnp.cos(ang), jnp.sin(ang))

        def rms_norm(x, w):
            var = jnp.mean(x * x, axis=-1, keepdims=True)
            return x * jax.lax.rsqrt(var + EPS) * w

        def apply_rope(t, cos, sin):
            cos = cos[None, None, :, :]
            sin = sin[None, None, :, :]
            t1, t2 = jnp.split(t, 2, axis=-1)
            return jnp.concatenate([t1 * cos - t2 * sin, t2 * cos + t1 * sin], axis=-1)
        B, T, C = x.shape
        S = context.shape[1]
        H, D = (N_HEADS, HEAD_DIM)
        q = (x @ Wq.T).reshape(B, T, H, D).transpose(0, 2, 1, 3)
        k = (context @ Wk.T).reshape(B, S, H, D).transpose(0, 2, 1, 3)
        v = (context @ Wv.T).reshape(B, S, H, D).transpose(0, 2, 1, 3)
        q = rms_norm(q, q_norm_w)
        k = rms_norm(k, k_norm_w)
        q_cos, q_sin = precompute_freqs_1d(D, T, Q_THETA)
        k_cos, k_sin = precompute_freqs_1d(D, S, K_THETA)
        q = apply_rope(q, q_cos, q_sin)
        k = apply_rope(k, k_cos, k_sin)
        scale = D ** (-0.5)
        attn = jnp.einsum('bhtd,bhsd->bhts', q, k) * scale
        attn = jax.nn.softmax(attn, axis=-1)
        out = jnp.einsum('bhts,bhsd->bhtd', attn, v)
        out = out.transpose(0, 2, 1, 3).reshape(B, T, C)
        return out @ Wo.T

    def _L1_ffn_ref(x, gate_W, gate_b, W1, b1, g1, be1, W2, b2, g2, be2):
        import jax, jax.numpy as jnp
        import numpy as np
        LN_EPS = 1e-05

        def _layernorm(x, g, b):
            m = jnp.mean(x, axis=-1, keepdims=True)
            v = jnp.mean(jnp.square(x - m), axis=-1, keepdims=True)
            return (x - m) * jax.lax.rsqrt(v + LN_EPS) * g + b
        K_TOP = 2
        B, N, D = x.shape
        BN = B * N
        xf = x.reshape(BN, D)
        gate_scores = xf @ gate_W + gate_b
        topk_scores, topk_idx = jax.lax.top_k(gate_scores, K_TOP)
        weights = jax.nn.softmax(topk_scores, axis=-1)

        def expert(w1, bb1, gg1, bbe1, w2, bb2, gg2, bbe2):
            h = jax.nn.relu(_layernorm(xf @ w1 + bb1, gg1, bbe1))
            return _layernorm(h @ w2 + bb2, gg2, bbe2)
        all_out = jax.vmap(expert)(W1, b1, g1, be1, W2, b2, g2, be2)
        exp_out = all_out[topk_idx, jnp.arange(BN)[:, None]]
        out = jnp.sum(weights[..., None] * exp_out, axis=1)
        return (out + xf).reshape(B, N, D)

    def _L2_xattn_ref(queries, keys, values, attn_mask, W_q, b_q, W_k, b_k, W_v, b_v, W_o, b_o):
        import jax, jax.numpy as jnp
        import numpy as np
        B, S, D, H = (2, 256, 128, 16)
        HD = D // H

        def _split_heads(x):
            b, s, _ = x.shape
            return x.reshape(b, s, H, HD).transpose(0, 2, 1, 3)
        Q = _split_heads(queries @ W_q + b_q)
        K = _split_heads(keys @ W_k + b_k)
        V = _split_heads(values @ W_v + b_v)
        scale = 1.0 / np.sqrt(HD)
        scores = jnp.einsum('bhqd,bhkd->bhqk', Q, K) * scale
        scores = jnp.where(attn_mask, jnp.float32(-1000000000.0), scores)
        probs = jax.nn.softmax(scores, axis=-1)
        ctx = jnp.einsum('bhqk,bhkd->bhqd', probs, V)
        ctx = ctx.transpose(0, 2, 1, 3).reshape(queries.shape[0], queries.shape[1], D)
        return ctx @ W_o + b_o

    def _L2_ffn_ref(x, router_W, router_b, W1, b1, W2, b2):
        import jax, jax.numpy as jnp
        import numpy as np
        D_MODEL = 128
        D_FF = 512
        N_EXPERTS = 8
        INIT_SCALE = 0.1

        def _trunc_normal(key, shape, std):
            return std * jax.random.truncated_normal(key, -2.0, 2.0, shape, dtype=jnp.float32)
        logits = jnp.einsum('bsd,de->bse', x.astype(jnp.float32), router_W) + router_b
        probs = jax.nn.softmax(logits, axis=-1)
        top1 = jnp.argmax(probs, axis=-1)
        mask = jax.nn.one_hot(top1, N_EXPERTS, dtype=x.dtype)
        gates = mask * probs.astype(x.dtype)
        h = jax.nn.relu(jnp.einsum('bsd,edf->besf', x, W1) + b1[:, None, :])
        y = jnp.einsum('besf,efd->besd', h, W2) + b2[:, None, :]
        out = jnp.einsum('bse,besd->bsd', gates, y)
        return out

    def _L3_xattn_ref(hidden_states, context_states, Wq, bq, Wk, bk, Wv, bv):
        import jax, jax.numpy as jnp
        import numpy as np
        import math
        H = 16

        def _split_heads(x):
            b, n, hd = x.shape
            return x.reshape(b, n, H, hd // H).transpose(0, 2, 1, 3)
        q = _split_heads(hidden_states @ Wq.T + bq)
        ctx = jnp.concatenate((hidden_states, context_states), axis=-2)
        k = _split_heads(ctx @ Wk.T + bk)
        v = _split_heads(ctx @ Wv.T + bv)
        d = q.shape[-1]
        scores = jnp.einsum('bhqd,bhkd->bhqk', q, k) / math.sqrt(d)
        probs = jax.nn.softmax(scores, axis=-1)
        out = jnp.einsum('bhqk,bhkd->bhqd', probs, v)
        b, h, n, dd = out.shape
        return out.transpose(0, 2, 1, 3).reshape(b, n, h * dd)

    def _L3_ffn_ref(x, gate_w, gate_b, w1, b1, w2, b2):
        import jax, jax.numpy as jnp
        import numpy as np
        B, S, D, H, E = (4, 256, 128, 512, 8)
        b, s, d = x.shape
        xf = x.reshape(-1, d)
        logits = xf @ gate_w.T + gate_b
        top1 = jnp.argmax(logits, axis=-1)
        out = jnp.zeros_like(xf)
        n_experts = w1.shape[0]
        for e in range(n_experts):
            h = jax.nn.relu(xf @ w1[e].T + b1[e])
            y = h @ w2[e].T + b2[e]
            out = out + jnp.where((top1 == e)[:, None], y, jnp.zeros((), y.dtype))
        return out.reshape(b, s, d)
    x = x + _L0_xattn_ref(_layernorm(x, axis=-1), ctx_1024, L0_xattn_Wq, L0_xattn_Wk, L0_xattn_Wv, L0_xattn_gru_wih, L0_xattn_gru_whh, L0_xattn_gru_bih, L0_xattn_gru_bhh, L0_xattn_slot_norm_w, L0_xattn_input_norm_w)
    x = x + _L0_ffn_ref(_layernorm(x, axis=-1), L0_ffn_w_red, L0_ffn_wg, L0_ffn_w1, L0_ffn_b1, L0_ffn_w2, L0_ffn_b2)
    x = x + _L1_xattn_ref(_layernorm(x, axis=-1), ctx_1024, L1_xattn_Wq, L1_xattn_Wk, L1_xattn_Wv, L1_xattn_Wo, L1_xattn_q_norm_w, L1_xattn_k_norm_w)
    x = x + _L1_ffn_ref(_layernorm(x, axis=-1), L1_ffn_gate_W, L1_ffn_gate_b, L1_ffn_W1, L1_ffn_b1, L1_ffn_g1, L1_ffn_be1, L1_ffn_W2, L1_ffn_b2, L1_ffn_g2, L1_ffn_be2)
    x = x + _L2_xattn_ref(_layernorm(x, axis=-1), ctx_1024, ctx_1024, mask_SxS2_bk1, L2_xattn_W_q, L2_xattn_b_q, L2_xattn_W_k, L2_xattn_b_k, L2_xattn_W_v, L2_xattn_b_v, L2_xattn_W_o, L2_xattn_b_o)
    x = x + _L2_ffn_ref(_layernorm(x, axis=-1), L2_ffn_router_W, L2_ffn_router_b, L2_ffn_W1, L2_ffn_b1, L2_ffn_W2, L2_ffn_b2)
    x = x + _L3_xattn_ref(_layernorm(x, axis=-1), ctx_1024, L3_xattn_Wq, L3_xattn_bq, L3_xattn_Wk, L3_xattn_bk, L3_xattn_Wv, L3_xattn_bv)
    x = x + _L3_ffn_ref(_layernorm(x, axis=-1), L3_ffn_gate_w, L3_ffn_gate_b, L3_ffn_w1, L3_ffn_b1, L3_ffn_w2, L3_ffn_b2)
    return x

_drawn_inputs = setup_inputs


def setup_inputs(seed=0):
    import zlib

    import numpy as np

    out = dict(_drawn_inputs(seed))
    spreads = {'L0_xattn_gru_bih': (0.0, 0.1),
     'L0_xattn_gru_bhh': (0.0, 0.1),
     'L0_xattn_slot_norm_w': (1.0, 0.2),
     'L0_xattn_input_norm_w': (1.0, 0.2),
     'L1_xattn_q_norm_w': (1.0, 0.2),
     'L1_xattn_k_norm_w': (1.0, 0.2),
     'L1_ffn_gate_b': (0.0, 0.1),
     'L1_ffn_b1': (0.0, 0.1),
     'L1_ffn_g1': (1.0, 0.2),
     'L1_ffn_be1': (0.0, 0.271),
     'L1_ffn_b2': (0.0, 0.1),
     'L1_ffn_g2': (1.0, 0.2),
     'L1_ffn_be2': (0.0, 0.1),
     'L2_xattn_b_q': (0.0, 0.452),
     'L2_xattn_b_k': (0.0, 0.8),
     'L2_xattn_b_v': (0.0, 0.1),
     'L2_xattn_b_o': (0.0, 0.1),
     'L2_ffn_router_b': (0.0, 0.8),
     'L2_ffn_b1': (0.0, 0.8),
     'L2_ffn_b2': (0.0, 0.774),
     'L3_xattn_bq': (0.0, 0.574),
     'L3_xattn_bk': (0.0, 0.8),
     'L3_xattn_bv': (0.0, 0.1)}
    factors = {'L0_ffn_w_red': 3.225,
     'L0_ffn_wg': 3.103,
     'L0_ffn_w1': 3.051,
     'L0_ffn_b1': 8.0,
     'L0_ffn_w2': 3.229,
     'L0_ffn_b2': 5.608,
     'L2_ffn_router_W': 6.226,
     'L2_ffn_W1': 8.0,
     'L2_ffn_W2': 8.0,
     'L3_ffn_b1': 7.233,
     'L3_ffn_b2': 5.675}
    for name, (base, spread) in spreads.items():
        noise = np.random.default_rng([zlib.crc32(name.encode()), seed]).standard_normal(out[name].shape)
        drawn = base * np.exp(spread * noise) if base else spread * noise
        out[name] = jnp.asarray(drawn.astype(out[name].dtype))
    for name, factor in factors.items():
        out[name] = (out[name] * factor).astype(out[name].dtype)
    return out
```

```python
from contextlib import ExitStack

import numpy as np

import concourse.bass as bass
from concourse import mybir

F32 = mybir.dt.float32
I32 = mybir.dt.int32
U8 = mybir.dt.uint8
ALU = mybir.AluOpType
ACT = mybir.ActivationFunctionType
AX = mybir.AxisListType

D = 128
TOKENS = 8192
NT = 4
GROUP = NT * D
GROUPS = TOKENS // GROUP
S = 64
LN_EPS = 1e-5
RMS_EPS = 1e-6


def rows(dram, start, tiles=NT):
    return dram[bass.ds(start, tiles * D), :].rearrange("(t p) f -> p t f", p=D)


class Space:

    def __init__(self, nc, ctx, phase):
        self.nc, self.ctx, self.phase, self.sems = nc, ctx, phase, []
        ctx.callback(self.clear)

    def clear(self):
        self.nc.clear_and_free_semaphores(self.sems)
        self.nc.all_engine_barrier()

    def sb(self, name, shape, dt=F32):
        return self.ctx.enter_context(self.nc.sbuf_tensor(f"{self.phase}_{name}", shape, dt))

    def psum(self, name, shape):
        return self.ctx.enter_context(self.nc.psum_tensor(f"{self.phase}_{name}", shape, F32))

    def sem(self, name):
        self.sems.append(self.nc.alloc_semaphore(f"{self.phase}_{name}"))
        return self.sems[-1]


def slot_attention(nc, c, x_in, ctx_in, x_out):
    U = 2
    ROUNDS = 3
    SCALE = float(D) ** -0.5
    with ExitStack() as ctx:
        m = Space(nc, ctx, "slots")
        wk, wq, wv = (m.sb(n, [D, D]) for n in ("wk", "wq", "wv"))
        wihT, whhT = m.sb("wihT", [D, 3 * D]), m.sb("whhT", [D, 3 * D])
        bih, bhh = m.sb("bih", [D, 3]), m.sb("bhh", [D, 3])
        w_slot, w_in = m.sb("w_slot", [D, 1]), m.sb("w_in", [D, 1])
        ident, ones, pair_ones = m.sb("ident", [D, D]), m.sb("ones", [D, D]), m.sb("pair_ones", [D, D])
        minus_half = m.sb("minus_half", [D, 2 * NT])
        keyT = m.sb("keyT", [D, D])
        val3 = m.sb("val3", [D, 3 * D])
        k_scale = m.sb("k_scale", [D, 1])
        half_b = m.sb("half_b", [D, 3])
        x_raw, c_raw = m.sb("x_raw", [D, U, NT, D]), m.sb("c_raw", [D, U, NT, D])
        stats, mv, mean = m.sb("stats", [D, U, 2 * NT, 6]), m.sb("mv", [D, U, 3, 2 * NT]), m.sb("mean", [D, U, 2 * NT])
        halves, quarters, per_row, eps = (m.sb(n, [D, 2 * NT]) for n in ("halves", "quarters", "per_row", "eps"))
        power, rstd = m.sb("power", [D, U, 2 * NT]), m.sb("rstd", [D, U, 2 * NT])
        xn, cn = m.sb("xn", [D, U, NT, D]), m.sb("cn", [D, U, NT, D])
        h, cT, kT = (m.sb(n, [D, U, GROUP]) for n in ("h", "cT", "kT"))
        v3 = m.sb("v3", [D, U, NT, 3 * D])
        sq = m.sb("sq", [D, U, GROUP])
        ms, rs = m.sb("ms", [D, U, NT]), m.sb("rs", [D, U, NT])
        r_diag, r_row = m.sb("r_diag", [D, U, NT, S]), m.sb("r_row", [D, U, NT * S])
        pair_ident = m.sb("pair_ident", [D, S])
        mx, total = m.sb("mx", [D, U, NT]), m.sb("total", [D, U, NT])
        expo, attn, colr = (m.sb(n, [D, U, NT, S]) for n in ("expo", "attn", "colr"))
        attn_bd = m.sb("attn_bd", [D, U, NT, 2, S])
        tr, tz, hn, n_in, n = (m.sb(k, [D, U, GROUP]) for k in ("tr", "tz", "hn", "n_in", "n"))
        x_res, x_new = m.sb("x_res", [D, U, NT, D]), m.sb("x_new", [D, U, NT, D])
        bank = m.psum("bank", [D, U, 4, GROUP])

        weights_in = m.sem("weights_in")
        pool_consts, dve_consts = m.sem("pool_consts"), m.sem("dve_consts")
        prep_mm, prep_set = m.sem("prep_mm"), m.sem("prep_set")
        raw_in = [m.sem(f"raw_in{u}") for u in range(U)]
        res_in = [m.sem(f"res_in{u}") for u in range(U)]
        out_done = [m.sem(f"out_done{u}") for u in range(U)]
        names = (
            "stats_done sums_done quartered squared power_raw power_done rstd_done norm_done turned_x turned_c hT_done cT_done "
            "keys_mm kT_done v3_mm v3_done sq_done ssq_mm ms_done rs_done r_diag_done r_row_mm r_row_done scores_mm scaled max_done shifted "
            "exp_done total_done inv_done attn_done colsum_mm coleps_done colr_done attn_bd_done gates_mm "
            "r_done z_done hn_done tn1_done n_in_done n_done diff_done upd_done h_done hback_mm new_done"
        ).split()
        s = {k: m.sem(k) for k in names}
        block = ctx.enter_context(nc.Block())

        LOADS = 13

        @block.sync
        def _(sp):
            for dst, src in ((wk, c["L0_Wk"]), (wq, c["L0_Wq"]), (wv, c["L0_Wv"]), (wihT, c["L0_wihT"]),
                             (whhT, c["L0_whhT"]), (bih, c["L0_bih"]), (bhh, c["L0_bhh"]), (w_slot, c["L0_w_slot"]),
                             (w_in, c["L0_w_in"]), (ident, c["ident"]), (ones, c["ones"]), (pair_ones, c["pair_ones"]), (pair_ident, c["pair_ident"])):
                sp.dma_start(dst[:], src).then_inc(weights_in, 16)
            for u in range(U):
                sp.dma_start(x_raw[:, u], rows(x_in, u * GROUP)).then_inc(raw_in[u], 16)
                sp.dma_start(c_raw[:, u], rows(ctx_in, u * GROUP)).then_inc(raw_in[u], 16)

            def body(i, last=False):
                if not last:
                    for u in range(U):
                        sp.wait_ge(s["norm_done"], i * U + u + 1)
                        sp.dma_start(x_raw[:, u], rows(x_in, (i + 1) * U * GROUP + u * GROUP)).then_inc(raw_in[u], 16)
                        sp.dma_start(c_raw[:, u], rows(ctx_in, (i + 1) * U * GROUP + u * GROUP)).then_inc(raw_in[u], 16)
                for u in range(U):
                    sp.wait_ge(s["new_done"], i * U)
                    sp.dma_start(x_res[:, u], rows(x_in, i * U * GROUP + u * GROUP)).then_inc(res_in[u], 16)
                for u in range(U):
                    sp.wait_ge(s["new_done"], i * U + u + 1)
                    sp.dma_start(rows(x_out, i * U * GROUP + u * GROUP), x_new[:, u]).then_inc(out_done[u], 16)

            with sp.Fori(0, GROUPS // U - 1) as i:
                body(i)
            body(GROUPS // U - 1, last=True)
            for u in range(U):
                sp.wait_ge(out_done[u], 16 * (GROUPS // U))

        @block.gpsimd
        def _(pool):
            nc.gpsimd.memset(minus_half[:], -0.5).then_inc(pool_consts, 1)
            nc.gpsimd.memset(attn_bd[:], 0.0).then_inc(pool_consts, 1)
            for dst, value in ((halves[:], 0.5), (quarters[:], 0.25), (per_row[:], 1.0 / D), (eps[:, :NT], LN_EPS), (eps[:, NT:], RMS_EPS)):
                nc.gpsimd.memset(dst, value).then_inc(pool_consts, 1)
            pool.wait_ge(pool_consts, 7)

            with pool.Fori(0, GROUPS // U) as i:
                for u in range(U):
                    k = i * U + u + 1
                    pool.wait_ge(s["stats_done"], k)
                    st = stats[:, u]
                    nc.gpsimd.tensor_tensor(mv[:, u, 0], st[:, :, 1], st[:, :, 4], ALU.add)
                    nc.gpsimd.tensor_tensor(mv[:, u, 1], st[:, :, 1], st[:, :, 4], ALU.subtract)
                    nc.gpsimd.tensor_tensor(mv[:, u, 2], st[:, :, 2], st[:, :, 5], ALU.add).then_inc(s["sums_done"], 1)
                    pool.wait_ge(s["sums_done"], k)
                    nc.gpsimd.tensor_tensor(mean[:, u], mv[:, u, 0], halves[:], ALU.mult)
                    nc.gpsimd.tensor_tensor(mv[:, u, 0], mv[:, u, 0], mv[:, u, 0], ALU.mult)
                    nc.gpsimd.tensor_tensor(mv[:, u, 1], mv[:, u, 1], mv[:, u, 1], ALU.mult)
                    nc.gpsimd.tensor_tensor(mv[:, u, 2], mv[:, u, 2], per_row[:], ALU.mult).then_inc(s["squared"], 1)
                    pool.wait_ge(s["squared"], k)
                    nc.gpsimd.tensor_tensor(mv[:, u, 1, NT:], mv[:, u, 1, NT:], mv[:, u, 0, NT:], ALU.add)
                    nc.gpsimd.tensor_tensor(mv[:, u, 2], mv[:, u, 2], eps[:], ALU.add).then_inc(s["power_raw"], 1)
                    pool.wait_ge(s["power_raw"], k)
                    nc.gpsimd.tensor_tensor(mv[:, u, 1], mv[:, u, 1], quarters[:], ALU.mult).then_inc(s["quartered"], 1)
                    pool.wait_ge(s["quartered"], k)
                    nc.gpsimd.tensor_tensor(power[:, u], mv[:, u, 1], mv[:, u, 2], ALU.add).then_inc(s["power_done"], 1)
                    pool.wait_ge(s["power_done"], k)
                    nc.gpsimd.tensor_tensor(rstd[:, u], power[:, u], minus_half[:], ALU.pow).then_inc(s["rstd_done"], 1)
                for r in range(ROUNDS):
                    for u in range(U):
                        k = (i * ROUNDS + r) * U + u + 1
                        pool.wait_ge(s["ms_done"], k)
                        nc.gpsimd.tensor_tensor(rs[:, u], ms[:, u], minus_half[:, :NT], ALU.pow).then_inc(s["rs_done"], 1)
                    for u in range(U):
                        k = (i * ROUNDS + r) * U + u + 1
                        pool.wait_ge(s["n_done"], k)
                        nc.gpsimd.tensor_tensor(sq[:, u], h[:, u], n[:, u], ALU.subtract).then_inc(s["diff_done"], 1)

        @block.scalar
        def _(act):
            act.wait_ge(prep_mm, 1)
            act.wait_ge(weights_in, 16 * LOADS)
            nc.scalar.activation(keyT[:], bank[:, 0, 0, :D], ACT.Copy, scale=w_in[:]).then_inc(prep_set, 1)
            nc.scalar.activation(val3[:], bank[:, 0, 1, :3 * D], ACT.Copy, scale=w_in[:]).then_inc(prep_set, 1)
            act.wait_ge(dve_consts, 3)
            with act.Fori(0, GROUPS // U) as i:
                for u in range(U):
                    k = i * U + u + 1
                    act.wait_ge(s["turned_x"], k)
                    nc.scalar.activation(h[:, u], bank[:, u, 0], ACT.Copy).then_inc(s["hT_done"], 1)
                    act.wait_ge(s["turned_c"], k)
                    nc.scalar.activation(cT[:, u], bank[:, u, 1], ACT.Copy).then_inc(s["cT_done"], 1)
                for u in range(U):
                    k = i * U + u + 1
                    act.wait_ge(s["keys_mm"], k)
                    nc.scalar.activation(kT[:, u], bank[:, u, 2], ACT.Copy, scale=k_scale[:]).then_inc(s["kT_done"], 1)
                for u in range(U):
                    for t, b in enumerate((3, 0, 1, 2)):
                        act.wait_ge(s["v3_mm"], (i * U + u) * NT + t + 1)
                        nc.scalar.activation(v3[:, u, t], bank[:, u, b, :3 * D], ACT.Copy).then_inc(s["v3_done"], 1)
                for r in range(ROUNDS):
                    for u in range(U):
                        k = (i * ROUNDS + r) * U + u + 1
                        if r == 0:
                            act.wait_ge(s["hT_done"], i * U + u + 1)
                        else:
                            act.wait_ge(s["h_done"], k - U)
                        nc.scalar.activation(sq[:, u], h[:, u], ACT.Square).then_inc(s["sq_done"], 1)
                    for u in range(U):
                        k = (i * ROUNDS + r) * U + u + 1
                        act.wait_ge(s["r_row_mm"], k)
                        nc.scalar.activation(r_row[:, u], bank[:, u, 0, :NT * S], ACT.Copy).then_inc(s["r_row_done"], 1)
                    for u in range(U):
                        k = (i * ROUNDS + r) * U + u + 1
                        act.wait_ge(s["shifted"], k)
                        nc.scalar.activation(expo[:, u], expo[:, u], ACT.Exp).then_inc(s["exp_done"], 1)
                    for u in range(U):
                        k = (i * ROUNDS + r) * U + u + 1
                        act.wait_ge(s["gates_mm"], k)
                        nc.scalar.activation(hn[:, u], bank[:, u, 3], ACT.Identity, scale=0.5, bias=half_b[:, 2:3]).then_inc(s["hn_done"], 1)
                        nc.scalar.activation(tr[:, u], bank[:, u, 0], ACT.Tanh, scale=0.5, bias=half_b[:, 0:1]).then_inc(s["r_done"], 1)
                        nc.scalar.activation(tz[:, u], bank[:, u, 1], ACT.Tanh, scale=0.5, bias=half_b[:, 1:2]).then_inc(s["z_done"], 1)
                    for u in range(U):
                        k = (i * ROUNDS + r) * U + u + 1
                        act.wait_ge(s["n_in_done"], k)
                        nc.scalar.activation(n[:, u], n_in[:, u], ACT.Tanh, bias=bih[:, 2:3]).then_inc(s["n_done"], 1)

        @block.vector
        def _(dve):
            dve.wait_ge(weights_in, 16 * LOADS)
            nc.vector.tensor_scalar(k_scale[:], w_slot[:], SCALE, None, ALU.mult).then_inc(dve_consts, 1)
            nc.vector.tensor_tensor(half_b[:, 0:2], bih[:, 0:2], bhh[:, 0:2], ALU.add).then_inc(dve_consts, 1)
            nc.vector.tensor_scalar(half_b[:, 2:3], bhh[:, 2:3], 0.5, None, ALU.mult)
            dve.wait_ge(dve_consts, 2)
            nc.vector.tensor_scalar(half_b[:, 0:2], half_b[:, 0:2], 0.5, None, ALU.mult).then_inc(dve_consts, 1)
            with dve.Fori(0, GROUPS // U) as i:
                for u in range(U):
                    k = i * U + u + 1
                    dve.wait_ge(raw_in[u], 32 * (i + 1))
                    for t in range(NT):
                        nc.vector.bn_stats(stats[:, u, t], x_raw[:, u, t])
                        last = nc.vector.bn_stats(stats[:, u, NT + t], c_raw[:, u, t])
                    last.then_inc(s["stats_done"], 1)
                for u in range(U):
                    k = i * U + u + 1
                    dve.wait_ge(s["rstd_done"], k)
                    for t in range(NT):
                        nc.vector.tensor_scalar(xn[:, u, t], x_raw[:, u, t], mean[:, u, t:t + 1], rstd[:, u, t:t + 1], ALU.subtract, ALU.mult)
                        last = nc.vector.tensor_scalar(cn[:, u, t], c_raw[:, u, t], rstd[:, u, NT + t:NT + t + 1], None, ALU.mult)
                    last.then_inc(s["norm_done"], 1)
                for r in range(ROUNDS):
                    count = lambda u: (i * ROUNDS + r) * U + u + 1
                    for u in range(U):
                        dve.wait_ge(s["ssq_mm"], count(u))
                        nc.vector.tensor_scalar(ms[:, u], bank[:, u, 0, :NT], 1.0 / D, RMS_EPS, ALU.mult, ALU.add).then_inc(s["ms_done"], 1)
                    for u in range(U):
                        dve.wait_ge(s["rs_done"], count(u))
                        nc.vector.tensor_tensor(r_diag[:, u], pair_ident[:].unsqueeze(1).broadcast_to([D, NT, S]),
                                                rs[:, u].unsqueeze(2).broadcast_to([D, NT, S]), ALU.mult).then_inc(s["r_diag_done"], 1)
                    for u in range(U):
                        dve.wait_ge(s["scores_mm"], count(u))
                        dve.wait_ge(s["r_row_done"], count(u))
                        for b in range(2):
                            p = slice(S * b, S * b + S)
                            own = bank[p, u, 1].rearrange("p (t b q) -> p t b q", t=NT, b=2)[:, :, b]
                            last = nc.vector.tensor_tensor(expo[p, u], own, r_row[p, u].rearrange("p (t q) -> p t q", t=NT), ALU.mult)
                        last.then_inc(s["scaled"], 1)
                        dve.wait_ge(s["scaled"], count(u))
                        nc.vector.tensor_reduce(mx[:, u], expo[:, u], AX.X, ALU.max).then_inc(s["max_done"], 1)
                        dve.wait_ge(s["max_done"], count(u))
                        nc.vector.tensor_tensor(expo[:, u], expo[:, u], mx[:, u].unsqueeze(2).broadcast_to([D, NT, S]),
                                                ALU.subtract).then_inc(s["shifted"], 1)
                    for u in range(U):
                        dve.wait_ge(s["exp_done"], count(u))
                        nc.vector.tensor_reduce(total[:, u], expo[:, u], AX.X, ALU.add).then_inc(s["total_done"], 1)
                        dve.wait_ge(s["total_done"], count(u))
                        nc.vector.reciprocal(total[:, u], total[:, u]).then_inc(s["inv_done"], 1)
                        dve.wait_ge(s["inv_done"], count(u))
                        nc.vector.tensor_tensor(attn[:, u], expo[:, u], total[:, u].unsqueeze(2).broadcast_to([D, NT, S]),
                                                ALU.mult).then_inc(s["attn_done"], 1)
                    for u in range(U):
                        dve.wait_ge(s["colsum_mm"], count(u))
                        nc.vector.tensor_scalar(colr[:, u], bank[:, u, 2, :NT * S], RMS_EPS, None, ALU.add).then_inc(s["coleps_done"], 1)
                        dve.wait_ge(s["coleps_done"], count(u))
                        nc.vector.reciprocal(colr[:, u], colr[:, u]).then_inc(s["colr_done"], 1)
                        dve.wait_ge(s["colr_done"], count(u))
                        for b in range(2):
                            p = slice(S * b, S * b + S)
                            last = nc.vector.tensor_tensor(attn_bd[p, u, :, b], attn[p, u], colr[p, u], ALU.mult)
                        last.then_inc(s["attn_bd_done"], 1)
                    for u in range(U):
                        dve.wait_ge(s["r_done"], count(u))
                        nc.vector.scalar_tensor_tensor(n_in[:, u], tr[:, u], 1.0, hn[:, u], ALU.add, ALU.mult).then_inc(s["tn1_done"], 1)
                        dve.wait_ge(s["tn1_done"], count(u))
                        nc.vector.tensor_tensor(n_in[:, u], n_in[:, u], bank[:, u, 2], ALU.add).then_inc(s["n_in_done"], 1)
                    for u in range(U):
                        dve.wait_ge(s["diff_done"], count(u))
                        dve.wait_ge(s["z_done"], count(u))
                        nc.vector.scalar_tensor_tensor(sq[:, u], tz[:, u], 1.0, sq[:, u], ALU.add, ALU.mult).then_inc(s["upd_done"], 1)
                        dve.wait_ge(s["upd_done"], count(u))
                        nc.vector.scalar_tensor_tensor(h[:, u], sq[:, u], 0.5, n[:, u], ALU.mult, ALU.add).then_inc(s["h_done"], 1)
                for u in range(U):
                    k = i * U + u + 1
                    dve.wait_ge(s["hback_mm"], k)
                    dve.wait_ge(res_in[u], 16 * (i + 1))
                    dve.wait_ge(out_done[u], 16 * i)
                    nc.vector.tensor_tensor(x_new[:, u], bank[:, u, 0], x_res[:, u].rearrange("p t f -> p (t f)"), ALU.add).then_inc(s["new_done"], 1)

        @block.tensor
        def _(pe):
            pe.wait_ge(weights_in, 16 * LOADS)
            nc.tensor.matmul(bank[:, 0, 0, :D], wk[:], wq[:], start=True, stop=True)
            nc.tensor.matmul(bank[:, 0, 1, :3 * D], wv[:], wihT[:], start=True, stop=True).then_inc(prep_mm, 1)
            pe.wait_ge(prep_set, 2)
            pe.wait_ge(pool_consts, 7)
            with pe.Fori(0, GROUPS // U) as i:
                for u in range(U):
                    k = i * U + u + 1
                    pe.wait_ge(s["norm_done"], k)
                    pe.wait_ge(s["new_done"], i * U)
                    for t in range(NT):
                        last = nc.tensor.transpose(bank[:, u, 0, t * D:(t + 1) * D], xn[:, u, t], ident[:])
                    last.then_inc(s["turned_x"], 1)
                    for t in range(NT):
                        last = nc.tensor.transpose(bank[:, u, 1, t * D:(t + 1) * D], cn[:, u, t], ident[:])
                    last.then_inc(s["turned_c"], 1)
                for u in range(U):
                    k = i * U + u + 1
                    pe.wait_ge(s["cT_done"], k)
                    nc.tensor.matmul(bank[:, u, 2], keyT[:], cT[:, u], start=True, stop=True).then_inc(s["keys_mm"], 1)
                for u in range(U):
                    k = i * U + u + 1
                    for t, b in enumerate((3, 0, 1, 2)):
                        if b == 2:
                            pe.wait_ge(s["kT_done"], k)
                        nc.tensor.matmul(bank[:, u, b, :3 * D], cT[:, u, t * D:(t + 1) * D], val3[:], start=True, stop=True).then_inc(s["v3_mm"], 1)
                for r in range(ROUNDS):
                    count = lambda u: (i * ROUNDS + r) * U + u + 1
                    for u in range(U):
                        pe.wait_ge(s["sq_done"], count(u))
                        if r == 0:
                            pe.wait_ge(s["v3_done"], (i * U + u) * NT + NT)
                        for t in range(NT):
                            last = nc.tensor.matmul(bank[:, u, 0, t:t + 1], sq[:, u, t * D:(t + 1) * D], ones[:, :1], start=True, stop=True)
                        last.then_inc(s["ssq_mm"], 1)
                        for t in range(NT):
                            c_ = slice(t * D, (t + 1) * D)
                            last = nc.tensor.matmul(bank[:, u, 1, c_], kT[:, u, c_], h[:, u, c_], start=True, stop=True)
                        last.then_inc(s["scores_mm"], 1)
                    for u in range(U):
                        nc.tensor.matmul(bank[:, u, 3], whhT[:, 2 * D:], h[:, u], start=True, stop=True)
                        pe.wait_ge(s["r_diag_done"], count(u))
                        nc.tensor.matmul(bank[:, u, 0, :NT * S], pair_ones[:], r_diag[:, u], start=True, stop=True).then_inc(s["r_row_mm"], 1)
                    for u in range(U):
                        pe.wait_ge(s["r_row_done"], count(u))
                        nc.tensor.matmul(bank[:, u, 0], whhT[:, :D], h[:, u], start=True, stop=False)
                        pe.wait_ge(s["attn_done"], count(u))
                        nc.tensor.matmul(bank[:, u, 2, :NT * S], pair_ones[:], attn[:, u], start=True, stop=True).then_inc(s["colsum_mm"], 1)
                    for u in range(U):
                        nc.tensor.matmul(bank[:, u, 1], whhT[:, D:2 * D], h[:, u], start=True, stop=False)
                        pe.wait_ge(s["attn_bd_done"], count(u))
                        for g, b in enumerate((0, 1, 2)):
                            for t in range(NT):
                                last = nc.tensor.matmul(bank[:, u, b, t * D:(t + 1) * D], v3[:, u, t, g * D:(g + 1) * D], attn_bd[:, u, t],
                                                        start=(b == 2), stop=(b == 2 or t == NT - 1))
                        last.then_inc(s["gates_mm"], 1)
                for u in range(U):
                    pe.wait_ge(s["h_done"], (i * ROUNDS + ROUNDS - 1) * U + u + 1)
                    for t in range(NT):
                        last = nc.tensor.transpose(bank[:, u, 0, t * D:(t + 1) * D], h[:, u, t * D:(t + 1) * D], ident[:])
                    last.then_inc(s["hback_mm"], 1)


E = 8
R_TILES = 16
R_STEPS = TOKENS // (R_TILES * D)
SLOT_TILES = 2
SLOT = SLOT_TILES * D
SLOTS = TOKENS // SLOT + E
XE_ROWS = SLOTS * SLOT


def moments(nc, dve, raw, tiles, stats, parts, mean, power, s, k):
    for t in range(tiles):
        last = nc.vector.bn_stats(stats[:, t], raw[:, t])
    last.then_inc(s["stats_done"], 1)
    dve.wait_ge(s["stats_done"], k)
    nc.vector.tensor_tensor(parts[:, 0], stats[:, :, 1], stats[:, :, 4], ALU.add)
    nc.vector.tensor_tensor(parts[:, 1], stats[:, :, 1], stats[:, :, 4], ALU.subtract)
    nc.vector.tensor_tensor(parts[:, 2], stats[:, :, 2], stats[:, :, 5], ALU.add).then_inc(s["parts_done"], 1)
    dve.wait_ge(s["parts_done"], k)
    nc.vector.tensor_scalar(mean, parts[:, 0], 0.5, None, ALU.mult)
    nc.vector.tensor_tensor(parts[:, 1], parts[:, 1], parts[:, 1], ALU.mult)
    nc.vector.tensor_scalar(parts[:, 2], parts[:, 2], 1.0 / D, LN_EPS, ALU.mult, ALU.add).then_inc(s["mean_done"], 1)
    dve.wait_ge(s["mean_done"], k)
    nc.vector.scalar_tensor_tensor(power, parts[:, 1], 0.25, parts[:, 2], ALU.mult, ALU.add).then_inc(s["power_done"], 1)


def route(nc, c, ph, x_in, gate, xe, pos_out, prob_out, table_out, weighted, clear):
    with ExitStack() as ctx:
        m = Space(nc, ctx, ph)
        T, N = R_TILES, TOKENS // D
        ident, ones, before = m.sb("ident", [D, D]), m.sb("ones", [D, D]), m.sb("before", [D, D])
        gw, gb = m.sb("gw", [D, E]), m.sb("gb", [D, E])
        minus_half = m.sb("minus_half", [D, T])
        falling, restart = m.sb("falling", [D, E]), m.sb("restart", [D, E, T])
        zeros = m.sb("zeros", [D, NT, D])
        raw, xn, xnT = m.sb("raw", [D, 2, T, D]), m.sb("xn", [D, N, D]), m.sb("xnT", [D, 2, T * D])
        stats, parts = m.sb("stats", [D, 2, T, 6]), m.sb("parts", [D, 2, 3, T])
        mean, power, rstd = (m.sb(n, [D, N]) for n in ("mean", "power", "rstd"))
        logit, hot, eq, expo, rank = (m.sb(n, [D, N, E]) for n in ("logit", "hot", "eq", "expo", "rank"))
        top, pick, prob, esum, posf, basef = (m.sb(n, [D, N]) for n in ("top", "pick", "prob", "esum", "posf", "basef"))
        tot, incl, base = (m.sb(n, [D, R_STEPS, E, T]) for n in ("tot", "incl", "base"))
        carry = m.sb("carry", [D, R_STEPS + 1, E])
        pos = m.sb("pos", [D, N], I32)
        steps, slot_no = m.sb("steps", [D, TOKENS // SLOT]), m.sb("slot_no", [D, SLOTS])
        over, need = m.sb("over", [D, E, TOKENS // SLOT]), m.sb("need", [D, E])
        cum, first = m.sb("cum", [D, E]), m.sb("first", [D, E])
        past, tabf, tab = m.sb("past", [D, SLOTS, E]), m.sb("tabf", [D, SLOTS]), m.sb("tab", [D, SLOTS], I32)
        pT = m.psum("pT", [D, 4, 4 * D])
        pL, pR, pS, pW = (m.psum(n, [D, 512]) for n in ("pL", "pR", "pS", "pW"))

        weights_in, pool_consts, gate_done = m.sem("weights_in"), m.sem("pool_consts"), m.sem("gate_done")
        gates, cleared, scattered, saved = m.sem("gate_steps"), m.sem("cleared"), m.sem("scattered"), m.sem("saved")
        raw_in = [m.sem(f"raw_in{u}") for u in range(2)]
        s = {k: m.sem(k) for k in (
            "stats_done parts_done mean_done power_done rstd_done norm_done turned xnT_done logits_mm logit_done top_done "
            "eq_done eqw_done pick_done hot_done shifted exp_done esum_done prob_done ranks_mm tot_done incl_done base0_done "
            "base_done rank_done carry_done table_step pos_done").split()}
        LOADS = 8
        if gate == "cosine":
            w_redT, wg, wgT = m.sb("w_redT", [16, D]), m.sb("wg", [E, 16]), m.sb("wgT", [16, E])
            wsq, wnorm, half8 = m.sb("wsq", [E, 16]), m.sb("wnorm", [E, 1]), m.sb("half8", [E, 1])
            LOADS = 9
        block = ctx.enter_context(nc.Block())

        @block.sync
        def _(sp):
            for i in range(2):
                sp.dma_start(raw[:, i], rows(x_in, i * T * D, T)).then_inc(raw_in[i], 16)
            own = ((w_redT, c["L0_w_redT"]), (wg, c["L0_wg"])) if gate == "cosine" else ((gw, gate[0]),)
            for dst, src in own + ((ident, c["ident"]), (ones, c["ones"]), (before, c["before"]), (falling, c["falling"]),
                                   (steps, c["steps"]), (slot_no, c["slot_no"])):
                sp.dma_start(dst[:], src).then_inc(weights_in, 16)
            bias = c["zero_row"][0:1, :E] if gate == "cosine" else gate[1]
            sp.dma_start(gb[:], bias.broadcast_to([D, E])).then_inc(weights_in, 16)
            for i in range(2, R_STEPS):
                sp.wait_ge(s["norm_done"], i - 1)
                sp.dma_start(raw[:, i % 2], rows(x_in, i * T * D, T)).then_inc(raw_in[i % 2], 16)
            if clear:
                sp.wait_ge(pool_consts, 3)
                for r in range(0, XE_ROWS, GROUP):
                    sp.dma_start(rows(xe, r), zeros[:]).then_inc(cleared, 16)
            sp.wait_ge(s["table_step"], 9)
            sp.dma_start(table_out, tab[0:1]).then_inc(saved, 16)
            sp.wait_ge(s["pos_done"], 1)
            sp.dma_start(pos_out, pos[:]).then_inc(saved, 16)
            if weighted:
                sp.wait_ge(s["prob_done"], R_STEPS)
                sp.dma_start(prob_out, prob[:]).then_inc(saved, 16)
            sp.wait_ge(saved, 48 if weighted else 32)

        @block.gpsimd
        def _(pool):
            nc.gpsimd.memset(minus_half[:], -0.5).then_inc(pool_consts, 1)
            nc.gpsimd.memset(zeros[:], 0.0).then_inc(pool_consts, 1)
            nc.gpsimd.memset(restart[:], 1.0).then_inc(pool_consts, 1)
            pool.wait_ge(pool_consts, 3)
            nc.gpsimd.memset(restart[:, :, 0:1], 0.0).then_inc(pool_consts, 1)
            if gate == "cosine":
                nc.gpsimd.memset(half8[:], 0.5).then_inc(pool_consts, 1)
                pool.wait_ge(pool_consts, 5)
                pool.wait_ge(gates, 1)
                nc.gpsimd.tensor_tensor(wnorm[:], wnorm[:], half8[:], ALU.pow).then_inc(gates, 1)
            for i in range(R_STEPS):
                own = slice(i * T, (i + 1) * T)
                pool.wait_ge(s["power_done"], i + 1)
                nc.gpsimd.tensor_tensor(rstd[:, own], power[:, own], minus_half[:], ALU.pow).then_inc(s["rstd_done"], 1)
            pool.wait_ge(s["norm_done"], R_STEPS)
            pool.wait_ge(s["pos_done"], 1)
            if clear:
                pool.wait_ge(cleared, 16 * (XE_ROWS // GROUP))
            for t in range(N):
                pool.indirect_dma_start(out=xe, out_offset=bass.IndirectOffsetOnAxis(ap=pos[:, t:t + 1], axis=0),
                                        in_=xn[:, t], in_offset=None).then_inc(scattered, 16)
            pool.wait_ge(scattered, 16 * N)

        @block.scalar
        def _(act):
            if gate == "cosine":
                act.wait_ge(weights_in, 16 * LOADS)
                nc.scalar.activation(wsq[:], wg[:], ACT.Square, accum_out=wnorm[:]).then_inc(gates, 1)
            for i in range(R_STEPS):
                for g in range(T // 4):
                    act.wait_ge(s["turned"], i * (T // 4) + g + 1)
                    nc.scalar.activation(xnT[:, i % 2, g * 4 * D:(g + 1) * 4 * D], pT[:, g], ACT.Copy).then_inc(s["xnT_done"], 1)
                if weighted:
                    own = slice(i * T, (i + 1) * T)
                    act.wait_ge(s["shifted"], i + 1)
                    nc.scalar.activation(expo[:, own], expo[:, own], ACT.Exp).then_inc(s["exp_done"], 1)

        @block.vector
        def _(dve):
            dve.wait_ge(weights_in, 16 * LOADS)
            if gate == "cosine":
                dve.wait_ge(gates, 2)
                nc.vector.tensor_scalar(wnorm[:], wnorm[:], 1e-4, None, ALU.max).then_inc(gates, 1)
                dve.wait_ge(gates, 3)
                nc.vector.reciprocal(wnorm[:], wnorm[:]).then_inc(gates, 1)
                dve.wait_ge(gates, 4)
                nc.vector.tensor_scalar(wg[:], wg[:], wnorm[:], None, ALU.mult).then_inc(gates, 1)
                dve.wait_ge(gates, 6)
                nc.vector.tensor_copy(wgT[:], pW[:16, :E]).then_inc(gates, 1)
                dve.wait_ge(gates, 8)
                nc.vector.tensor_copy(gw[:], pW[:, 16:16 + E]).then_inc(gate_done, 1)
            nc.vector.memset(carry[:, 0], 0.0).then_inc(s["carry_done"], 1)
            dve.wait_ge(pool_consts, 4)

            def normalise(i):
                own = slice(i * T, (i + 1) * T)
                dve.wait_ge(raw_in[i % 2], 16 * (i // 2 + 1))
                moments(nc, dve, raw[:, i % 2], T, stats[:, i % 2], parts[:, i % 2], mean[:, own], power[:, own], s, i + 1)
                dve.wait_ge(s["rstd_done"], i + 1)
                for t in range(T):
                    a = i * T + t
                    last = nc.vector.tensor_scalar(xn[:, a], raw[:, i % 2, t], mean[:, a:a + 1], rstd[:, a:a + 1], ALU.subtract, ALU.mult)
                last.then_inc(s["norm_done"], 1)

            def choose(i):
                own = slice(i * T, (i + 1) * T)
                per_tile = lambda a: a.unsqueeze(2).broadcast_to([D, T, E])
                per_expert = lambda a: a.unsqueeze(1).broadcast_to([D, T, E])
                k = i + 1
                dve.wait_ge(s["logits_mm"], k)
                nc.vector.tensor_tensor(logit[:, own], pL[:, :T * E].rearrange("p (t e) -> p t e", t=T), per_expert(gb[:]), ALU.add).then_inc(s["logit_done"], 1)
                dve.wait_ge(s["logit_done"], k)
                nc.vector.tensor_reduce(top[:, own], logit[:, own], AX.X, ALU.max).then_inc(s["top_done"], 1)
                dve.wait_ge(s["top_done"], k)
                nc.vector.tensor_tensor(eq[:, own], logit[:, own], per_tile(top[:, own]), ALU.is_equal).then_inc(s["eq_done"], 1)
                if weighted:
                    nc.vector.tensor_tensor(expo[:, own], logit[:, own], per_tile(top[:, own]), ALU.subtract).then_inc(s["shifted"], 1)
                dve.wait_ge(s["eq_done"], k)
                nc.vector.tensor_tensor(eq[:, own], eq[:, own], per_expert(falling[:]), ALU.mult).then_inc(s["eqw_done"], 1)
                dve.wait_ge(s["eqw_done"], k)
                nc.vector.tensor_reduce(pick[:, own], eq[:, own], AX.X, ALU.max).then_inc(s["pick_done"], 1)
                dve.wait_ge(s["pick_done"], k)
                nc.vector.tensor_tensor(hot[:, own], eq[:, own], per_tile(pick[:, own]), ALU.is_equal).then_inc(s["hot_done"], 1)
                dve.wait_ge(s["ranks_mm"], k)
                nc.vector.tensor_copy(tot[:, i], pS[:, :T * E].rearrange("p (t e) -> p e t", t=T)).then_inc(s["tot_done"], 1)
                dve.wait_ge(s["tot_done"], k)
                flat = lambda a: a.rearrange("p e t -> p (e t)")
                nc.vector.tensor_tensor_scan(flat(incl[:, i]), flat(restart[:]), flat(tot[:, i]), 0.0, ALU.mult, ALU.add).then_inc(s["incl_done"], 1)
                dve.wait_ge(s["incl_done"], k)
                nc.vector.tensor_tensor(base[:, i], incl[:, i], tot[:, i], ALU.subtract).then_inc(s["base0_done"], 1)
                dve.wait_ge(s["carry_done"], k)
                nc.vector.tensor_tensor(carry[:, i + 1], carry[:, i], incl[:, i, :, T - 1], ALU.add).then_inc(s["carry_done"], 1)
                dve.wait_ge(s["base0_done"], k)
                nc.vector.tensor_tensor(base[:, i], base[:, i], carry[:, i].unsqueeze(2).broadcast_to([D, E, T]), ALU.add).then_inc(s["base_done"], 1)
                dve.wait_ge(s["base_done"], k)
                nc.vector.tensor_tensor(rank[:, own], pR[:, :T * E].rearrange("p (t e) -> p t e", t=T),
                                        base[:, i].rearrange("p e t -> p t e"), ALU.add).then_inc(s["rank_done"], 1)
                if weighted:
                    dve.wait_ge(s["exp_done"], k)
                    nc.vector.tensor_reduce(esum[:, own], expo[:, own], AX.X, ALU.add).then_inc(s["esum_done"], 1)
                    dve.wait_ge(s["esum_done"], k)
                    nc.vector.reciprocal(prob[:, own], esum[:, own]).then_inc(s["prob_done"], 1)

            for i in range(R_STEPS + 1):
                if i < R_STEPS:
                    normalise(i)
                if i:
                    choose(i - 1)
            NS = TOKENS // SLOT
            steps_done = [0]

            def step(ins):
                steps_done[0] += 1
                ins.then_inc(s["table_step"], 1)
                dve.wait_ge(s["table_step"], steps_done[0])

            dve.wait_ge(s["carry_done"], R_STEPS + 1)
            step(nc.vector.tensor_tensor(over[:], carry[:, R_STEPS].unsqueeze(2).broadcast_to([D, E, NS]), steps[:].unsqueeze(1).broadcast_to([D, E, NS]), ALU.is_gt))
            step(nc.vector.tensor_reduce(need[:], over[:], AX.X, ALU.add))
            step(nc.vector.tensor_tensor_scan(cum[:], ones[:, :E], need[:], 0.0, ALU.mult, ALU.add))
            step(nc.vector.tensor_tensor(past[:], slot_no[:].unsqueeze(2).broadcast_to([D, SLOTS, E]), cum[:].unsqueeze(1).broadcast_to([D, SLOTS, E]), ALU.is_ge))
            step(nc.vector.tensor_tensor(first[:], cum[:], need[:], ALU.subtract))
            step(nc.vector.tensor_scalar(first[:], first[:], float(SLOT), None, ALU.mult))
            step(nc.vector.tensor_reduce(tabf[:], past[:], AX.X, ALU.add))
            step(nc.vector.tensor_scalar(tabf[:], tabf[:], float(E - 1), None, ALU.min))
            step(nc.vector.tensor_copy(tab[:], tabf[:]))
            step(nc.vector.tensor_tensor(rank[:], rank[:], first[:].unsqueeze(1).broadcast_to([D, N, E]), ALU.add))
            step(nc.vector.tensor_tensor(rank[:], rank[:], hot[:], ALU.mult))
            step(nc.vector.tensor_reduce(posf[:], rank[:], AX.X, ALU.add))
            nc.vector.tensor_copy(pos[:], posf[:]).then_inc(s["pos_done"], 1)

        @block.tensor
        def _(pe):
            pe.wait_ge(weights_in, 16 * LOADS)
            if gate == "cosine":
                pe.wait_ge(gates, 5)
                nc.tensor.transpose(pW[:16, :E], wg[:], ident[:E, :E]).then_inc(gates, 1)
                pe.wait_ge(gates, 7)
                nc.tensor.matmul(pW[:, 16:16 + E], w_redT[:], wgT[:], start=True, stop=True).then_inc(gates, 1)
                pe.wait_ge(gate_done, 1)

            def logits(i):
                pe.wait_ge(s["norm_done"], i + 1)
                for g in range(T // 4):
                    if i:
                        pe.wait_ge(s["xnT_done"], (i - 1) * (T // 4) + g + 1)
                    for t in range(4):
                        last = nc.tensor.transpose(pT[:, g, t * D:(t + 1) * D], xn[:, i * T + g * 4 + t], ident[:])
                    last.then_inc(s["turned"], 1)
                if i:
                    pe.wait_ge(s["logit_done"], i)
                for g in range(T // 4):
                    pe.wait_ge(s["xnT_done"], i * (T // 4) + g + 1)
                    for t in range(4 * g, 4 * g + 4):
                        last = nc.tensor.matmul(pL[:, t * E:(t + 1) * E], xnT[:, i % 2, t * D:(t + 1) * D], gw[:], start=True, stop=True)
                last.then_inc(s["logits_mm"], 1)

            def ranks(i):
                pe.wait_ge(s["hot_done"], i + 1)
                if i:
                    pe.wait_ge(s["rank_done"], i)
                hot_all = hot[:, i * T:(i + 1) * T].rearrange("p t e -> p (t e)")
                nc.tensor.matmul(pR[:, :T * E], before[:], hot_all, start=True, stop=True)
                nc.tensor.matmul(pS[:, :T * E], ones[:], hot_all, start=True, stop=True).then_inc(s["ranks_mm"], 1)

            for i in range(R_STEPS):
                logits(i)
                ranks(i)


def experts(nc, c, ph, xe, table_in, w, ye, gelu):
    U = 2
    F = 4
    with ExitStack() as ctx:
        m = Space(nc, ctx, ph)
        ident, tab = m.sb("ident", [D, D]), m.sb("tab", [1, SLOTS], I32)
        w1, w2 = m.sb("w1", [D, U, F * D]), m.sb("w2", [D, U, F * D])
        b1, b2 = m.sb("b1", [D, U, F]), m.sb("b2", [D, U, D])
        x, xT, h, y = m.sb("x", [D, U, SLOT_TILES, D]), m.sb("xT", [D, U, SLOT]), m.sb("h", [D, U, F, SLOT]), m.sb("y", [D, U, SLOT_TILES, D])
        pX, pH, pY = m.psum("pX", [D, U, 512]), m.psum("pH", [D, U, F, SLOT]), m.psum("pY", [D, U, 512])
        setup_in, tab_in, store_turn = m.sem("setup_in"), m.sem("tab_in"), m.sem("store_turn")
        w1_in, w2_in, x_loaded, saved = ([m.sem(f"{n}{u}") for u in range(U)] for n in ("w1_in", "w2_in", "x_loaded", "saved"))
        s = {k: m.sem(k) for k in "turned xT_done hidden_mm act_done y_mm y_done".split()}
        block = ctx.enter_context(nc.Block())

        @block.sync
        def _(sp):
            sp.dma_start(ident[:], c["ident"]).then_inc(setup_in, 16)
            sp.dma_start(tab[:], table_in).then_inc(tab_in, 16)
            sp.wait_ge(tab_in, 16)
            with sp.Fori(0, SLOTS // U) as i:
                for u in range(U):
                    e = sp.value_load(tab[0:1, bass.ds(i * U + u, 1)], min_val=0, max_val=E - 1)
                    sp.wait_ge(s["turned"], i * U)
                    sp.dma_start(x[:, u], rows(xe, (i * U + u) * SLOT, SLOT_TILES)).then_inc(x_loaded[u], 16)
                    sp.wait_ge(s["act_done"], (i * U) * F)
                    sp.dma_start(w1[:, u], w[0][bass.ds(e * D, D), :]).then_inc(w1_in[u], 16)
                    sp.dma_start(b1[:, u], w[1][bass.ds(e * D, D), :]).then_inc(w1_in[u], 16)
                    sp.wait_ge(s["y_done"], i * U)
                    sp.dma_start(w2[:, u], w[2][bass.ds(e * D, D), :]).then_inc(w2_in[u], 16)
                    sp.dma_start(b2[:, u], w[3][bass.ds(e, 1), :].broadcast_to([D, D])).then_inc(w2_in[u], 16)

        @block.gpsimd
        def _(pool):
            with pool.Fori(0, SLOTS // U) as i:
                for u in range(U):
                    pool.wait_ge(s["y_done"], i * U + u + 1)
                    pool.sem_inc(store_turn, 1)
                    pool.dma_start(rows(ye, (i * U + u) * SLOT, SLOT_TILES), y[:, u]).then_inc(saved[u], 16)
            for u in range(U):
                pool.wait_ge(saved[u], 16 * (SLOTS // U))

        @block.scalar
        def _(act):
            with act.Fori(0, SLOTS // U) as i:
                for u in range(U):
                    k = i * U + u
                    act.wait_ge(s["turned"], k + 1)
                    nc.scalar.activation(xT[:, u], pX[:, u, :SLOT], ACT.Copy).then_inc(s["xT_done"], 1)
                    for f in range(F):
                        act.wait_ge(s["hidden_mm"], k * F + (f | 1) + 1)
                        if gelu:
                            nc.scalar.activation(h[:, u, f], pH[:, u, f], ACT.Gelu, bias=b1[:, u, f:f + 1]).then_inc(s["act_done"], 1)
                        else:
                            nc.scalar.activation(h[:, u, f], pH[:, u, f], ACT.Relu, bias=b1[:, u, f:f + 1]).then_inc(s["act_done"], 1)

        @block.vector
        def _(dve):
            with dve.Fori(0, SLOTS // U) as i:
                for u in range(U):
                    k = i * U + u
                    dve.wait_ge(s["y_mm"], k + 1)
                    dve.wait_ge(saved[u], 16 * i)
                    nc.vector.tensor_tensor(y[:, u], pY[:, u, :SLOT].rearrange("p (t f) -> p t f", t=SLOT_TILES),
                                            b2[:, u].unsqueeze(1).broadcast_to([D, SLOT_TILES, D]), ALU.add).then_inc(s["y_done"], 1)

        @block.tensor
        def _(pe):
            pe.wait_ge(setup_in, 16)

            def turn(i, u):
                pe.wait_ge(x_loaded[u], 16 * (i + 1))
                for t in range(SLOT_TILES):
                    last = nc.tensor.transpose(pX[:, u, t * D:(t + 1) * D], x[:, u, t], ident[:])
                last.then_inc(s["turned"], 1)

            with pe.Fori(0, SLOTS // U) as i:
                for u in range(U):
                    turn(i, u)
                for u in range(U):
                    k = i * U + u
                    pe.wait_ge(w1_in[u], 32 * (i + 1))
                    pe.wait_ge(s["xT_done"], k + 1)
                    for f in range(F):
                        nc.tensor.matmul(pH[:, u, f], w1[:, u, f * D:(f + 1) * D], xT[:, u], start=True, stop=True).then_inc(s["hidden_mm"], 1)
                for u in range(U):
                    k = i * U + u
                    pe.wait_ge(w2_in[u], 32 * (i + 1))
                    pe.wait_ge(s["y_done"], i * U)
                    for t in range(SLOT_TILES):
                        for f in range(F):
                            pe.wait_ge(s["act_done"], k * F + f + 1)
                            last = nc.tensor.matmul(pY[:, u, t * D:(t + 1) * D], h[:, u, f, t * D:(t + 1) * D], w2[:, u, f * D:(f + 1) * D],
                                                    start=(f == 0), stop=(f == F - 1))
                    last.then_inc(s["y_mm"], 1)


H = 16
HD = D // H
B = GROUP // S


def attention(nc, c, ph, layer, x_in, ctx_in, w, x_out, combined=None):
    own_keys = layer == 3
    NS = 2 if own_keys else 1
    AHEAD = 1 if own_keys else 2
    RING = 2 * AHEAD
    SCALE = float(HD) ** -0.5
    rope = layer == 1
    project = layer != 3
    with ExitStack() as ctx:
        m = Space(nc, ctx, ph)
        ident, n_mask = m.sb("ident", [D, D]), m.sb("n_mask", [D, 8])
        wq, wk, wv = (m.sb(n, [D, D]) for n in ("wq", "wk", "wv"))
        minus_half = m.sb("minus_half", [D, NT])
        x_res, c_raw, xn = m.sb("x_res", [D, 2, NT, D]), m.sb("c_raw", [D, NT, D]), m.sb("xn", [D, NT, D])
        stats, parts = m.sb("stats", [D, NT, 6]), m.sb("parts", [D, 3, NT])
        mean, power, rstd = (m.sb(n, [D, NT]) for n in ("mean", "power", "rstd"))
        xT, cT = m.sb("xT", [D, GROUP]), m.sb("cT", [D, GROUP])
        twice = [m.sb(f"twice{n}", [D, B, 2, S]) for n in range(NS)]
        qg = m.sb("qg", [D, 2, B, 2, S])
        kT = m.sb("kT", [D, 2, NS, GROUP])
        kn = m.sb("kn", [D, 2, NS, 8, S])
        vx = m.sb("vx", [D, 2, NS, B, 8, 2, HD + 1])
        e = m.sb("e", [D, RING, NS, 8, S])
        mx, rden = m.sb("mx", [D, 2, 8]), m.sb("rden", [D, 2, H])
        pt = m.sb("pt", [D, 2, NS, 4, D])
        attn, x_new = m.sb("attn", [D, 2, NT, D]), m.sb("x_new", [D, NT, D])
        front = m.psum("front", [D, 2, GROUP])
        sc = m.psum("sc", [D, AHEAD, NS, 8 * S])
        turn = m.psum("turn", [D, NS, GROUP])
        pv = m.psum("pv", [D, 2, 512])

        loads = [(ident[:], c["ident"]), (n_mask[:], c["n_mask"]), (wq[:], w["q"]), (wk[:], w["k"]), (wv[:], w["v"])]
        if project:
            wo, aT = m.sb("wo", [D, D]), m.sb("aT", [D, GROUP])
            loads += [(wo[:], w["o"])]
        if not rope:
            bq, bk, bv = m.sb("bq", [D, 1]), m.sb("bk", [D, 1]), m.sb("bv", [D, D])
            loads += [(bq[:], w["bq"]), (bk[:], w["bk"]), (bv[:], w["bv"].broadcast_to([D, D]))]
        if layer == 2:
            bo, m8 = m.sb("bo", [D, D]), m.sb("m8", [D, S // 4], mybir.dt.uint32)
            keep, neg = m.sb("keep", [D, S]), m.sb("neg", [D, S])
            loads += [(bo[:], w["bo"].broadcast_to([D, D])), (m8[:S], w["mask"]), (m8[S:], w["mask"])]
        if rope:
            tab, wrow = m.sb("tab", [D, 4, HD]), m.sb("wrow", [D, 4, HD])
            qk, qs = m.sb("qk", [D, 2, NT * H, HD]), m.sb("qs", [D, 2, NT * H, HD])
            ssq, rr = m.sb("ssq", [D, 2, NT * H]), m.sb("rr", [D, 2, NT * H])
            loads += [(tab[:], c["rope"])]
            for k, v in enumerate(w["norm"]):
                loads += [(wrow[:, 2 * k], v.broadcast_to([D, HD]))]
                loads += [(wrow[:, 2 * k + 1, a:a + HD // 2], v[:, HD // 2 - a:HD - a].broadcast_to([D, HD // 2])) for a in (0, HD // 2)]
        if combined:
            pos, prob = m.sb("pos", [D, TOKENS // D], I32), m.sb("prob", [D, TOKENS // D])
            pos_now, y = m.sb("pos_now", [D, NT], I32), m.sb("y", [D, NT, D])
            loads += [(pos[:], combined[1]), (prob[:], combined[2])]
            pos_step, pos_turn, y_in, y_used = m.sem("pos_step"), m.sem("pos_turn"), m.sem("y_in"), m.sem("y_used")
        LOADS = 16 * len(loads)

        weights_in, pool_consts, dve_consts, dve_ready = (m.sem(n) for n in ("weights_in", "pool_consts", "dve_consts", "dve_ready"))
        x_loaded = [m.sem(f"x_loaded{p}") for p in range(2)]
        c_loaded, saved = m.sem("c_loaded"), m.sem("saved")
        s = {k: m.sem(k) for k in (
            "stats_done parts_done mean_done power_done rstd_done norm_done turned_x turned_c xT_done cT_done twice_done "
            "q_mm k_mm q_done k_done own_k_mm own_k_done v_mm v_done masked scores_mm kept negated max_done shifted exp_done "
            "turned_e pt_done pv_mm rden_done normed fin_turned aT_done fin_mm fin_added new_done "
            "q_sq k_sq ssq_done ssqeps_done sqrt_done rr_done qk_scaled swapped cosed roped turned_q turned_k").split()}
        block = ctx.enter_context(nc.Block())
        LAST = GROUPS - 1
        V_STEPS = [(src, half) for half in range(2) for src in range(NS)]

        def at(j, p, b):
            return (j, p, b) if b < B else (j + 1, 1 - p, b - B)

        def schedule(eng, slot):
            with eng.Fori(0, GROUPS // 2 - 1) as i:
                for p in range(2):
                    for b in range(B):
                        slot(i * 2 + p, p, b, True)
            for p in range(2):
                for b in range(B):
                    slot(LAST - 1 + p, p, b, p == 0)

        @block.sync
        def _(sp):
            for dst, src in loads:
                sp.dma_start(dst, src).then_inc(weights_in, 16)

            def load(j, p):
                sp.dma_start(x_res[:, p], rows(x_in, j * GROUP)).then_inc(x_loaded[p], 16)
                sp.wait_ge(s["turned_c"], j)
                sp.dma_start(c_raw[:], rows(ctx_in, j * GROUP)).then_inc(c_loaded, 16)

            load(0, 0)

            def slot(j, p, b, more):
                if b == 0 and more:
                    sp.wait_ge(s["new_done"], j)
                    load(j + 1, 1 - p)
                if b == B - 1:
                    sp.wait_ge(s["new_done"], j + 1)
                    sp.dma_start(rows(x_out, j * GROUP), x_new[:]).then_inc(saved, 16)

            schedule(sp, slot)
            sp.wait_ge(saved, 16 * GROUPS)

        @block.gpsimd
        def _(pool):
            nc.gpsimd.memset(minus_half[:], -0.5).then_inc(pool_consts, 1)
            nc.gpsimd.memset(qg[:], 0.0).then_inc(pool_consts, 1)
            nc.gpsimd.memset(vx[:], 0.0).then_inc(pool_consts, 1)
            pool.wait_ge(pool_consts, 3)
            for a in range(2):
                nc.gpsimd.memset(vx[a * S:a * S + S, :, :, :, :, a, HD:].rearrange("p x s b n o -> p (x s b n) o"), 1.0).then_inc(pool_consts, 1)
            pool.wait_ge(weights_in, LOADS)
            pool.wait_ge(pool_consts, 5)

            def gather(j):
                if not combined:
                    return
                nc.gpsimd.tensor_copy(pos_now[:], pos[:, bass.ds(j * NT, NT)]).then_inc(pos_step, 1)
                pool.wait_ge(pos_step, j + 1)
                pool.wait_ge(y_used, j)
                pool.sem_inc(pos_turn, 1)
                for t in range(NT):
                    pool.indirect_dma_start(out=y[:, t], out_offset=None, in_=combined[0],
                                            in_offset=bass.IndirectOffsetOnAxis(ap=pos_now[:, t:t + 1], axis=0)).then_inc(y_in, 16)

            def rstd_of(j):
                pool.wait_ge(s["power_done"], j + 1)
                nc.gpsimd.tensor_tensor(rstd[:], power[:], minus_half[:], ALU.pow).then_inc(s["rstd_done"], 1)

            def cosines(j):
                if rope:
                    pool.wait_ge(s["swapped"], j + 1)
                    for k in range(2):
                        last = nc.gpsimd.tensor_tensor(qk[:, k], qk[:, k], tab[:, 2 * k].unsqueeze(1).broadcast_to([D, NT * H, HD]), ALU.mult)
                    last.then_inc(s["cosed"], 1)

            def mask(j, p, b):
                n = j * B + b
                pool.wait_ge(s["own_k_done" if own_keys else "k_done"], j + 1)
                pool.wait_ge(s["scores_mm"], n - 1 if b else j * B)
                for src in range(NS):
                    last = nc.gpsimd.tensor_tensor(kn[:, b % 2, src], kT[:, p, src, b * S:(b + 1) * S].unsqueeze(1).broadcast_to([D, 8, S]),
                                                   n_mask[:].unsqueeze(2).broadcast_to([D, 8, S]), ALU.mult)
                last.then_inc(s["masked"], 1)

            def negate(j, p, b):
                if layer == 2:
                    pool.wait_ge(s["kept"], j * B + b + 1)
                    nc.gpsimd.tensor_tensor(e[:, b % RING, 0], e[:, b % RING, 0], neg[:].unsqueeze(1).broadcast_to([D, 8, S]), ALU.add).then_inc(s["negated"], 1)

            gather(0)
            rstd_of(0)
            gather(1)
            cosines(0)
            mask(0, 0, 0)
            if layer == 2:
                pool.wait_ge(dve_ready, 1)
            for b in range(AHEAD):
                mask(0, 0, b + 1)
                negate(0, 0, b)

            def slot(j, p, b, more):
                if more or b + AHEAD + 1 < B:
                    mask(*at(j, p, b + AHEAD + 1))
                if more or b + AHEAD < B:
                    negate(*at(j, p, b + AHEAD))
                if more and b == 1:
                    rstd_of(j + 1)
                if more and b == 3:
                    cosines(j + 1)
                if more and b == 4 and not (isinstance(j, int) and j + 2 > LAST):
                    gather(j + 2)

            schedule(pool, slot)

        @block.scalar
        def _(act):
            act.wait_ge(weights_in, LOADS)
            act.wait_ge(dve_consts, 1)

            def turned(j):
                act.wait_ge(s["turned_x"], j + 1)
                nc.scalar.activation(xT[:], front[:, 0], ACT.Copy).then_inc(s["xT_done"], 1)
                act.wait_ge(s["turned_c"], j + 1)
                nc.scalar.activation(cT[:], front[:, 1], ACT.Copy).then_inc(s["cT_done"], 1)
                for n, one in enumerate((cT, xT)[:NS]):
                    act.wait_ge(s[("cT_done", "xT_done")[n]], j + 1)
                    last = nc.scalar.activation(twice[n][:], one[:].rearrange("p (b k) -> p b k", b=B).unsqueeze(2).broadcast_to([D, B, 2, S]), ACT.Copy)
                last.then_inc(s["twice_done"], 1)

            def keys_queries(j, p):
                act.wait_ge(s["turned_q" if rope else "q_mm"], j + 1)
                for g in range(2):
                    f = slice(g * S, g * S + S)
                    src = front[f, 0].rearrange("p (b q) -> p b q", b=B)
                    if rope:
                        last = nc.scalar.activation(qg[f, p, :, g], src, ACT.Copy)
                    else:
                        last = nc.scalar.activation(qg[f, p, :, g], src, ACT.Identity, scale=SCALE, bias=bq[f])
                last.then_inc(s["q_done"], 1)
                act.wait_ge(s["turned_k" if rope else "k_mm"], j + 1)
                if rope:
                    nc.scalar.activation(kT[:, p, 0], front[:, 1], ACT.Copy).then_inc(s["k_done"], 1)
                else:
                    nc.scalar.activation(kT[:, p, 0], front[:, 1], ACT.Identity, bias=bk[:]).then_inc(s["k_done"], 1)
                if own_keys:
                    act.wait_ge(s["own_k_mm"], j + 1)
                    nc.scalar.activation(kT[:, p, 1], front[:, 0], ACT.Identity, bias=bk[:]).then_inc(s["own_k_done"], 1)

            def squares(j):
                act.wait_ge(s["q_mm"], j + 1)
                nc.scalar.activation(qs[:, 0].rearrange("p n d -> p (n d)"), front[:, 0], ACT.Square).then_inc(s["q_sq"], 1)
                act.wait_ge(s["k_mm"], j + 1)
                nc.scalar.activation(qs[:, 1].rearrange("p n d -> p (n d)"), front[:, 1], ACT.Square).then_inc(s["k_sq"], 1)

            def roots(j):
                act.wait_ge(s["ssqeps_done"], j + 1)
                nc.scalar.activation(rr[:], ssq[:], ACT.Sqrt).then_inc(s["sqrt_done"], 1)

            def piece(j, p, n):
                if n == 1:
                    turned(j)
                    if rope:
                        squares(j)
                    else:
                        keys_queries(j, p)
                if n == 2 and rope:
                    roots(j)
                if n == 3 and rope:
                    keys_queries(j, p)

            def exps(j, p, b):
                act.wait_ge(s["shifted"], j * B + b + 1)
                nc.scalar.activation(e[:, b % RING], e[:, b % RING], ACT.Exp).then_inc(s["exp_done"], 1)

            for n in range(5):
                piece(0, 0, n)
            for b in range(AHEAD):
                exps(0, 0, b)

            def slot(j, p, b, more):
                n = j * B + b
                for src in range(NS):
                    act.wait_ge(s["turned_e"], n * NS + src + 1)
                    nc.scalar.activation(pt[:, b % 2, src].rearrange("p m q -> p (m q)"), turn[:, src], ACT.Copy).then_inc(s["pt_done"], 1)
                if more or b + AHEAD < B:
                    exps(*at(j, p, b + AHEAD))
                if more and b:
                    piece(j + 1, 1 - p, b - 1)
                if b == B - 1 and project:
                    act.wait_ge(s["fin_turned"], j + 1)
                    nc.scalar.activation(aT[:], pv[:, 0], ACT.Copy).then_inc(s["aT_done"], 1)

            schedule(act, slot)

        @block.vector
        def _(dve):
            dve.wait_ge(weights_in, LOADS)
            if rope:
                nc.vector.tensor_tensor(tab[:], tab[:], wrow[:], ALU.mult).then_inc(dve_consts, 1)
            elif layer == 2:
                nc.vector.tensor_scalar(bq[:], bq[:], SCALE, None, ALU.mult).then_inc(dve_consts, 1)
                dve.wait_ge(dve_consts, 1)
                nc.vector.tensor_scalar(keep[:], m8[:].bitcast(U8), -1.0, 1.0, ALU.mult, ALU.add)
                nc.vector.tensor_scalar(neg[:], m8[:].bitcast(U8), -1e9, None, ALU.mult).then_inc(dve_ready, 1)
                dve.wait_ge(dve_ready, 1)
            else:
                nc.vector.tensor_scalar(bq[:], bq[:], SCALE, None, ALU.mult).then_inc(dve_consts, 1)
            dve.wait_ge(dve_consts, 1)
            dve.wait_ge(pool_consts, 5)

            def norm(j, p):
                raw = x_res[:, p]
                dve.wait_ge(x_loaded[p], 16 * ((j - p) // 2 + 1) if isinstance(j, int) else 8 * (j - p) + 16)
                if combined:
                    dve.wait_ge(y_in, 16 * NT * (j + 1))
                    for t in range(NT):
                        last = nc.vector.scalar_tensor_tensor(raw[:, t], y[:, t], prob[:, bass.ds(j * NT + t, 1)], raw[:, t], ALU.mult, ALU.add)
                    last.then_inc(y_used, 1)
                    dve.wait_ge(y_used, j + 1)
                moments(nc, dve, raw, NT, stats, parts, mean[:], power[:], s, j + 1)
                dve.wait_ge(s["rstd_done"], j + 1)
                for t in range(NT):
                    last = nc.vector.tensor_scalar(xn[:, t], raw[:, t], mean[:, t:t + 1], rstd[:, t:t + 1], ALU.subtract, ALU.mult)
                last.then_inc(s["norm_done"], 1)

            def values(j, p, steps):
                for n in steps:
                    src, half = V_STEPS[n]
                    bank = front[:, n % 2].rearrange("p (b n a d) -> p b n a d", b=4, a=2, d=HD)
                    dve.wait_ge(s["v_mm"], j * len(V_STEPS) + n + 1)
                    for a in range(2):
                        f = slice(a * S, a * S + S)
                        for_heads = vx[f, p, src, half * 4:half * 4 + 4, :, a, :HD]
                        if rope:
                            last = nc.vector.tensor_copy(for_heads, bank[f, :, :, a])
                        else:
                            bias = bv[f].rearrange("p (n a d) -> p n a d", a=2, d=HD)[:, :, a].unsqueeze(1).broadcast_to([S, 4, 8, HD])
                            last = nc.vector.tensor_tensor(for_heads, bank[f, :, :, a], bias, ALU.add)
                    last.then_inc(s["v_done"], 1)

            def rms(j):
                dve.wait_ge(s["q_sq"], j + 1)
                dve.wait_ge(s["k_sq"], j + 1)
                nc.vector.tensor_reduce(ssq[:], qs[:], AX.X, ALU.add).then_inc(s["ssq_done"], 1)
                dve.wait_ge(s["ssq_done"], j + 1)
                nc.vector.tensor_scalar(ssq[:], ssq[:], 1.0 / HD, RMS_EPS, ALU.mult, ALU.add).then_inc(s["ssqeps_done"], 1)
                dve.wait_ge(s["sqrt_done"], j + 1)
                nc.vector.reciprocal(rr[:], rr[:]).then_inc(s["rr_done"], 1)
                dve.wait_ge(s["rr_done"], j + 1)
                for k in range(2):
                    last = nc.vector.tensor_tensor(qk[:, k], front[:, k].rearrange("p (n d) -> p n d", d=HD),
                                                   rr[:, k].unsqueeze(2).broadcast_to([D, NT * H, HD]), ALU.mult)
                last.then_inc(s["qk_scaled"], 1)
                dve.wait_ge(s["qk_scaled"], j + 1)
                half = HD // 2
                for k in range(2):
                    for lo, hi in ((0, half), (half, 0)):
                        last = nc.vector.tensor_tensor(qs[:, k, :, lo:lo + half], qk[:, k, :, hi:hi + half],
                                                       tab[:, 2 * k + 1, lo:lo + half].unsqueeze(1).broadcast_to([D, NT * H, half]), ALU.mult)
                last.then_inc(s["swapped"], 1)

            def turn_rope(j):
                dve.wait_ge(s["swapped"], j + 1)
                dve.wait_ge(s["cosed"], j + 1)
                nc.vector.tensor_tensor(qk[:], qk[:], qs[:], ALU.add).then_inc(s["roped"], 1)

            def piece(j, p, n):
                if n == 0:
                    norm(j, p)
                if n == 2 and rope:
                    rms(j)
                if n == 3 and rope:
                    turn_rope(j)
                if n == 4:
                    values(j, p, range(0, NS))
                if n == 5:
                    values(j, p, range(NS, 2 * NS))

            def softmax(j, p, b):
                n = j * B + b
                dve.wait_ge(s["scores_mm"], n + 1)
                r = b % RING
                if layer == 2:
                    nc.vector.tensor_tensor(e[:, r, 0], sc[:, b % AHEAD, 0].rearrange("p (n k) -> p n k", n=8),
                                            keep[:].unsqueeze(1).broadcast_to([D, 8, S]), ALU.mult).then_inc(s["kept"], 1)
                    dve.wait_ge(s["negated"], n + 1)
                    src = e[:, r, 0]
                    nc.vector.tensor_reduce(mx[:, b % 2], src, AX.X, ALU.max).then_inc(s["max_done"], 1)
                elif NS == 1:
                    src = sc[:, b % AHEAD, 0].rearrange("p (n k) -> p n k", n=8)
                    nc.vector.tensor_reduce(mx[:, b % 2], src, AX.X, ALU.max).then_inc(s["max_done"], 1)
                else:
                    src = sc[:, b % AHEAD].rearrange("p s (n k) -> p s n k", n=8)
                    nc.vector.tensor_reduce(mx[:, b % 2], src.rearrange("p s n k -> p n s k"), AX.XY, ALU.max).then_inc(s["max_done"], 1)
                dve.wait_ge(s["max_done"], n + 1)
                if NS == 1:
                    nc.vector.tensor_tensor(e[:, r, 0], src, mx[:, b % 2].unsqueeze(2).broadcast_to([D, 8, S]), ALU.subtract).then_inc(s["shifted"], 1)
                else:
                    nc.vector.tensor_tensor(e[:, r], src, mx[:, b % 2].unsqueeze(1).unsqueeze(3).broadcast_to([D, NS, 8, S]), ALU.subtract).then_inc(s["shifted"], 1)

            for n in range(6):
                piece(0, 0, n)
            for b in range(AHEAD):
                softmax(0, 0, b)

            def slot(j, p, b, more):
                n = j * B + b
                if more or b + AHEAD < B:
                    softmax(*at(j, p, b + AHEAD))
                dve.wait_ge(s["pv_mm"], n + 1)
                sums = pv[:, b % 2, :2 * 8 * (HD + 1)].rearrange("p (n d) -> p n d", d=HD + 1)
                nc.vector.reciprocal(rden[:, b % 2], sums[:, :, HD]).then_inc(s["rden_done"], 1)
                dve.wait_ge(s["rden_done"], n + 1)
                out = slice((b % 2) * S, (b % 2) * S + S)
                for g in range(2):
                    f = slice(g * S, g * S + S)
                    last = nc.vector.tensor_tensor(attn[out, p, b // 2, g * S:(g + 1) * S].rearrange("p (n d) -> p n d", d=HD),
                                                   sums[f, g * 8:(g + 1) * 8, :HD], rden[f, b % 2, g * 8:(g + 1) * 8].unsqueeze(2).broadcast_to([S, 8, HD]), ALU.mult)
                last.then_inc(s["normed"], 1)
                if more and b:
                    piece(j + 1, 1 - p, b - 1)
                if b == B - 1:
                    res = x_res[:, p].rearrange("p t f -> p (t f)")
                    new = x_new[:].rearrange("p t f -> p (t f)")
                    dve.wait_ge(saved, 16 * j)
                    if project:
                        dve.wait_ge(s["fin_mm"], j + 1)
                        if layer == 2:
                            nc.vector.tensor_tensor(new, pv[:, 1], res, ALU.add).then_inc(s["fin_added"], 1)
                            dve.wait_ge(s["fin_added"], j + 1)
                            nc.vector.tensor_tensor(x_new[:], x_new[:], bo[:].unsqueeze(1).broadcast_to([D, NT, D]), ALU.add).then_inc(s["new_done"], 1)
                        else:
                            nc.vector.tensor_tensor(new, pv[:, 1], res, ALU.add).then_inc(s["new_done"], 1)
                    else:
                        dve.wait_ge(s["normed"], (j + 1) * B)
                        nc.vector.tensor_tensor(new, attn[:, p].rearrange("p t f -> p (t f)"), res, ALU.add).then_inc(s["new_done"], 1)

            schedule(dve, slot)

        @block.tensor
        def _(pe):
            pe.wait_ge(weights_in, LOADS)
            pe.wait_ge(pool_consts, 5)

            def turn_inputs(j):
                pe.wait_ge(s["norm_done"], j + 1)
                pe.wait_ge(s["v_done"], j * len(V_STEPS))
                for t in range(NT):
                    last = nc.tensor.transpose(front[:, 0, t * D:(t + 1) * D], xn[:, t], ident[:])
                last.then_inc(s["turned_x"], 1)
                pe.wait_ge(c_loaded, 16 * (j + 1))
                for t in range(NT):
                    last = nc.tensor.transpose(front[:, 1, t * D:(t + 1) * D], c_raw[:, t], ident[:])
                last.then_inc(s["turned_c"], 1)

            def keys_queries(j):
                if rope:
                    for (mm, done), a, wt, k in ((("q_mm", "xT_done"), xT, wq, 0), (("k_mm", "cT_done"), cT, wk, 1)):
                        pe.wait_ge(s[done], j + 1)
                        for t in range(NT):
                            last = nc.tensor.matmul(front[:, k, t * D:(t + 1) * D], a[:, t * D:(t + 1) * D], wt[:], start=True, stop=True)
                        last.then_inc(s[mm], 1)
                else:
                    pe.wait_ge(s["xT_done"], j + 1)
                    nc.tensor.matmul(front[:, 0], wq[:], xT[:], start=True, stop=True).then_inc(s["q_mm"], 1)
                    pe.wait_ge(s["cT_done"], j + 1)
                    nc.tensor.matmul(front[:, 1], wk[:], cT[:], start=True, stop=True).then_inc(s["k_mm"], 1)
                    if own_keys:
                        pe.wait_ge(s["q_done"], j + 1)
                        nc.tensor.matmul(front[:, 0], wk[:], xT[:], start=True, stop=True).then_inc(s["own_k_mm"], 1)

            def turn_roped(j):
                pe.wait_ge(s["roped"], j + 1)
                for k, name in enumerate(("turned_q", "turned_k")):
                    for t in range(NT):
                        last = nc.tensor.transpose(front[:, k, t * D:(t + 1) * D], qk[:, k, t * H:(t + 1) * H].rearrange("p n d -> p (n d)"), ident[:])
                    last.then_inc(s[name], 1)

            def values(j, steps):
                for n in steps:
                    src, half = V_STEPS[n]
                    if n < 2:
                        pe.wait_ge(s["twice_done"], j + 1)
                        pe.wait_ge(s["own_k_done" if own_keys and n == 0 else "k_done"], j + 1)
                    else:
                        pe.wait_ge(s["v_done"], j * len(V_STEPS) + n - 1)
                    for b in range(4):
                        feats = twice[src][:, half * 4 + b].rearrange("p a k -> p (a k)")
                        last = nc.tensor.matmul(front[:, n % 2, b * D:(b + 1) * D], feats, wv[:], start=True, stop=True)
                    last.then_inc(s["v_mm"], 1)

            def piece(j, n):
                if n == 1:
                    turn_inputs(j)
                    keys_queries(j)
                if n == 3 and rope:
                    turn_roped(j)
                if n == 4:
                    values(j, range(0, NS))
                if n == 5:
                    values(j, range(NS, 2 * NS))

            def scores(j, p, b):
                n = j * B + b
                pe.wait_ge(s["q_done"], j + 1)
                pe.wait_ge(s["masked"], n + 1)
                for src in range(NS):
                    last = nc.tensor.matmul(sc[:, b % AHEAD, src], qg[:, p, b].rearrange("p g q -> p (g q)"),
                                            kn[:, b % 2, src].rearrange("p n k -> p (n k)"), start=True, stop=True)
                last.then_inc(s["scores_mm"], 1)

            for n in range(6):
                piece(0, n)
            for b in range(AHEAD):
                scores(0, 0, b)

            def slot(j, p, b, more):
                n = j * B + b
                pe.wait_ge(s["exp_done"], n + 1)
                for src in range(NS):
                    pe.wait_ge(s["pt_done"], n * NS)
                    for k in range(4):
                        last = nc.tensor.transpose(turn[:, src, k * D:(k + 1) * D], e[:, b % RING, src, 2 * k:2 * k + 2].rearrange("p n k -> p (n k)"), ident[:])
                    last.then_inc(s["turned_e"], 1)
                if more or b + AHEAD < B:
                    scores(*at(j, p, b + AHEAD))
                if b == 0:
                    pe.wait_ge(s["new_done"], j)
                    pe.wait_ge(s["v_done"], (j + 1) * len(V_STEPS))
                else:
                    pe.wait_ge(s["normed"], n - 1)
                out = pv[:, b % 2, :144].rearrange("p (g m x) -> p g m x", g=2, m=4)
                for src in range(NS):
                    pe.wait_ge(s["pt_done"], n * NS + src + 1)
                    for k in range(4):
                        values_of = vx[:, p, src, b].rearrange("p (g m) a d -> p g m (a d)", g=2)[:, :, k]
                        last = nc.tensor.matmul(out[:, :, k], pt[:, b % 2, src, k], values_of, start=(src == 0 and k == 0), stop=(src == NS - 1), skip_group_check=True)
                last.then_inc(s["pv_mm"], 1)
                if more and b:
                    piece(j + 1, b - 1)
                if b == B - 1 and project:
                    pe.wait_ge(s["normed"], n + 1)
                    for t in range(NT):
                        last = nc.tensor.transpose(pv[:, 0, t * D:(t + 1) * D], attn[:, p, t], ident[:])
                    last.then_inc(s["fin_turned"], 1)
                    pe.wait_ge(s["aT_done"], j + 1)
                    for t in range(NT):
                        last = nc.tensor.matmul(pv[:, 1, t * D:(t + 1) * D], aT[:, t * D:(t + 1) * D], wo[:], start=True, stop=True)
                    last.then_inc(s["fin_mm"], 1)

            schedule(pe, slot)


E4 = 4


def layernorm_experts(nc, c, ph, x_in, w, x_out):
    U = 2
    with ExitStack() as ctx:
        m = Space(nc, ctx, ph)
        ident, ones = m.sb("ident", [D, D]), m.sb("ones", [D, D])
        gw, gb, falling = m.sb("gw", [D, E4]), m.sb("gb", [D, E4]), m.sb("falling", [D, E4])
        w1, w2 = m.sb("w1", [D, E4, D]), m.sb("w2", [D, E4, D])
        b1, g1, be1 = (m.sb(n, [D, E4]) for n in ("b1", "g1", "be1"))
        b2, g2, be2 = m.sb("b2", [D, E4, D]), m.sb("g2", [D, E4, D]), m.sb("be2", [E4, D])
        wmean = m.sb("wmean", [D, 4, E4])
        minus_half, euler = m.sb("minus_half", [D, NT]), m.sb("euler", [D, NT])
        x, xn, xT = m.sb("x", [D, U, NT, D]), m.sb("xn", [D, U, NT, D]), m.sb("xT", [D, U, GROUP])
        stats, parts = m.sb("stats", [D, U, NT, 6]), m.sb("parts", [D, U, 3, NT])
        mean, power, rstd = (m.sb(n, [D, U, NT]) for n in ("mean", "power", "rstd"))
        score, eq, hot1, hot2, share, left = (m.sb(n, [D, U, NT, E4]) for n in ("score", "eq", "hot1", "hot2", "share", "left"))
        top1, top2, pick, ratio, w_first, w_second = (m.sb(n, [D, U, NT]) for n in ("top1", "top2", "pick", "ratio", "w_first", "w_second"))
        sq, std, hid = (m.sb(n, [D, U, E4, GROUP]) for n in ("sq", "std", "hid"))
        y, ysq = m.sb("y", [D, U, NT, E4, D]), m.sb("ysq", [D, 2, E4 * D])
        ssq = m.sb("ssq", [D, U, NT, E4])
        shareT = m.sb("shareT", [E4, U, GROUP])
        mixed, x_new, x_sum = (m.sb(n, [D, U, NT, D]) for n in ("mixed", "x_new", "x_sum"))
        ln_eps = m.sb("ln_eps", [D, 1])
        bank = m.psum("bank", [D, U, 4, GROUP])

        loads = [(ident[:], c["ident"]), (ones[:], c["ones"]), (gw[:], w["gate_W"]), (gb[:], w["gate_b"].broadcast_to([D, E4])),
                 (falling[:], c["falling"][:, :E4]), (b1[:], w["b1T"]), (g1[:], w["g1T"]), (be1[:], w["be1T"]), (be2[:], w["be2"]),
                 (w1[:], w["W1"].rearrange("(e p) f -> p e f", e=E4)), (w2[:], w["W2"].rearrange("(e p) f -> p e f", e=E4)),
                 (b2[:].rearrange("p e f -> p (e f)"), w["b2"].broadcast_to([D, E4 * D])),
                 (g2[:].rearrange("p e f -> p (e f)"), w["g2"].broadcast_to([D, E4 * D]))]
        LOADS = 16 * len(loads)
        weights_in, pool_consts, mean_steps, b1_mm = (m.sem(n) for n in ("weights_in", "pool_consts", "mean_steps", "b1_mm"))
        x_loaded = [m.sem(f"x_loaded{u}") for u in range(U)]
        saved = [m.sem(f"saved{u}") for u in range(U)]
        s = {k: m.sem(k) for k in (
            "stats_done parts_done mean_done power_done rstd_done norm_done turned xT_done logits_mm score_done top1_done eq1_done "
            "eqw1_done pick1_done hot1_done left_done top2_done eq2_done eqw2_done pick2_done hot2_done diff_done ratio_done "
            "den_done first_done second_done share1_done share_done hid_mm sq_done var_mm std_done inv_done scaled_done hid_done "
            "y_mm y_done ysq_done ssq_done var2_done std2_done inv2_done factor_done weighed gained mixed_done share_turned "
            "shareT_done offset_mm sum_done sum2_done new_done").split()}
        block = ctx.enter_context(nc.Block())
        STEPS = GROUPS // U

        def pair_count(i, u, e):
            return i * (U * E4) + (e // 2) * (2 * U) + u * 2 + e % 2 + 1

        @block.sync
        def _(sp):
            for u in range(U):
                sp.dma_start(x[:, u], rows(x_in, u * GROUP)).then_inc(x_loaded[u], 16)
            for dst, src in loads:
                sp.dma_start(dst, src).then_inc(weights_in, 16)

            def body(i, last=False):
                for u in range(U):
                    if not last:
                        sp.wait_ge(s["mixed_done"], (i * U + u) * NT + NT)
                        sp.dma_start(x[:, u], rows(x_in, (i + 1) * U * GROUP + u * GROUP)).then_inc(x_loaded[u], 16)
                for u in range(U):
                    sp.wait_ge(s["new_done"], i * U + u + 1)
                    sp.dma_start(rows(x_out, i * U * GROUP + u * GROUP), x_new[:, u]).then_inc(saved[u], 16)

            with sp.Fori(0, STEPS - 1) as i:
                body(i)
            body(STEPS - 1, last=True)
            for u in range(U):
                sp.wait_ge(saved[u], 16 * STEPS)

        @block.gpsimd
        def _(pool):
            nc.gpsimd.memset(minus_half[:], -0.5).then_inc(pool_consts, 1)
            nc.gpsimd.memset(euler[:], float(np.e)).then_inc(pool_consts, 1)
            pool.wait_ge(pool_consts, 2)
            pool.wait_ge(weights_in, LOADS)
            with pool.Fori(0, STEPS) as i:
                for u in range(U):
                    k = i * U + u + 1
                    pool.wait_ge(s["power_done"], k)
                    nc.gpsimd.tensor_tensor(rstd[:, u], power[:, u], minus_half[:], ALU.pow).then_inc(s["rstd_done"], 1)
                for u in range(U):
                    k = i * U + u + 1
                    pool.wait_ge(s["diff_done"], k)
                    nc.gpsimd.tensor_tensor(ratio[:, u], euler[:], ratio[:, u], ALU.pow).then_inc(s["ratio_done"], 1)
                for u in range(U):
                    for t in range(NT):
                        k = (i * U + u) * NT + t + 1
                        if t == 0:
                            pool.wait_ge(s["factor_done"], i * U + u + 1)
                        nc.gpsimd.tensor_tensor(y[:, u, t], y[:, u, t], ssq[:, u, t].unsqueeze(2).broadcast_to([D, E4, D]), ALU.mult).then_inc(s["weighed"], 1)
                        pool.wait_ge(s["weighed"], k)
                        nc.gpsimd.tensor_tensor(y[:, u, t], y[:, u, t], g2[:], ALU.mult).then_inc(s["gained"], 1)

        @block.scalar
        def _(act):
            act.wait_ge(mean_steps, 4)
            with act.Fori(0, STEPS) as i:
                for u in range(U):
                    act.wait_ge(s["turned"], i * U + u + 1)
                    nc.scalar.activation(xT[:, u], bank[:, u, 0], ACT.Copy).then_inc(s["xT_done"], 1)
                for pair in range(2):
                    both = (2 * pair, 2 * pair + 1)
                    for u in range(U):
                        for e in both:
                            act.wait_ge(s["hid_mm"], pair_count(i, u, e))
                            nc.scalar.activation(sq[:, u, e], bank[:, u, 2 + e % 2], ACT.Square, bias=b1[:, e:e + 1]).then_inc(s["sq_done"], 1)
                    for u in range(U):
                        for e in both:
                            act.wait_ge(s["var_mm"], pair_count(i, u, e))
                            nc.scalar.activation(std[:, u, e], bank[:, u, e % 2], ACT.Sqrt, scale=1.0 / D, bias=ln_eps[:]).then_inc(s["std_done"], 1)
                    for u in range(U):
                        for e in both:
                            act.wait_ge(s["scaled_done"], pair_count(i, u, e))
                            nc.scalar.activation(hid[:, u, e], sq[:, u, e], ACT.Relu, scale=g1[:, e:e + 1], bias=be1[:, e:e + 1]).then_inc(s["hid_done"], 1)
                for u in range(U):
                    for t in range(NT):
                        k = (i * U + u) * NT + t + 1
                        act.wait_ge(s["y_done"], k)
                        act.wait_ge(s["ssq_done"], k - 2 if u * NT + t >= 2 else i * U * NT)
                        nc.scalar.activation(ysq[:, t % 2], y[:, u, t].rearrange("p e f -> p (e f)"), ACT.Square).then_inc(s["ysq_done"], 1)
                    act.wait_ge(s["var2_done"], i * U + u + 1)
                    nc.scalar.activation(ssq[:, u], ssq[:, u], ACT.Sqrt).then_inc(s["std2_done"], 1)
                    act.wait_ge(s["share_turned"], i * U + u + 1)
                    nc.scalar.activation(shareT[:, u], bank[:E4, u, 0], ACT.Copy).then_inc(s["shareT_done"], 1)

        @block.vector
        def _(dve):
            dve.wait_ge(weights_in, LOADS)
            dve.wait_ge(pool_consts, 2)
            nc.vector.memset(ln_eps[:], LN_EPS)
            nc.vector.tensor_reduce(wmean[:, 0], w1[:], AX.X, ALU.add)
            nc.vector.tensor_reduce(wmean[:, 1], w2[:], AX.X, ALU.add)
            nc.vector.tensor_reduce(wmean[:, 2], b2[:], AX.X, ALU.add).then_inc(mean_steps, 1)
            dve.wait_ge(b1_mm, 1)
            nc.vector.tensor_copy(wmean[:, 3], bank[:, 0, 0, :E4]).then_inc(mean_steps, 1)
            dve.wait_ge(mean_steps, 2)
            nc.vector.tensor_scalar(wmean[:], wmean[:], 1.0 / D, None, ALU.mult).then_inc(mean_steps, 1)
            dve.wait_ge(mean_steps, 3)
            for a, k in ((w1, 0), (w2, 1), (b2, 2)):
                nc.vector.tensor_tensor(a[:], a[:], wmean[:, k].unsqueeze(2).broadcast_to([D, E4, D]), ALU.subtract)
            nc.vector.tensor_tensor(b1[:], b1[:], wmean[:, 3], ALU.subtract).then_inc(mean_steps, 1)
            dve.wait_ge(mean_steps, 4)
            with dve.Fori(0, STEPS) as i:
                for u in range(U):
                    dve.wait_ge(x_loaded[u], 16 * (i + 1))
                    moments(nc, dve, x[:, u], NT, stats[:, u], parts[:, u], mean[:, u], power[:, u], s, i * U + u + 1)
                for u in range(U):
                    dve.wait_ge(s["rstd_done"], i * U + u + 1)
                    for t in range(NT):
                        last = nc.vector.tensor_scalar(xn[:, u, t], x[:, u, t], mean[:, u, t:t + 1], rstd[:, u, t:t + 1], ALU.subtract, ALU.mult)
                    last.then_inc(s["norm_done"], 1)
                for u in range(U):
                    k = i * U + u + 1
                    per_tile = lambda a: a[:, u].unsqueeze(2).broadcast_to([D, NT, E4])
                    per_expert = lambda a: a.unsqueeze(1).broadcast_to([D, NT, E4])
                    dve.wait_ge(s["logits_mm"], k)
                    nc.vector.tensor_tensor(score[:, u], bank[:, u, 1, :NT * E4].rearrange("p (t e) -> p t e", t=NT), per_expert(gb[:]), ALU.add).then_inc(s["score_done"], 1)
                    dve.wait_ge(s["score_done"], k)
                    for n, (src, top, hot) in enumerate(((score, top1, hot1), (left, top2, hot2)), 1):
                        if n == 2:
                            nc.vector.scalar_tensor_tensor(left[:, u], hot1[:, u], -3.0e38, score[:, u], ALU.mult, ALU.add).then_inc(s["left_done"], 1)
                            dve.wait_ge(s["left_done"], k)
                        nc.vector.tensor_reduce(top[:, u], src[:, u], AX.X, ALU.max).then_inc(s[f"top{n}_done"], 1)
                        dve.wait_ge(s[f"top{n}_done"], k)
                        nc.vector.tensor_tensor(eq[:, u], src[:, u], per_tile(top), ALU.is_equal).then_inc(s[f"eq{n}_done"], 1)
                        dve.wait_ge(s[f"eq{n}_done"], k)
                        nc.vector.tensor_tensor(eq[:, u], eq[:, u], per_expert(falling[:]), ALU.mult).then_inc(s[f"eqw{n}_done"], 1)
                        dve.wait_ge(s[f"eqw{n}_done"], k)
                        nc.vector.tensor_reduce(pick[:, u], eq[:, u], AX.X, ALU.max).then_inc(s[f"pick{n}_done"], 1)
                        dve.wait_ge(s[f"pick{n}_done"], k)
                        nc.vector.tensor_tensor(hot[:, u], eq[:, u], per_tile(pick), ALU.is_equal).then_inc(s[f"hot{n}_done"], 1)
                        dve.wait_ge(s[f"hot{n}_done"], k)
                    nc.vector.tensor_tensor(ratio[:, u], top2[:, u], top1[:, u], ALU.subtract).then_inc(s["diff_done"], 1)
                    nc.vector.tensor_tensor(x_sum[:, u], x[:, u], xn[:, u], ALU.add).then_inc(s["sum_done"], 1)
                    dve.wait_ge(s["ratio_done"], k)
                    nc.vector.tensor_scalar(w_first[:, u], ratio[:, u], 1.0, None, ALU.add).then_inc(s["den_done"], 1)
                    dve.wait_ge(s["den_done"], k)
                    nc.vector.reciprocal(w_first[:, u], w_first[:, u]).then_inc(s["first_done"], 1)
                    dve.wait_ge(s["first_done"], k)
                    nc.vector.tensor_tensor(w_second[:, u], ratio[:, u], w_first[:, u], ALU.mult).then_inc(s["second_done"], 1)
                    dve.wait_ge(s["second_done"], k)
                    nc.vector.tensor_tensor(hot1[:, u], hot1[:, u], per_tile(w_first), ALU.mult)
                    nc.vector.tensor_tensor(hot2[:, u], hot2[:, u], per_tile(w_second), ALU.mult).then_inc(s["share1_done"], 1)
                    dve.wait_ge(s["share1_done"], k)
                    nc.vector.tensor_tensor(share[:, u], hot1[:, u], hot2[:, u], ALU.add).then_inc(s["share_done"], 1)
                for pair in range(2):
                    for u in range(U):
                        for e in (2 * pair, 2 * pair + 1):
                            n = pair_count(i, u, e)
                            dve.wait_ge(s["std_done"], n)
                            nc.vector.reciprocal(std[:, u, e], std[:, u, e]).then_inc(s["inv_done"], 1)
                            dve.wait_ge(s["inv_done"], n)
                            nc.vector.scalar_tensor_tensor(sq[:, u, e], bank[:, u, 2 + e % 2], b1[:, e:e + 1], std[:, u, e], ALU.add, ALU.mult).then_inc(s["scaled_done"], 1)
                for u in range(U):
                    k = i * U + u + 1
                    for t in range(NT):
                        n = (i * U + u) * NT + t + 1
                        dve.wait_ge(s["y_mm"], n)
                        nc.vector.tensor_tensor(y[:, u, t], bank[:, u, t].rearrange("p (e f) -> p e f", e=E4), b2[:], ALU.add).then_inc(s["y_done"], 1)
                        if t:
                            dve.wait_ge(s["ysq_done"], n - 1)
                            nc.vector.tensor_reduce(ssq[:, u, t - 1], ysq[:, (t - 1) % 2].rearrange("p (e f) -> p e f", e=E4), AX.X, ALU.add).then_inc(s["ssq_done"], 1)
                    dve.wait_ge(s["ysq_done"], n)
                    nc.vector.tensor_reduce(ssq[:, u, NT - 1], ysq[:, (NT - 1) % 2].rearrange("p (e f) -> p e f", e=E4), AX.X, ALU.add).then_inc(s["ssq_done"], 1)
                    dve.wait_ge(s["ssq_done"], n)
                    nc.vector.tensor_scalar(ssq[:, u], ssq[:, u], 1.0 / D, LN_EPS, ALU.mult, ALU.add).then_inc(s["var2_done"], 1)
                    dve.wait_ge(s["std2_done"], k)
                    nc.vector.reciprocal(ssq[:, u], ssq[:, u]).then_inc(s["inv2_done"], 1)
                    dve.wait_ge(s["inv2_done"], k)
                    nc.vector.tensor_tensor(ssq[:, u], ssq[:, u], share[:, u], ALU.mult).then_inc(s["factor_done"], 1)
                for u in range(U):
                    k = i * U + u + 1
                    for t in range(NT):
                        dve.wait_ge(s["gained"], (i * U + u) * NT + t + 1)
                        nc.vector.tensor_reduce(mixed[:, u, t], y[:, u, t].rearrange("p e f -> p f e"), AX.X, ALU.add).then_inc(s["mixed_done"], 1)
                    dve.wait_ge(s["mixed_done"], (i * U + u) * NT + NT)
                    nc.vector.tensor_tensor(mixed[:, u], mixed[:, u], x_sum[:, u], ALU.add).then_inc(s["sum2_done"], 1)
                    dve.wait_ge(s["sum2_done"], k)
                    dve.wait_ge(s["offset_mm"], k)
                    dve.wait_ge(saved[u], 16 * i)
                    nc.vector.tensor_tensor(x_new[:, u].rearrange("p t f -> p (t f)"), bank[:, u, 1], mixed[:, u].rearrange("p t f -> p (t f)"), ALU.add).then_inc(s["new_done"], 1)

        @block.tensor
        def _(pe):
            pe.wait_ge(weights_in, LOADS)
            nc.tensor.matmul(bank[:, 0, 0, :E4], ones[:], b1[:], start=True, stop=True).then_inc(b1_mm, 1)
            pe.wait_ge(mean_steps, 4)
            with pe.Fori(0, STEPS) as i:
                for u in range(U):
                    pe.wait_ge(s["norm_done"], i * U + u + 1)
                    pe.wait_ge(s["new_done"], i * U)
                    for t in range(NT):
                        last = nc.tensor.transpose(bank[:, u, 0, t * D:(t + 1) * D], xn[:, u, t], ident[:])
                    last.then_inc(s["turned"], 1)
                for u in range(U):
                    pe.wait_ge(s["xT_done"], i * U + u + 1)
                    for t in range(NT):
                        last = nc.tensor.matmul(bank[:, u, 1, t * E4:(t + 1) * E4], xT[:, u, t * D:(t + 1) * D], gw[:], start=True, stop=True)
                    last.then_inc(s["logits_mm"], 1)
                for pair in range(2):
                    both = (2 * pair, 2 * pair + 1)
                    for u in range(U):
                        for e in both:
                            if pair:
                                pe.wait_ge(s["scaled_done"], pair_count(i, u, e - 2))
                            nc.tensor.matmul(bank[:, u, 2 + e % 2], w1[:, e], xT[:, u], start=True, stop=True).then_inc(s["hid_mm"], 1)
                    for u in range(U):
                        for e in both:
                            pe.wait_ge(s["sq_done"], pair_count(i, u, e))
                            if pair:
                                pe.wait_ge(s["std_done"], pair_count(i, u, e - 2))
                            elif e == 1:
                                pe.wait_ge(s["score_done"], i * U + u + 1)
                            nc.tensor.matmul(bank[:, u, e % 2], ones[:], sq[:, u, e], start=True, stop=True).then_inc(s["var_mm"], 1)
                for u in range(U):
                    pe.wait_ge(s["hid_done"], pair_count(i, u, E4 - 1))
                    for t in range(NT):
                        for e in range(E4):
                            last = nc.tensor.matmul(bank[:, u, t, e * D:(e + 1) * D], hid[:, u, e, t * D:(t + 1) * D], w2[:, e], start=True, stop=True)
                        last.then_inc(s["y_mm"], 1)
                for u in range(U):
                    k = i * U + u + 1
                    pe.wait_ge(s["share_done"], k)
                    pe.wait_ge(s["y_done"], (i * U + u) * NT + NT)
                    for t in range(NT):
                        last = nc.tensor.transpose(bank[:E4, u, 0, t * D:(t + 1) * D], share[:, u, t], ident[:])
                    last.then_inc(s["share_turned"], 1)
                    pe.wait_ge(s["shareT_done"], k)
                    for t in range(NT):
                        last = nc.tensor.matmul(bank[:, u, 1, t * D:(t + 1) * D], shareT[:, u, t * D:(t + 1) * D], be2[:], start=True, stop=True)
                    last.then_inc(s["offset_mm"], 1)


def combine(nc, ph, x_in, ye, pos_in, x_out):
    RING = 4
    with ExitStack() as ctx:
        m = Space(nc, ctx, ph)
        pos = m.sb("pos", [D, TOKENS // D], I32)
        x, y, x_new = (m.sb(n, [D, RING, NT, D]) for n in ("x", "y", "x_new"))
        pos_loaded, added = m.sem("pos_loaded"), m.sem("added")
        x_loaded, gathered, saved = ([m.sem(f"{n}{r}") for r in range(RING)] for n in ("x_loaded", "gathered", "saved"))
        block = ctx.enter_context(nc.Block())

        @block.sync
        def _(sp):
            sp.dma_start(pos[:], pos_in).then_inc(pos_loaded, 16)
            for g in range(GROUPS):
                if g >= RING:
                    sp.wait_ge(added, g - RING + 1)
                sp.dma_start(x[:, g % RING], rows(x_in, g * GROUP)).then_inc(x_loaded[g % RING], 16)

        @block.gpsimd
        def _(pool):
            pool.wait_ge(pos_loaded, 16)
            for g in range(GROUPS):
                if g >= RING:
                    pool.wait_ge(added, g - RING + 1)
                for t in range(NT):
                    pool.indirect_dma_start(out=y[:, g % RING, t], out_offset=None, in_=ye,
                                            in_offset=bass.IndirectOffsetOnAxis(ap=pos[:, g * NT + t:g * NT + t + 1], axis=0)).then_inc(gathered[g % RING], 16)

        @block.vector
        def _(dve):
            for g in range(GROUPS):
                r, turn = g % RING, g // RING + 1
                dve.wait_ge(x_loaded[r], 16 * turn)
                dve.wait_ge(gathered[r], 16 * NT * turn)
                if turn > 1:
                    dve.wait_ge(saved[r], 16 * (turn - 1))
                nc.vector.tensor_tensor(x_new[:, r], y[:, r], x[:, r], ALU.add).then_inc(added, 1)

        @block.scalar
        def _(act):
            for g in range(GROUPS):
                act.wait_ge(added, g + 1)
                act.dma_start(rows(x_out, g * GROUP), x_new[:, g % RING]).then_inc(saved[g % RING], 16)
            for r in range(RING):
                act.wait_ge(saved[r], 16 * (GROUPS // RING))


def build(nc, t, x, out):
    def scratch(name, shape, dt=F32):
        return nc.dram_tensor(name, shape, dt).ap()

    x1, x2, x3, x4, x5, x6 = (scratch(f"x_{n}", (TOKENS, D)) for n in range(1, 7))
    xe, ye = scratch("expert_in", (XE_ROWS, D)), scratch("expert_out", (XE_ROWS, D))
    pos, prob, table = scratch("pos", (D, TOKENS // D), I32), scratch("prob", (D, TOKENS // D)), scratch("table", (1, SLOTS), I32)
    part = lambda prefix: {k[len(prefix):]: v for k, v in t.items() if k.startswith(prefix)}
    expert = lambda prefix: [t[prefix + k] for k in ("w1", "b1", "w2", "b2")]

    slot_attention(nc, t, x, t["ctx"], x1)
    route(nc, t, "route0", x1, "cosine", xe, pos, prob, table, True, True)
    experts(nc, t, "experts0", xe, table, expert("L0f_"), ye, True)

    w = part("L1a_")
    w["norm"] = (w["qn"], w["kn"])
    attention(nc, t, "att1", 1, x1, t["ctx"], w, x2, (ye, pos, prob))
    layernorm_experts(nc, t, "lnx1", x2, part("L1f_"), x3)

    attention(nc, t, "att2", 2, x3, t["ctx"], part("L2a_"), x4)
    route(nc, t, "route2", x4, (t["L2f_gw"], t["L2f_gb"]), xe, pos, prob, table, True, False)
    experts(nc, t, "experts2", xe, table, expert("L2f_"), ye, False)

    attention(nc, t, "att3", 3, x4, t["ctx"], part("L3a_"), x5, (ye, pos, prob))
    route(nc, t, "route3", x5, (t["L3f_gw"], t["L3f_gb"]), xe, pos, prob, table, False, False)
    experts(nc, t, "experts3", xe, table, expert("L3f_"), ye, False)
    combine(nc, "combine3", x5, ye, pos, out)


def rope_tables():
    out = np.zeros((D, 4, HD), np.float32)
    for k, (theta, scale) in enumerate(((32.0, HD ** -0.5), (1000.0, 1.0))):
        freqs = np.float32(theta) ** (-np.arange(0, HD, 2, dtype=np.float32) / HD)
        angle = np.arange(S, dtype=np.float32)[:, None] * freqs[None, :]
        cos, sin = np.cos(angle), np.sin(angle)
        out[:, 2 * k] = np.tile(np.concatenate([cos, cos], 1), (2, 1)) * scale
        out[:, 2 * k + 1] = np.tile(np.concatenate([-sin, sin], 1), (2, 1)) * scale
    return out


def constants():
    ar = np.arange
    return {
        "ident": np.eye(D, dtype=np.float32),
        "ones": np.ones((D, D), np.float32),
        "pair_ones": np.kron(np.eye(2, dtype=np.float32), np.ones((S, S), np.float32)),
        "pair_ident": np.tile(np.eye(S, dtype=np.float32), (2, 1)),
        "before": np.triu(np.ones((D, D), np.float32), 1),
        "falling": np.tile(ar(E, 0, -1, dtype=np.float32), (D, 1)),
        "steps": np.tile(ar(TOKENS // SLOT, dtype=np.float32) * SLOT, (D, 1)),
        "slot_no": np.tile(ar(SLOTS, dtype=np.float32), (D, 1)),
        "n_mask": (((ar(D) // HD) % 8)[:, None] == ar(8)[None]).astype(np.float32),
        "rope": rope_tables(),
        "zero_row": np.zeros((1, E), np.float32),
    }


def layout(a):
    col = lambda v: v.reshape(D, 1)
    row = lambda v: v.reshape(1, -1)
    chunks = lambda b: b.reshape(E, 4, D).transpose(0, 2, 1).reshape(E * D, 4)
    second = lambda w: w.reshape(E, 4, D, D).transpose(0, 2, 1, 3).reshape(E * D, 4 * D)
    t = {
        "ctx": a["ctx_1024"].reshape(TOKENS, D),
        "L0_Wk": a["L0_xattn_Wk"], "L0_Wq": a["L0_xattn_Wq"], "L0_Wv": a["L0_xattn_Wv"],
        "L0_wihT": a["L0_xattn_gru_wih"].T, "L0_whhT": a["L0_xattn_gru_whh"].T,
        "L0_bih": a["L0_xattn_gru_bih"].reshape(3, D).T, "L0_bhh": a["L0_xattn_gru_bhh"].reshape(3, D).T,
        "L0_w_slot": col(a["L0_xattn_slot_norm_w"]), "L0_w_in": col(a["L0_xattn_input_norm_w"]),
        "L0_w_redT": a["L0_ffn_w_red"].T, "L0_wg": a["L0_ffn_wg"],
        "L0f_w1": a["L0_ffn_w1"].reshape(E * D, -1), "L0f_b1": chunks(a["L0_ffn_b1"]),
        "L0f_w2": second(a["L0_ffn_w2"]), "L0f_b2": a["L0_ffn_b2"],
        "L1a_q": a["L1_xattn_Wq"].T, "L1a_k": a["L1_xattn_Wk"].T, "L1a_v": a["L1_xattn_Wv"].T, "L1a_o": a["L1_xattn_Wo"].T,
        "L1a_qn": row(a["L1_xattn_q_norm_w"]), "L1a_kn": row(a["L1_xattn_k_norm_w"]),
        "L1f_gate_W": a["L1_ffn_gate_W"], "L1f_gate_b": row(a["L1_ffn_gate_b"]),
        "L1f_W1": a["L1_ffn_W1"].reshape(E4 * D, D), "L1f_W2": a["L1_ffn_W2"].reshape(E4 * D, D),
        "L1f_b1T": a["L1_ffn_b1"].T, "L1f_g1T": a["L1_ffn_g1"].T, "L1f_be1T": a["L1_ffn_be1"].T,
        "L1f_b2": row(a["L1_ffn_b2"]), "L1f_g2": row(a["L1_ffn_g2"]), "L1f_be2": a["L1_ffn_be2"],
        "L2a_q": a["L2_xattn_W_q"], "L2a_k": a["L2_xattn_W_k"], "L2a_v": a["L2_xattn_W_v"], "L2a_o": a["L2_xattn_W_o"],
        "L2a_bq": col(a["L2_xattn_b_q"]), "L2a_bk": col(a["L2_xattn_b_k"]), "L2a_bv": row(a["L2_xattn_b_v"]),
        "L2a_bo": row(a["L2_xattn_b_o"]), "L2a_mask": np.ascontiguousarray(a["mask_SxS2_bk1"]).view(np.uint32),
        "L2f_gw": a["L2_ffn_router_W"], "L2f_gb": row(a["L2_ffn_router_b"]),
        "L2f_w1": a["L2_ffn_W1"].reshape(E * D, -1), "L2f_b1": chunks(a["L2_ffn_b1"]),
        "L2f_w2": second(a["L2_ffn_W2"]), "L2f_b2": a["L2_ffn_b2"],
        "L3a_q": a["L3_xattn_Wq"].T, "L3a_k": a["L3_xattn_Wk"].T, "L3a_v": a["L3_xattn_Wv"].T,
        "L3a_bq": col(a["L3_xattn_bq"]), "L3a_bk": col(a["L3_xattn_bk"]), "L3a_bv": row(a["L3_xattn_bv"]),
        "L3f_gw": a["L3_ffn_gate_w"].T, "L3f_gb": row(a["L3_ffn_gate_b"]),
        "L3f_w1": a["L3_ffn_w1"].transpose(0, 2, 1).reshape(E * D, -1), "L3f_b1": chunks(a["L3_ffn_b1"]),
        "L3f_w2": second(a["L3_ffn_w2"].transpose(0, 2, 1)), "L3f_b2": a["L3_ffn_b2"],
    }
    return {k: np.ascontiguousarray(v) for k, v in t.items()}


def kernel(**inputs):
    import concourse.bacc as bacc
    from concourse.bass_utils import run_bass_kernel_spmd

    a = {k: np.asarray(v) for k, v in inputs.items()}
    arrays = {"x": a["x"].reshape(TOKENS, D), **layout(a), **constants()}
    nc = bacc.Bacc("TRN2", target_bir_lowering=False, num_devices=1)
    t = {k: nc.dram_tensor(f"in_{k}", v.shape, mybir.dt.from_np(v.dtype), kind="ExternalInput").ap() for k, v in arrays.items()}
    out = nc.dram_tensor("out", (TOKENS, D), F32, kind="ExternalOutput").ap()
    build(nc, t, t["x"], out)
    r = run_bass_kernel_spmd(nc, [{f"in_{k}": v for k, v in arrays.items()}], core_ids=[0])
    return r.results[0]["out"].reshape(a["x"].shape)
```

```python
from contextlib import ExitStack

import numpy as np

import concourse.bass as bass
from concourse import mybir

F32 = mybir.dt.float32
I32 = mybir.dt.int32
U8 = mybir.dt.uint8
ALU = mybir.AluOpType
ACT = mybir.ActivationFunctionType
AX = mybir.AxisListType

D = 128
TOKENS = 8192
NT = 4
GROUP = NT * D
GROUPS = TOKENS // GROUP
S = 64
LN_EPS = 1e-5
RMS_EPS = 1e-6


def rows(dram, start, tiles=NT):
    return dram[bass.ds(start, tiles * D), :].rearrange("(t p) f -> p t f", p=D)


def at_start(i):
    return isinstance(i, int) and i == 0


def turns(eng, count, turn, last_apart=False):
    turn(0)
    with eng.Fori(1, count - 1 if last_apart else count) as i:
        turn(i)
    if last_apart:
        turn(count - 1, last=True)


class Space:

    def __init__(self, nc, ctx, phase):
        self.nc, self.ctx, self.phase, self.sems = nc, ctx, phase, []
        ctx.callback(self.clear)

    def clear(self):
        self.nc.clear_and_free_semaphores(self.sems)
        self.nc.all_engine_barrier()

    def sb(self, name, shape, dt=F32):
        return self.ctx.enter_context(self.nc.sbuf_tensor(f"{self.phase}_{name}", shape, dt))

    def psum(self, name, shape):
        return self.ctx.enter_context(self.nc.psum_tensor(f"{self.phase}_{name}", shape, F32))

    def sem(self, name):
        self.sems.append(self.nc.alloc_semaphore(f"{self.phase}_{name}"))
        return self.sems[-1]


def slot_attention(nc, c, x_in, ctx_in, x_out):
    U = 2
    ROUNDS = 3
    SCALE = float(D) ** -0.5
    with ExitStack() as ctx:
        m = Space(nc, ctx, "slots")
        wk, wq, wv = (m.sb(n, [D, D]) for n in ("wk", "wq", "wv"))
        wihT, whhT = m.sb("wihT", [D, 3 * D]), m.sb("whhT", [D, 3 * D])
        bih, bhh = m.sb("bih", [D, 3]), m.sb("bhh", [D, 3])
        w_slot, w_in = m.sb("w_slot", [D, 1]), m.sb("w_in", [D, 1])
        ident, ones, pair_ones = m.sb("ident", [D, D]), m.sb("ones", [D, D]), m.sb("pair_ones", [D, D])
        minus_half = m.sb("minus_half", [D, 2 * NT])
        keyT = m.sb("keyT", [D, D])
        val3 = m.sb("val3", [D, 3 * D])
        k_scale = m.sb("k_scale", [D, 1])
        half_b = m.sb("half_b", [D, 3])
        x_raw, c_raw = m.sb("x_raw", [D, U, NT, D]), m.sb("c_raw", [D, U, NT, D])
        stats, mv, mean = m.sb("stats", [D, U, 2 * NT, 6]), m.sb("mv", [D, U, 3, 2 * NT]), m.sb("mean", [D, U, 2 * NT])
        halves, quarters, per_row, eps = (m.sb(n, [D, 2 * NT]) for n in ("halves", "quarters", "per_row", "eps"))
        power, rstd = m.sb("power", [D, U, 2 * NT]), m.sb("rstd", [D, U, 2 * NT])
        xn, cn = m.sb("xn", [D, U, NT, D]), m.sb("cn", [D, U, NT, D])
        h, cT, kT = (m.sb(n, [D, U, GROUP]) for n in ("h", "cT", "kT"))
        v3 = m.sb("v3", [D, U, NT, 3 * D])
        sq = m.sb("sq", [D, U, GROUP])
        ms, rs = m.sb("ms", [D, U, NT]), m.sb("rs", [D, U, NT])
        r_diag, r_row = m.sb("r_diag", [D, U, NT, S]), m.sb("r_row", [D, U, NT * S])
        pair_ident = m.sb("pair_ident", [D, S])
        mx, total = m.sb("mx", [D, U, NT]), m.sb("total", [D, U, NT])
        expo, attn, colr = (m.sb(n, [D, U, NT, S]) for n in ("expo", "attn", "colr"))
        attn_bd = m.sb("attn_bd", [D, U, NT, 2, S])
        tr, tz, hn, n_in, n = (m.sb(k, [D, U, GROUP]) for k in ("tr", "tz", "hn", "n_in", "n"))
        x_res, x_new = m.sb("x_res", [D, U, NT, D]), m.sb("x_new", [D, U, NT, D])
        bank = m.psum("bank", [D, U, 4, GROUP])

        weights_in = m.sem("weights_in")
        pool_consts, dve_consts = m.sem("pool_consts"), m.sem("dve_consts")
        prep_mm, prep_set = m.sem("prep_mm"), m.sem("prep_set")
        raw_in = [m.sem(f"raw_in{u}") for u in range(U)]
        res_in = [m.sem(f"res_in{u}") for u in range(U)]
        out_done = [m.sem(f"out_done{u}") for u in range(U)]
        names = (
            "stats_done sums_done quartered squared power_raw power_done rstd_done norm_done turned_x turned_c hT_done cT_done "
            "keys_mm kT_done v3_mm v3_done sq_done ssq_mm ms_done rs_done r_diag_done r_row_mm r_row_done scores_mm scaled max_done shifted "
            "exp_done total_done inv_done attn_done colsum_mm coleps_done colr_done attn_bd_done gates_mm "
            "r_done z_done hn_done tn1_done n_in_done n_done diff_done upd_done h_done hback_mm new_done"
        ).split()
        s = {k: m.sem(k) for k in names}
        block = ctx.enter_context(nc.Block())

        LOADS = 13

        @block.sync
        def _(sp):
            for dst, src in ((wk, c["L0_Wk"]), (wq, c["L0_Wq"]), (wv, c["L0_Wv"]), (wihT, c["L0_wihT"]),
                             (whhT, c["L0_whhT"]), (bih, c["L0_bih"]), (bhh, c["L0_bhh"]), (w_slot, c["L0_w_slot"]),
                             (w_in, c["L0_w_in"]), (ident, c["ident"]), (ones, c["ones"]), (pair_ones, c["pair_ones"]), (pair_ident, c["pair_ident"])):
                sp.dma_start(dst[:], src).then_inc(weights_in, 16)
            for u in range(U):
                sp.dma_start(x_raw[:, u], rows(x_in, u * GROUP)).then_inc(raw_in[u], 16)
                sp.dma_start(c_raw[:, u], rows(ctx_in, u * GROUP)).then_inc(raw_in[u], 16)

            def body(i, last=False):
                if not last:
                    for u in range(U):
                        sp.wait_ge(s["norm_done"], i * U + u + 1)
                        sp.dma_start(x_raw[:, u], rows(x_in, (i + 1) * U * GROUP + u * GROUP)).then_inc(raw_in[u], 16)
                        sp.dma_start(c_raw[:, u], rows(ctx_in, (i + 1) * U * GROUP + u * GROUP)).then_inc(raw_in[u], 16)
                for u in range(U):
                    if not at_start(i):
                        sp.wait_ge(s["new_done"], i * U)
                    sp.dma_start(x_res[:, u], rows(x_in, i * U * GROUP + u * GROUP)).then_inc(res_in[u], 16)
                for u in range(U):
                    sp.wait_ge(s["new_done"], i * U + u + 1)
                    sp.dma_start(rows(x_out, i * U * GROUP + u * GROUP), x_new[:, u]).then_inc(out_done[u], 16)

            turns(sp, GROUPS // U, body, True)
            for u in range(U):
                sp.wait_ge(out_done[u], 16 * (GROUPS // U))

        @block.gpsimd
        def _(pool):
            nc.gpsimd.memset(minus_half[:], -0.5).then_inc(pool_consts, 1)
            nc.gpsimd.memset(attn_bd[:], 0.0).then_inc(pool_consts, 1)
            for dst, value in ((halves[:], 0.5), (quarters[:], 0.25), (per_row[:], 1.0 / D), (eps[:, :NT], LN_EPS), (eps[:, NT:], RMS_EPS)):
                nc.gpsimd.memset(dst, value).then_inc(pool_consts, 1)
            pool.wait_ge(pool_consts, 7)

            def turn(i):
                for u in range(U):
                    k = i * U + u + 1
                    pool.wait_ge(s["stats_done"], k)
                    st = stats[:, u]
                    nc.gpsimd.tensor_tensor(mv[:, u, 0], st[:, :, 1], st[:, :, 4], ALU.add)
                    nc.gpsimd.tensor_tensor(mv[:, u, 1], st[:, :, 1], st[:, :, 4], ALU.subtract)
                    nc.gpsimd.tensor_tensor(mv[:, u, 2], st[:, :, 2], st[:, :, 5], ALU.add).then_inc(s["sums_done"], 1)
                    pool.wait_ge(s["sums_done"], k)
                    nc.gpsimd.tensor_tensor(mean[:, u], mv[:, u, 0], halves[:], ALU.mult)
                    nc.gpsimd.tensor_tensor(mv[:, u, 0], mv[:, u, 0], mv[:, u, 0], ALU.mult)
                    nc.gpsimd.tensor_tensor(mv[:, u, 1], mv[:, u, 1], mv[:, u, 1], ALU.mult)
                    nc.gpsimd.tensor_tensor(mv[:, u, 2], mv[:, u, 2], per_row[:], ALU.mult).then_inc(s["squared"], 1)
                    pool.wait_ge(s["squared"], k)
                    nc.gpsimd.tensor_tensor(mv[:, u, 1, NT:], mv[:, u, 1, NT:], mv[:, u, 0, NT:], ALU.add)
                    nc.gpsimd.tensor_tensor(mv[:, u, 2], mv[:, u, 2], eps[:], ALU.add).then_inc(s["power_raw"], 1)
                    pool.wait_ge(s["power_raw"], k)
                    nc.gpsimd.tensor_tensor(mv[:, u, 1], mv[:, u, 1], quarters[:], ALU.mult).then_inc(s["quartered"], 1)
                    pool.wait_ge(s["quartered"], k)
                    nc.gpsimd.tensor_tensor(power[:, u], mv[:, u, 1], mv[:, u, 2], ALU.add).then_inc(s["power_done"], 1)
                    pool.wait_ge(s["power_done"], k)
                    nc.gpsimd.tensor_tensor(rstd[:, u], power[:, u], minus_half[:], ALU.pow).then_inc(s["rstd_done"], 1)
                for r in range(ROUNDS):
                    for u in range(U):
                        k = (i * ROUNDS + r) * U + u + 1
                        pool.wait_ge(s["ms_done"], k)
                        nc.gpsimd.tensor_tensor(rs[:, u], ms[:, u], minus_half[:, :NT], ALU.pow).then_inc(s["rs_done"], 1)
                    for u in range(U):
                        k = (i * ROUNDS + r) * U + u + 1
                        pool.wait_ge(s["n_done"], k)
                        nc.gpsimd.tensor_tensor(sq[:, u], h[:, u], n[:, u], ALU.subtract).then_inc(s["diff_done"], 1)

            turns(pool, GROUPS // U, turn)

        @block.scalar
        def _(act):
            act.wait_ge(prep_mm, 1)
            act.wait_ge(weights_in, 16 * LOADS)
            nc.scalar.activation(keyT[:], bank[:, 0, 0, :D], ACT.Copy, scale=w_in[:]).then_inc(prep_set, 1)
            nc.scalar.activation(val3[:], bank[:, 0, 1, :3 * D], ACT.Copy, scale=w_in[:]).then_inc(prep_set, 1)
            act.wait_ge(dve_consts, 3)
            def turn(i):
                for u in range(U):
                    k = i * U + u + 1
                    act.wait_ge(s["turned_x"], k)
                    nc.scalar.activation(h[:, u], bank[:, u, 0], ACT.Copy).then_inc(s["hT_done"], 1)
                    act.wait_ge(s["turned_c"], k)
                    nc.scalar.activation(cT[:, u], bank[:, u, 1], ACT.Copy).then_inc(s["cT_done"], 1)
                for u in range(U):
                    k = i * U + u + 1
                    act.wait_ge(s["keys_mm"], k)
                    nc.scalar.activation(kT[:, u], bank[:, u, 2], ACT.Copy, scale=k_scale[:]).then_inc(s["kT_done"], 1)
                for u in range(U):
                    for t, b in enumerate((3, 0, 1, 2)):
                        act.wait_ge(s["v3_mm"], (i * U + u) * NT + t + 1)
                        nc.scalar.activation(v3[:, u, t], bank[:, u, b, :3 * D], ACT.Copy).then_inc(s["v3_done"], 1)
                for r in range(ROUNDS):
                    for u in range(U):
                        k = (i * ROUNDS + r) * U + u + 1
                        if r == 0:
                            act.wait_ge(s["hT_done"], i * U + u + 1)
                        else:
                            act.wait_ge(s["h_done"], k - U)
                        nc.scalar.activation(sq[:, u], h[:, u], ACT.Square).then_inc(s["sq_done"], 1)
                    for u in range(U):
                        k = (i * ROUNDS + r) * U + u + 1
                        act.wait_ge(s["r_row_mm"], k)
                        nc.scalar.activation(r_row[:, u], bank[:, u, 0, :NT * S], ACT.Copy).then_inc(s["r_row_done"], 1)
                    for u in range(U):
                        k = (i * ROUNDS + r) * U + u + 1
                        act.wait_ge(s["shifted"], k)
                        nc.scalar.activation(expo[:, u], expo[:, u], ACT.Exp).then_inc(s["exp_done"], 1)
                    for u in range(U):
                        k = (i * ROUNDS + r) * U + u + 1
                        act.wait_ge(s["gates_mm"], k)
                        nc.scalar.activation(hn[:, u], bank[:, u, 3], ACT.Identity, scale=0.5, bias=half_b[:, 2:3]).then_inc(s["hn_done"], 1)
                        nc.scalar.activation(tr[:, u], bank[:, u, 0], ACT.Tanh, scale=0.5, bias=half_b[:, 0:1]).then_inc(s["r_done"], 1)
                        nc.scalar.activation(tz[:, u], bank[:, u, 1], ACT.Tanh, scale=0.5, bias=half_b[:, 1:2]).then_inc(s["z_done"], 1)
                    for u in range(U):
                        k = (i * ROUNDS + r) * U + u + 1
                        act.wait_ge(s["n_in_done"], k)
                        nc.scalar.activation(n[:, u], n_in[:, u], ACT.Tanh, bias=bih[:, 2:3]).then_inc(s["n_done"], 1)

            turns(act, GROUPS // U, turn)

        @block.vector
        def _(dve):
            dve.wait_ge(weights_in, 16 * LOADS)
            nc.vector.tensor_scalar(k_scale[:], w_slot[:], SCALE, None, ALU.mult).then_inc(dve_consts, 1)
            nc.vector.tensor_tensor(half_b[:, 0:2], bih[:, 0:2], bhh[:, 0:2], ALU.add).then_inc(dve_consts, 1)
            nc.vector.tensor_scalar(half_b[:, 2:3], bhh[:, 2:3], 0.5, None, ALU.mult)
            dve.wait_ge(dve_consts, 2)
            nc.vector.tensor_scalar(half_b[:, 0:2], half_b[:, 0:2], 0.5, None, ALU.mult).then_inc(dve_consts, 1)
            def turn(i):
                for u in range(U):
                    k = i * U + u + 1
                    dve.wait_ge(raw_in[u], 32 * (i + 1))
                    for t in range(NT):
                        nc.vector.bn_stats(stats[:, u, t], x_raw[:, u, t])
                        last = nc.vector.bn_stats(stats[:, u, NT + t], c_raw[:, u, t])
                    last.then_inc(s["stats_done"], 1)
                for u in range(U):
                    k = i * U + u + 1
                    dve.wait_ge(s["rstd_done"], k)
                    for t in range(NT):
                        nc.vector.tensor_scalar(xn[:, u, t], x_raw[:, u, t], mean[:, u, t:t + 1], rstd[:, u, t:t + 1], ALU.subtract, ALU.mult)
                        last = nc.vector.tensor_scalar(cn[:, u, t], c_raw[:, u, t], rstd[:, u, NT + t:NT + t + 1], None, ALU.mult)
                    last.then_inc(s["norm_done"], 1)
                for r in range(ROUNDS):
                    count = lambda u: (i * ROUNDS + r) * U + u + 1
                    for u in range(U):
                        dve.wait_ge(s["ssq_mm"], count(u))
                        nc.vector.tensor_scalar(ms[:, u], bank[:, u, 0, :NT], 1.0 / D, RMS_EPS, ALU.mult, ALU.add).then_inc(s["ms_done"], 1)
                    for u in range(U):
                        dve.wait_ge(s["rs_done"], count(u))
                        nc.vector.tensor_tensor(r_diag[:, u], pair_ident[:].unsqueeze(1).broadcast_to([D, NT, S]),
                                                rs[:, u].unsqueeze(2).broadcast_to([D, NT, S]), ALU.mult).then_inc(s["r_diag_done"], 1)
                    for u in range(U):
                        dve.wait_ge(s["scores_mm"], count(u))
                        dve.wait_ge(s["r_row_done"], count(u))
                        for b in range(2):
                            p = slice(S * b, S * b + S)
                            own = bank[p, u, 1].rearrange("p (t b q) -> p t b q", t=NT, b=2)[:, :, b]
                            last = nc.vector.tensor_tensor(expo[p, u], own, r_row[p, u].rearrange("p (t q) -> p t q", t=NT), ALU.mult)
                        last.then_inc(s["scaled"], 1)
                        dve.wait_ge(s["scaled"], count(u))
                        nc.vector.tensor_reduce(mx[:, u], expo[:, u], AX.X, ALU.max).then_inc(s["max_done"], 1)
                        dve.wait_ge(s["max_done"], count(u))
                        nc.vector.tensor_tensor(expo[:, u], expo[:, u], mx[:, u].unsqueeze(2).broadcast_to([D, NT, S]),
                                                ALU.subtract).then_inc(s["shifted"], 1)
                    for u in range(U):
                        dve.wait_ge(s["exp_done"], count(u))
                        nc.vector.tensor_reduce(total[:, u], expo[:, u], AX.X, ALU.add).then_inc(s["total_done"], 1)
                        dve.wait_ge(s["total_done"], count(u))
                        nc.vector.reciprocal(total[:, u], total[:, u]).then_inc(s["inv_done"], 1)
                        dve.wait_ge(s["inv_done"], count(u))
                        nc.vector.tensor_tensor(attn[:, u], expo[:, u], total[:, u].unsqueeze(2).broadcast_to([D, NT, S]),
                                                ALU.mult).then_inc(s["attn_done"], 1)
                    for u in range(U):
                        dve.wait_ge(s["colsum_mm"], count(u))
                        nc.vector.tensor_scalar(colr[:, u], bank[:, u, 2, :NT * S], RMS_EPS, None, ALU.add).then_inc(s["coleps_done"], 1)
                        dve.wait_ge(s["coleps_done"], count(u))
                        nc.vector.reciprocal(colr[:, u], colr[:, u]).then_inc(s["colr_done"], 1)
                        dve.wait_ge(s["colr_done"], count(u))
                        for b in range(2):
                            p = slice(S * b, S * b + S)
                            last = nc.vector.tensor_tensor(attn_bd[p, u, :, b], attn[p, u], colr[p, u], ALU.mult)
                        last.then_inc(s["attn_bd_done"], 1)
                    for u in range(U):
                        dve.wait_ge(s["r_done"], count(u))
                        nc.vector.scalar_tensor_tensor(n_in[:, u], tr[:, u], 1.0, hn[:, u], ALU.add, ALU.mult).then_inc(s["tn1_done"], 1)
                        dve.wait_ge(s["tn1_done"], count(u))
                        nc.vector.tensor_tensor(n_in[:, u], n_in[:, u], bank[:, u, 2], ALU.add).then_inc(s["n_in_done"], 1)
                    for u in range(U):
                        dve.wait_ge(s["diff_done"], count(u))
                        dve.wait_ge(s["z_done"], count(u))
                        nc.vector.scalar_tensor_tensor(sq[:, u], tz[:, u], 1.0, sq[:, u], ALU.add, ALU.mult).then_inc(s["upd_done"], 1)
                        dve.wait_ge(s["upd_done"], count(u))
                        nc.vector.scalar_tensor_tensor(h[:, u], sq[:, u], 0.5, n[:, u], ALU.mult, ALU.add).then_inc(s["h_done"], 1)
                for u in range(U):
                    k = i * U + u + 1
                    dve.wait_ge(s["hback_mm"], k)
                    dve.wait_ge(res_in[u], 16 * (i + 1))
                    if not at_start(i):
                        dve.wait_ge(out_done[u], 16 * i)
                    nc.vector.tensor_tensor(x_new[:, u], bank[:, u, 0], x_res[:, u].rearrange("p t f -> p (t f)"), ALU.add).then_inc(s["new_done"], 1)

            turns(dve, GROUPS // U, turn)

        @block.tensor
        def _(pe):
            pe.wait_ge(weights_in, 16 * LOADS)
            nc.tensor.matmul(bank[:, 0, 0, :D], wk[:], wq[:], start=True, stop=True)
            nc.tensor.matmul(bank[:, 0, 1, :3 * D], wv[:], wihT[:], start=True, stop=True).then_inc(prep_mm, 1)
            pe.wait_ge(prep_set, 2)
            pe.wait_ge(pool_consts, 7)
            def turn(i):
                for u in range(U):
                    k = i * U + u + 1
                    pe.wait_ge(s["norm_done"], k)
                    if not at_start(i):
                        pe.wait_ge(s["new_done"], i * U)
                    for t in range(NT):
                        last = nc.tensor.transpose(bank[:, u, 0, t * D:(t + 1) * D], xn[:, u, t], ident[:])
                    last.then_inc(s["turned_x"], 1)
                    for t in range(NT):
                        last = nc.tensor.transpose(bank[:, u, 1, t * D:(t + 1) * D], cn[:, u, t], ident[:])
                    last.then_inc(s["turned_c"], 1)
                for u in range(U):
                    k = i * U + u + 1
                    pe.wait_ge(s["cT_done"], k)
                    nc.tensor.matmul(bank[:, u, 2], keyT[:], cT[:, u], start=True, stop=True).then_inc(s["keys_mm"], 1)
                for u in range(U):
                    k = i * U + u + 1
                    for t, b in enumerate((3, 0, 1, 2)):
                        if b == 2:
                            pe.wait_ge(s["kT_done"], k)
                        nc.tensor.matmul(bank[:, u, b, :3 * D], cT[:, u, t * D:(t + 1) * D], val3[:], start=True, stop=True).then_inc(s["v3_mm"], 1)
                for r in range(ROUNDS):
                    count = lambda u: (i * ROUNDS + r) * U + u + 1
                    for u in range(U):
                        pe.wait_ge(s["sq_done"], count(u))
                        if r == 0:
                            pe.wait_ge(s["v3_done"], (i * U + u) * NT + NT)
                        for t in range(NT):
                            last = nc.tensor.matmul(bank[:, u, 0, t:t + 1], sq[:, u, t * D:(t + 1) * D], ones[:, :1], start=True, stop=True)
                        last.then_inc(s["ssq_mm"], 1)
                        for t in range(NT):
                            c_ = slice(t * D, (t + 1) * D)
                            last = nc.tensor.matmul(bank[:, u, 1, c_], kT[:, u, c_], h[:, u, c_], start=True, stop=True)
                        last.then_inc(s["scores_mm"], 1)
                    for u in range(U):
                        nc.tensor.matmul(bank[:, u, 3], whhT[:, 2 * D:], h[:, u], start=True, stop=True)
                        pe.wait_ge(s["r_diag_done"], count(u))
                        nc.tensor.matmul(bank[:, u, 0, :NT * S], pair_ones[:], r_diag[:, u], start=True, stop=True).then_inc(s["r_row_mm"], 1)
                    for u in range(U):
                        pe.wait_ge(s["r_row_done"], count(u))
                        nc.tensor.matmul(bank[:, u, 0], whhT[:, :D], h[:, u], start=True, stop=False)
                        pe.wait_ge(s["attn_done"], count(u))
                        nc.tensor.matmul(bank[:, u, 2, :NT * S], pair_ones[:], attn[:, u], start=True, stop=True).then_inc(s["colsum_mm"], 1)
                    for u in range(U):
                        nc.tensor.matmul(bank[:, u, 1], whhT[:, D:2 * D], h[:, u], start=True, stop=False)
                        pe.wait_ge(s["attn_bd_done"], count(u))
                        for g, b in enumerate((0, 1, 2)):
                            for t in range(NT):
                                last = nc.tensor.matmul(bank[:, u, b, t * D:(t + 1) * D], v3[:, u, t, g * D:(g + 1) * D], attn_bd[:, u, t],
                                                        start=(b == 2), stop=(b == 2 or t == NT - 1))
                        last.then_inc(s["gates_mm"], 1)
                for u in range(U):
                    pe.wait_ge(s["h_done"], (i * ROUNDS + ROUNDS - 1) * U + u + 1)
                    for t in range(NT):
                        last = nc.tensor.transpose(bank[:, u, 0, t * D:(t + 1) * D], h[:, u, t * D:(t + 1) * D], ident[:])
                    last.then_inc(s["hback_mm"], 1)

            turns(pe, GROUPS // U, turn)


E = 8
R_TILES = 16
R_STEPS = TOKENS // (R_TILES * D)
SLOT_TILES = 2
SLOT = SLOT_TILES * D
SLOTS = TOKENS // SLOT + E
XE_ROWS = SLOTS * SLOT


def moments(nc, dve, raw, tiles, stats, parts, mean, power, s, k):
    for t in range(tiles):
        last = nc.vector.bn_stats(stats[:, t], raw[:, t])
    last.then_inc(s["stats_done"], 1)
    dve.wait_ge(s["stats_done"], k)
    nc.vector.tensor_tensor(parts[:, 0], stats[:, :, 1], stats[:, :, 4], ALU.add)
    nc.vector.tensor_tensor(parts[:, 1], stats[:, :, 1], stats[:, :, 4], ALU.subtract)
    nc.vector.tensor_tensor(parts[:, 2], stats[:, :, 2], stats[:, :, 5], ALU.add).then_inc(s["parts_done"], 1)
    dve.wait_ge(s["parts_done"], k)
    nc.vector.tensor_scalar(mean, parts[:, 0], 0.5, None, ALU.mult)
    nc.vector.tensor_tensor(parts[:, 1], parts[:, 1], parts[:, 1], ALU.mult)
    nc.vector.tensor_scalar(parts[:, 2], parts[:, 2], 1.0 / D, LN_EPS, ALU.mult, ALU.add).then_inc(s["mean_done"], 1)
    dve.wait_ge(s["mean_done"], k)
    nc.vector.scalar_tensor_tensor(power, parts[:, 1], 0.25, parts[:, 2], ALU.mult, ALU.add).then_inc(s["power_done"], 1)


def route(nc, c, ph, x_in, gate, xe, pos_out, prob_out, table_out, weighted, clear):
    with ExitStack() as ctx:
        m = Space(nc, ctx, ph)
        T, N = R_TILES, TOKENS // D
        ident, ones, before = m.sb("ident", [D, D]), m.sb("ones", [D, D]), m.sb("before", [D, D])
        gw, gb = m.sb("gw", [D, E]), m.sb("gb", [D, E])
        minus_half = m.sb("minus_half", [D, T])
        falling, restart = m.sb("falling", [D, E]), m.sb("restart", [D, E, T])
        zeros = m.sb("zeros", [D, NT, D])
        raw, xn, xnT = m.sb("raw", [D, 2, T, D]), m.sb("xn", [D, N, D]), m.sb("xnT", [D, 2, T * D])
        stats, parts = m.sb("stats", [D, 2, T, 6]), m.sb("parts", [D, 2, 3, T])
        mean, power, rstd = (m.sb(n, [D, N]) for n in ("mean", "power", "rstd"))
        logit, hot, eq, expo, rank = (m.sb(n, [D, N, E]) for n in ("logit", "hot", "eq", "expo", "rank"))
        top, pick, prob, esum, posf, basef = (m.sb(n, [D, N]) for n in ("top", "pick", "prob", "esum", "posf", "basef"))
        tot, incl, base = (m.sb(n, [D, R_STEPS, E, T]) for n in ("tot", "incl", "base"))
        carry = m.sb("carry", [D, R_STEPS + 1, E])
        pos = m.sb("pos", [D, N], I32)
        steps, slot_no = m.sb("steps", [D, TOKENS // SLOT]), m.sb("slot_no", [D, SLOTS])
        over, need = m.sb("over", [D, E, TOKENS // SLOT]), m.sb("need", [D, E])
        cum, first = m.sb("cum", [D, E]), m.sb("first", [D, E])
        past, tabf, tab = m.sb("past", [D, SLOTS, E]), m.sb("tabf", [D, SLOTS]), m.sb("tab", [D, SLOTS], I32)
        pT = m.psum("pT", [D, 4, 4 * D])
        pL, pR, pS, pW = (m.psum(n, [D, 512]) for n in ("pL", "pR", "pS", "pW"))

        weights_in, pool_consts, gate_done = m.sem("weights_in"), m.sem("pool_consts"), m.sem("gate_done")
        gates, cleared, scattered, saved = m.sem("gate_steps"), m.sem("cleared"), m.sem("scattered"), m.sem("saved")
        raw_in = [m.sem(f"raw_in{u}") for u in range(2)]
        s = {k: m.sem(k) for k in (
            "stats_done parts_done mean_done power_done rstd_done norm_done turned xnT_done logits_mm logit_done top_done "
            "eq_done eqw_done pick_done hot_done shifted exp_done esum_done prob_done ranks_mm tot_done incl_done base0_done "
            "base_done rank_done carry_done table_step pos_done").split()}
        LOADS = 8
        if gate == "cosine":
            w_redT, wg, wgT = m.sb("w_redT", [16, D]), m.sb("wg", [E, 16]), m.sb("wgT", [16, E])
            wsq, wnorm, half8 = m.sb("wsq", [E, 16]), m.sb("wnorm", [E, 1]), m.sb("half8", [E, 1])
            LOADS = 9
        block = ctx.enter_context(nc.Block())

        @block.sync
        def _(sp):
            for i in range(2):
                sp.dma_start(raw[:, i], rows(x_in, i * T * D, T)).then_inc(raw_in[i], 16)
            own = ((w_redT, c["L0_w_redT"]), (wg, c["L0_wg"])) if gate == "cosine" else ((gw, gate[0]),)
            for dst, src in own + ((ident, c["ident"]), (ones, c["ones"]), (before, c["before"]), (falling, c["falling"]),
                                   (steps, c["steps"]), (slot_no, c["slot_no"])):
                sp.dma_start(dst[:], src).then_inc(weights_in, 16)
            bias = c["zero_row"][0:1, :E] if gate == "cosine" else gate[1]
            sp.dma_start(gb[:], bias.broadcast_to([D, E])).then_inc(weights_in, 16)
            for i in range(2, R_STEPS):
                sp.wait_ge(s["norm_done"], i - 1)
                sp.dma_start(raw[:, i % 2], rows(x_in, i * T * D, T)).then_inc(raw_in[i % 2], 16)
            if clear:
                sp.wait_ge(pool_consts, 3)
                for r in range(0, XE_ROWS, GROUP):
                    sp.dma_start(rows(xe, r), zeros[:]).then_inc(cleared, 16)
            sp.wait_ge(s["table_step"], 9)
            sp.dma_start(table_out, tab[0:1]).then_inc(saved, 16)
            sp.wait_ge(s["pos_done"], 1)
            sp.dma_start(pos_out, pos[:]).then_inc(saved, 16)
            if weighted:
                sp.wait_ge(s["prob_done"], R_STEPS)
                sp.dma_start(prob_out, prob[:]).then_inc(saved, 16)
            sp.wait_ge(saved, 48 if weighted else 32)

        @block.gpsimd
        def _(pool):
            nc.gpsimd.memset(minus_half[:], -0.5).then_inc(pool_consts, 1)
            nc.gpsimd.memset(zeros[:], 0.0).then_inc(pool_consts, 1)
            nc.gpsimd.memset(restart[:], 1.0).then_inc(pool_consts, 1)
            pool.wait_ge(pool_consts, 3)
            nc.gpsimd.memset(restart[:, :, 0:1], 0.0).then_inc(pool_consts, 1)
            if gate == "cosine":
                nc.gpsimd.memset(half8[:], 0.5).then_inc(pool_consts, 1)
                pool.wait_ge(pool_consts, 5)
                pool.wait_ge(gates, 1)
                nc.gpsimd.tensor_tensor(wnorm[:], wnorm[:], half8[:], ALU.pow).then_inc(gates, 1)
            for i in range(R_STEPS):
                own = slice(i * T, (i + 1) * T)
                pool.wait_ge(s["power_done"], i + 1)
                nc.gpsimd.tensor_tensor(rstd[:, own], power[:, own], minus_half[:], ALU.pow).then_inc(s["rstd_done"], 1)
            pool.wait_ge(s["norm_done"], R_STEPS)
            pool.wait_ge(s["pos_done"], 1)
            if clear:
                pool.wait_ge(cleared, 16 * (XE_ROWS // GROUP))
            for t in range(N):
                pool.indirect_dma_start(out=xe, out_offset=bass.IndirectOffsetOnAxis(ap=pos[:, t:t + 1], axis=0),
                                        in_=xn[:, t], in_offset=None).then_inc(scattered, 16)
            pool.wait_ge(scattered, 16 * N)

        @block.scalar
        def _(act):
            if gate == "cosine":
                act.wait_ge(weights_in, 16 * LOADS)
                nc.scalar.activation(wsq[:], wg[:], ACT.Square, accum_out=wnorm[:]).then_inc(gates, 1)
            for i in range(R_STEPS):
                for g in range(T // 4):
                    act.wait_ge(s["turned"], i * (T // 4) + g + 1)
                    nc.scalar.activation(xnT[:, i % 2, g * 4 * D:(g + 1) * 4 * D], pT[:, g], ACT.Copy).then_inc(s["xnT_done"], 1)
                if weighted:
                    own = slice(i * T, (i + 1) * T)
                    act.wait_ge(s["shifted"], i + 1)
                    nc.scalar.activation(expo[:, own], expo[:, own], ACT.Exp).then_inc(s["exp_done"], 1)

        @block.vector
        def _(dve):
            dve.wait_ge(weights_in, 16 * LOADS)
            if gate == "cosine":
                dve.wait_ge(gates, 2)
                nc.vector.tensor_scalar(wnorm[:], wnorm[:], 1e-4, None, ALU.max).then_inc(gates, 1)
                dve.wait_ge(gates, 3)
                nc.vector.reciprocal(wnorm[:], wnorm[:]).then_inc(gates, 1)
                dve.wait_ge(gates, 4)
                nc.vector.tensor_scalar(wg[:], wg[:], wnorm[:], None, ALU.mult).then_inc(gates, 1)
                dve.wait_ge(gates, 6)
                nc.vector.tensor_copy(wgT[:], pW[:16, :E]).then_inc(gates, 1)
                dve.wait_ge(gates, 8)
                nc.vector.tensor_copy(gw[:], pW[:, 16:16 + E]).then_inc(gate_done, 1)
            nc.vector.memset(carry[:, 0], 0.0).then_inc(s["carry_done"], 1)
            dve.wait_ge(pool_consts, 4)

            def normalise(i):
                own = slice(i * T, (i + 1) * T)
                dve.wait_ge(raw_in[i % 2], 16 * (i // 2 + 1))
                moments(nc, dve, raw[:, i % 2], T, stats[:, i % 2], parts[:, i % 2], mean[:, own], power[:, own], s, i + 1)
                dve.wait_ge(s["rstd_done"], i + 1)
                for t in range(T):
                    a = i * T + t
                    last = nc.vector.tensor_scalar(xn[:, a], raw[:, i % 2, t], mean[:, a:a + 1], rstd[:, a:a + 1], ALU.subtract, ALU.mult)
                last.then_inc(s["norm_done"], 1)

            def choose(i):
                own = slice(i * T, (i + 1) * T)
                per_tile = lambda a: a.unsqueeze(2).broadcast_to([D, T, E])
                per_expert = lambda a: a.unsqueeze(1).broadcast_to([D, T, E])
                k = i + 1
                dve.wait_ge(s["logits_mm"], k)
                nc.vector.tensor_tensor(logit[:, own], pL[:, :T * E].rearrange("p (t e) -> p t e", t=T), per_expert(gb[:]), ALU.add).then_inc(s["logit_done"], 1)
                dve.wait_ge(s["logit_done"], k)
                nc.vector.tensor_reduce(top[:, own], logit[:, own], AX.X, ALU.max).then_inc(s["top_done"], 1)
                dve.wait_ge(s["top_done"], k)
                nc.vector.tensor_tensor(eq[:, own], logit[:, own], per_tile(top[:, own]), ALU.is_equal).then_inc(s["eq_done"], 1)
                if weighted:
                    nc.vector.tensor_tensor(expo[:, own], logit[:, own], per_tile(top[:, own]), ALU.subtract).then_inc(s["shifted"], 1)
                dve.wait_ge(s["eq_done"], k)
                nc.vector.tensor_tensor(eq[:, own], eq[:, own], per_expert(falling[:]), ALU.mult).then_inc(s["eqw_done"], 1)
                dve.wait_ge(s["eqw_done"], k)
                nc.vector.tensor_reduce(pick[:, own], eq[:, own], AX.X, ALU.max).then_inc(s["pick_done"], 1)
                dve.wait_ge(s["pick_done"], k)
                nc.vector.tensor_tensor(hot[:, own], eq[:, own], per_tile(pick[:, own]), ALU.is_equal).then_inc(s["hot_done"], 1)
                dve.wait_ge(s["ranks_mm"], k)
                nc.vector.tensor_copy(tot[:, i], pS[:, :T * E].rearrange("p (t e) -> p e t", t=T)).then_inc(s["tot_done"], 1)
                dve.wait_ge(s["tot_done"], k)
                flat = lambda a: a.rearrange("p e t -> p (e t)")
                nc.vector.tensor_tensor_scan(flat(incl[:, i]), flat(restart[:]), flat(tot[:, i]), 0.0, ALU.mult, ALU.add).then_inc(s["incl_done"], 1)
                dve.wait_ge(s["incl_done"], k)
                nc.vector.tensor_tensor(base[:, i], incl[:, i], tot[:, i], ALU.subtract).then_inc(s["base0_done"], 1)
                dve.wait_ge(s["carry_done"], k)
                nc.vector.tensor_tensor(carry[:, i + 1], carry[:, i], incl[:, i, :, T - 1], ALU.add).then_inc(s["carry_done"], 1)
                dve.wait_ge(s["base0_done"], k)
                nc.vector.tensor_tensor(base[:, i], base[:, i], carry[:, i].unsqueeze(2).broadcast_to([D, E, T]), ALU.add).then_inc(s["base_done"], 1)
                dve.wait_ge(s["base_done"], k)
                nc.vector.tensor_tensor(rank[:, own], pR[:, :T * E].rearrange("p (t e) -> p t e", t=T),
                                        base[:, i].rearrange("p e t -> p t e"), ALU.add).then_inc(s["rank_done"], 1)
                if weighted:
                    dve.wait_ge(s["exp_done"], k)
                    nc.vector.tensor_reduce(esum[:, own], expo[:, own], AX.X, ALU.add).then_inc(s["esum_done"], 1)
                    dve.wait_ge(s["esum_done"], k)
                    nc.vector.reciprocal(prob[:, own], esum[:, own]).then_inc(s["prob_done"], 1)

            for i in range(R_STEPS + 1):
                if i < R_STEPS:
                    normalise(i)
                if i:
                    choose(i - 1)
            NS = TOKENS // SLOT
            steps_done = [0]

            def step(ins):
                steps_done[0] += 1
                ins.then_inc(s["table_step"], 1)
                dve.wait_ge(s["table_step"], steps_done[0])

            dve.wait_ge(s["carry_done"], R_STEPS + 1)
            step(nc.vector.tensor_tensor(over[:], carry[:, R_STEPS].unsqueeze(2).broadcast_to([D, E, NS]), steps[:].unsqueeze(1).broadcast_to([D, E, NS]), ALU.is_gt))
            step(nc.vector.tensor_reduce(need[:], over[:], AX.X, ALU.add))
            step(nc.vector.tensor_tensor_scan(cum[:], ones[:, :E], need[:], 0.0, ALU.mult, ALU.add))
            step(nc.vector.tensor_tensor(past[:], slot_no[:].unsqueeze(2).broadcast_to([D, SLOTS, E]), cum[:].unsqueeze(1).broadcast_to([D, SLOTS, E]), ALU.is_ge))
            step(nc.vector.tensor_tensor(first[:], cum[:], need[:], ALU.subtract))
            step(nc.vector.tensor_scalar(first[:], first[:], float(SLOT), None, ALU.mult))
            step(nc.vector.tensor_reduce(tabf[:], past[:], AX.X, ALU.add))
            step(nc.vector.tensor_scalar(tabf[:], tabf[:], float(E - 1), None, ALU.min))
            step(nc.vector.tensor_copy(tab[:], tabf[:]))
            step(nc.vector.tensor_tensor(rank[:], rank[:], first[:].unsqueeze(1).broadcast_to([D, N, E]), ALU.add))
            step(nc.vector.tensor_tensor(rank[:], rank[:], hot[:], ALU.mult))
            step(nc.vector.tensor_reduce(posf[:], rank[:], AX.X, ALU.add))
            nc.vector.tensor_copy(pos[:], posf[:]).then_inc(s["pos_done"], 1)

        @block.tensor
        def _(pe):
            pe.wait_ge(weights_in, 16 * LOADS)
            if gate == "cosine":
                pe.wait_ge(gates, 5)
                nc.tensor.transpose(pW[:16, :E], wg[:], ident[:E, :E]).then_inc(gates, 1)
                pe.wait_ge(gates, 7)
                nc.tensor.matmul(pW[:, 16:16 + E], w_redT[:], wgT[:], start=True, stop=True).then_inc(gates, 1)
                pe.wait_ge(gate_done, 1)

            def logits(i):
                pe.wait_ge(s["norm_done"], i + 1)
                for g in range(T // 4):
                    if i:
                        pe.wait_ge(s["xnT_done"], (i - 1) * (T // 4) + g + 1)
                    for t in range(4):
                        last = nc.tensor.transpose(pT[:, g, t * D:(t + 1) * D], xn[:, i * T + g * 4 + t], ident[:])
                    last.then_inc(s["turned"], 1)
                if i:
                    pe.wait_ge(s["logit_done"], i)
                for g in range(T // 4):
                    pe.wait_ge(s["xnT_done"], i * (T // 4) + g + 1)
                    for t in range(4 * g, 4 * g + 4):
                        last = nc.tensor.matmul(pL[:, t * E:(t + 1) * E], xnT[:, i % 2, t * D:(t + 1) * D], gw[:], start=True, stop=True)
                last.then_inc(s["logits_mm"], 1)

            def ranks(i):
                pe.wait_ge(s["hot_done"], i + 1)
                if i:
                    pe.wait_ge(s["rank_done"], i)
                hot_all = hot[:, i * T:(i + 1) * T].rearrange("p t e -> p (t e)")
                nc.tensor.matmul(pR[:, :T * E], before[:], hot_all, start=True, stop=True)
                nc.tensor.matmul(pS[:, :T * E], ones[:], hot_all, start=True, stop=True).then_inc(s["ranks_mm"], 1)

            for i in range(R_STEPS):
                logits(i)
                ranks(i)


def experts(nc, c, ph, xe, table_in, w, ye, gelu):
    RING = 4
    U = 2
    F = 4
    TURNS = SLOTS // RING
    with ExitStack() as ctx:
        m = Space(nc, ctx, ph)
        ident, tab = m.sb("ident", [D, D]), m.sb("tab", [1, SLOTS], I32)
        w1, w2 = m.sb("w1", [D, RING, F * D]), m.sb("w2", [D, RING, F * D])
        b1, b2 = m.sb("b1", [D, RING, F]), m.sb("b2", [D, RING, D])
        x, xT = m.sb("x", [D, RING, SLOT_TILES, D]), m.sb("xT", [D, U, SLOT])
        h, y = m.sb("h", [D, U, F, SLOT]), m.sb("y", [D, RING, SLOT_TILES, D])
        pX, pH, pY = m.psum("pX", [D, U, 512]), m.psum("pH", [D, U, F, SLOT]), m.psum("pY", [D, U, 512])
        setup_in, tab_in, store_turn = m.sem("setup_in"), m.sem("tab_in"), m.sem("store_turn")
        x_loaded, w1_in, w2_in, saved = ([m.sem(f"{n}{r}") for r in range(RING)] for n in ("x_loaded", "w1_in", "w2_in", "saved"))
        s = {k: m.sem(k) for k in "turned xT_done hidden_mm act_done y_mm y_done".split()}
        block = ctx.enter_context(nc.Block())

        @block.sync
        def _(sp):
            sp.dma_start(tab[:], table_in).then_inc(tab_in, 16)
            sp.dma_start(ident[:], c["ident"]).then_inc(setup_in, 16)
            sp.wait_ge(tab_in, 16)

            def turn(i):
                for r in range(RING):
                    k = i * RING + r
                    e = sp.value_load(tab[0:1, bass.ds(k, 1)], min_val=0, max_val=E - 1)
                    if not at_start(i):
                        sp.wait_ge(s["y_done"], k - RING + 1)
                    sp.dma_start(x[:, r], rows(xe, k * SLOT, SLOT_TILES)).then_inc(x_loaded[r], 16)
                    sp.dma_start(w1[:, r], w[0][bass.ds(e * D, D), :]).then_inc(w1_in[r], 16)
                    sp.dma_start(b1[:, r], w[1][bass.ds(e * D, D), :]).then_inc(w1_in[r], 16)
                    sp.dma_start(w2[:, r], w[2][bass.ds(e * D, D), :]).then_inc(w2_in[r], 16)
                    sp.dma_start(b2[:, r], w[3][bass.ds(e, 1), :].broadcast_to([D, D])).then_inc(w2_in[r], 16)

            turns(sp, TURNS, turn)

        @block.gpsimd
        def _(pool):
            def turn(i):
                for r in range(RING):
                    pool.wait_ge(s["y_done"], i * RING + r + 1)
                    pool.sem_inc(store_turn, 1)
                    pool.dma_start(rows(ye, (i * RING + r) * SLOT, SLOT_TILES), y[:, r]).then_inc(saved[r], 16)

            turns(pool, TURNS, turn)
            for r in range(RING):
                pool.wait_ge(saved[r], 16 * TURNS)

        @block.scalar
        def _(act):
            def copy_turned(k, u):
                act.wait_ge(s["turned"], k + 1)
                nc.scalar.activation(xT[:, u], pX[:, u, :SLOT], ACT.Copy).then_inc(s["xT_done"], 1)

            def turn(i, last=False):
                for r in range(RING):
                    k, u = i * RING + r, r % 2
                    act.wait_ge(w1_in[r], 32 * (i + 1))
                    for f in range(F):
                        act.wait_ge(s["hidden_mm"], k * F + (f | 1) + 1)
                        if f == 0 and not (last and r == RING - 1):
                            copy_turned(k + 1, 1 - u)
                        if gelu:
                            nc.scalar.activation(h[:, u, f], pH[:, u, f], ACT.Gelu, bias=b1[:, r, f:f + 1]).then_inc(s["act_done"], 1)
                        else:
                            nc.scalar.activation(h[:, u, f], pH[:, u, f], ACT.Relu, bias=b1[:, r, f:f + 1]).then_inc(s["act_done"], 1)

            copy_turned(0, 0)
            turns(act, TURNS, turn, True)

        @block.vector
        def _(dve):
            def turn(i):
                for r in range(RING):
                    k = i * RING + r
                    dve.wait_ge(s["y_mm"], k + 1)
                    if not at_start(i):
                        dve.wait_ge(saved[r], 16 * i)
                    nc.vector.tensor_tensor(y[:, r], pY[:, r % 2, :SLOT].rearrange("p (t f) -> p t f", t=SLOT_TILES),
                                            b2[:, r].unsqueeze(1).broadcast_to([D, SLOT_TILES, D]), ALU.add).then_inc(s["y_done"], 1)

            turns(dve, TURNS, turn)

        @block.tensor
        def _(pe):
            pe.wait_ge(setup_in, 16)

            def turn_rows(i, r):
                k = i * RING + r
                pe.wait_ge(x_loaded[r], 16 * (i + 1))
                if not (at_start(i) and r < 2):
                    pe.wait_ge(s["xT_done"], k - 1)
                for t in range(SLOT_TILES):
                    last = nc.tensor.transpose(pX[:, r % 2, t * D:(t + 1) * D], x[:, r, t], ident[:])
                last.then_inc(s["turned"], 1)

            def hidden(i, r):
                k, u = i * RING + r, r % 2
                pe.wait_ge(w1_in[r], 32 * (i + 1))
                pe.wait_ge(s["xT_done"], k + 1)
                for f in range(F):
                    if not (at_start(i) and r < 2):
                        pe.wait_ge(s["act_done"], (k - 2) * F + (f | 1) + 1)
                    nc.tensor.matmul(pH[:, u, f], w1[:, r, f * D:(f + 1) * D], xT[:, u], start=True, stop=True).then_inc(s["hidden_mm"], 1)

            def second(i, r):
                k, u = i * RING + r, r % 2
                pe.wait_ge(w2_in[r], 32 * (i + 1))
                if not (at_start(i) and r < 2):
                    pe.wait_ge(s["y_done"], k - 1)
                for t in range(SLOT_TILES):
                    for f in range(F):
                        pe.wait_ge(s["act_done"], k * F + f + 1)
                        last = nc.tensor.matmul(pY[:, u, t * D:(t + 1) * D], h[:, u, f, t * D:(t + 1) * D], w2[:, r, f * D:(f + 1) * D],
                                                start=(f == 0), stop=(f == F - 1))
                last.then_inc(s["y_mm"], 1)

            def turn(i, last=False):
                for r in range(RING):
                    if r < RING - 1:
                        turn_rows(i, r + 1)
                    elif not last:
                        turn_rows(i + 1, 0)
                    hidden(i, r)
                    if r:
                        second(i, r - 1)
                    elif not at_start(i):
                        second(i - 1, RING - 1)

            turn_rows(0, 0)
            turns(pe, TURNS, turn, True)
            second(TURNS - 1, RING - 1)


H = 16
HD = D // H
B = GROUP // S


def attention(nc, c, ph, layer, x_in, ctx_in, w, x_out, combined):
    own_keys = layer == 3
    NS = 2 if own_keys else 1
    LEAD = 3 if layer == 2 else 2
    AHEAD = 1 if own_keys else 2
    RING = 2 * AHEAD
    SCALE = float(HD) ** -0.5
    rope = layer == 1
    project = layer != 3
    TURN = 3 if layer == 2 else 2
    ROPE = TURN + 3
    VALUES = 6 if rope else 5
    with ExitStack() as ctx:
        m = Space(nc, ctx, ph)
        ident, n_mask = m.sb("ident", [D, D]), m.sb("n_mask", [D, 8])
        wq, wk, wv = (m.sb(n, [D, D]) for n in ("wq", "wk", "wv"))
        minus_half = m.sb("minus_half", [D, NT])
        x_res, c_raw, xn = m.sb("x_res", [D, 2, NT, D]), m.sb("c_raw", [D, NT, D]), m.sb("xn", [D, NT, D])
        stats, parts = m.sb("stats", [D, NT, 6]), m.sb("parts", [D, 3, NT])
        mean, power, rstd = (m.sb(n, [D, NT]) for n in ("mean", "power", "rstd"))
        xT, cT = m.sb("xT", [D, GROUP]), m.sb("cT", [D, GROUP])
        twice = [m.sb(f"twice{n}", [D, B, 2, S]) for n in range(NS)]
        qg = m.sb("qg", [D, 2, B, 2, S])
        kT = m.sb("kT", [D, 2, NS, GROUP])
        kn = m.sb("kn", [D, 2, NS, 8, S])
        vx = m.sb("vx", [D, 2, NS, B, 8, 2, HD + 1])
        e = m.sb("e", [D, RING, NS, 8, S])
        mx, rden = m.sb("mx", [D, 2, 8]), m.sb("rden", [D, 2, H])
        pt = m.sb("pt", [D, 2, NS, 4, D])
        attn, x_new = m.sb("attn", [D, 2, NT, D]), m.sb("x_new", [D, NT, D])
        front = m.psum("front", [D, 2, GROUP])
        sc = m.psum("sc", [D, AHEAD, NS, 8 * S])
        turn = m.psum("turn", [D, NS, GROUP])
        pv = m.psum("pv", [D, 2, 512])

        loads = [(ident[:], c["ident"]), (n_mask[:], c["n_mask"]), (wq[:], w["q"]), (wk[:], w["k"]), (wv[:], w["v"])]
        if project:
            wo, aT = m.sb("wo", [D, D]), m.sb("aT", [D, GROUP])
            loads += [(wo[:], w["o"])]
        if not rope:
            bq, bk, bv = m.sb("bq", [D, 1]), m.sb("bk", [D, 1]), m.sb("bv", [D, D])
            loads += [(bq[:], w["bq"]), (bk[:], w["bk"]), (bv[:], w["bv"].broadcast_to([D, D]))]
        if layer == 2:
            bo, m8 = m.sb("bo", [D, D]), m.sb("m8", [D, S // 4], mybir.dt.uint32)
            keep, neg = m.sb("keep", [D, S]), m.sb("neg", [D, S])
            loads += [(bo[:], w["bo"].broadcast_to([D, D])), (m8[:S], w["mask"]), (m8[S:], w["mask"])]
        if rope:
            tab, wrow = m.sb("tab", [D, 4, HD]), m.sb("wrow", [D, 4, HD])
            qk, qs = m.sb("qk", [D, 2, NT * H, HD]), m.sb("qs", [D, 2, NT * H, HD])
            ssq, rr = m.sb("ssq", [D, 2, NT * H]), m.sb("rr", [D, 2, NT * H])
            loads += [(tab[:], c["rope"])]
            for k, v in enumerate(w["norm"]):
                loads += [(wrow[:, 2 * k], v.broadcast_to([D, HD]))]
                loads += [(wrow[:, 2 * k + 1, a:a + HD // 2], v[:, HD // 2 - a:HD - a].broadcast_to([D, HD // 2])) for a in (0, HD // 2)]
        if combined:
            pos, prob = m.sb("pos", [D, TOKENS // D], I32), m.sb("prob", [D, TOKENS // D])
            pos_now, y, x_raw = m.sb("pos_now", [D, NT], I32), m.sb("y", [D, NT, D]), m.sb("x_raw", [D, NT, D])
            loads += [(pos[:], combined[1]), (prob[:], combined[2])]
            pos_step, pos_turn, y_in, y_used = m.sem("pos_step"), m.sem("pos_turn"), m.sem("y_in"), m.sem("y_used")
        LOADS = 16 * len(loads)

        weights_in, pool_consts, dve_consts, dve_ready = (m.sem(n) for n in ("weights_in", "pool_consts", "dve_consts", "dve_ready"))
        x_loaded = [m.sem(f"x_loaded{p}") for p in range(2)]
        c_loaded, saved = m.sem("c_loaded"), m.sem("saved")
        s = {k: m.sem(k) for k in (
            "stats_done parts_done mean_done power_done rstd_done norm_done turned_x turned_c xT_done cT_done twice_done "
            "q_mm k_mm q_done k_done own_k_mm own_k_done v_mm v_done masked scores_mm kept negated max_done shifted exp_done "
            "turned_e pt_done pv_mm rden_done normed fin_turned aT_done fin_mm fin_added new_done "
            "q_sq k_sq ssq_done ssqeps_done sqrt_done rr_done qk_scaled swapped cosed roped turned_q turned_k").split()}
        block = ctx.enter_context(nc.Block())
        LAST = GROUPS - 1
        V_STEPS = [(src, half) for half in range(2) for src in range(NS)]

        def at(j, p, b):
            return (j, p, b) if b < B else (j + 1, 1 - p, b - B)

        def schedule(eng, slot):
            for p in range(2):
                for b in range(B):
                    slot(p, p, b, True)
            with eng.Fori(1, GROUPS // 2 - 1) as i:
                for p in range(2):
                    for b in range(B):
                        slot(i * 2 + p, p, b, True)
            for p in range(2):
                for b in range(B):
                    slot(LAST - 1 + p, p, b, p == 0)

        @block.sync
        def _(sp):
            for dst, src in loads:
                sp.dma_start(dst, src).then_inc(weights_in, 16)

            def load(j, p):
                sp.dma_start(x_raw[:] if combined else x_res[:, p], rows(x_in, j * GROUP)).then_inc(x_loaded[p], 16)
                if not at_start(j):
                    sp.wait_ge(s["turned_c"], j)
                sp.dma_start(c_raw[:], rows(ctx_in, j * GROUP)).then_inc(c_loaded, 16)

            def store(j):
                sp.wait_ge(s["new_done"], j + 1)
                sp.dma_start(rows(x_out, j * GROUP), x_new[:]).then_inc(saved, 16)

            load(0, 0)

            def slot(j, p, b, more):
                if b == 0 and more and combined:
                    sp.wait_ge(y_used, j + 1)
                    load(j + 1, 1 - p)
                if b == 1 and project and not at_start(j):
                    store(j - 1)
                if b == 1 and more and not combined:
                    load(j + 1, 1 - p)
                if b == B - 1 and not project:
                    store(j)

            schedule(sp, slot)
            if project:
                store(LAST)
            sp.wait_ge(saved, 16 * GROUPS)

        @block.gpsimd
        def _(pool):
            nc.gpsimd.memset(minus_half[:], -0.5).then_inc(pool_consts, 1)
            nc.gpsimd.memset(qg[:], 0.0).then_inc(pool_consts, 1)
            nc.gpsimd.memset(vx[:], 0.0).then_inc(pool_consts, 1)
            pool.wait_ge(pool_consts, 3)
            for a in range(2):
                nc.gpsimd.memset(vx[a * S:a * S + S, :, :, :, :, a, HD:].rearrange("p x s b n o -> p (x s b n) o"), 1.0).then_inc(pool_consts, 1)
            pool.wait_ge(weights_in, LOADS)
            pool.wait_ge(pool_consts, 5)

            def gather(j):
                if not combined:
                    return
                nc.gpsimd.tensor_copy(pos_now[:], pos[:, bass.ds(j * NT, NT)]).then_inc(pos_step, 1)
                pool.wait_ge(pos_step, j + 1)
                if not at_start(j):
                    pool.wait_ge(y_used, j)
                pool.sem_inc(pos_turn, 1)
                for t in range(NT):
                    pool.indirect_dma_start(out=y[:, t], out_offset=None, in_=combined[0],
                                            in_offset=bass.IndirectOffsetOnAxis(ap=pos_now[:, t:t + 1], axis=0)).then_inc(y_in, 16)

            def rstd_of(j):
                pool.wait_ge(s["power_done"], j + 1)
                nc.gpsimd.tensor_tensor(rstd[:], power[:], minus_half[:], ALU.pow).then_inc(s["rstd_done"], 1)

            def cosines(j):
                if rope:
                    pool.wait_ge(s["swapped"], j + 1)
                    for k in range(2):
                        last = nc.gpsimd.tensor_tensor(qk[:, k], qk[:, k], tab[:, 2 * k].unsqueeze(1).broadcast_to([D, NT * H, HD]), ALU.mult)
                    last.then_inc(s["cosed"], 1)

            def mask(j, p, b):
                n = j * B + b
                pool.wait_ge(s["own_k_done" if own_keys else "k_done"], j + 1)
                if not isinstance(n, int) or n > 1:
                    pool.wait_ge(s["scores_mm"], n - 1)
                for src in range(NS):
                    last = nc.gpsimd.tensor_tensor(kn[:, b % 2, src], kT[:, p, src, b * S:(b + 1) * S].unsqueeze(1).broadcast_to([D, 8, S]),
                                                   n_mask[:].unsqueeze(2).broadcast_to([D, 8, S]), ALU.mult)
                last.then_inc(s["masked"], 1)

            def negate(j, p, b):
                if layer == 2:
                    pool.wait_ge(s["kept"], j * B + b + 1)
                    nc.gpsimd.tensor_tensor(e[:, b % RING, 0], e[:, b % RING, 0], neg[:].unsqueeze(1).broadcast_to([D, 8, S]), ALU.add).then_inc(s["negated"], 1)

            gather(0)
            rstd_of(0)
            gather(1)
            cosines(0)
            mask(0, 0, 0)
            if layer == 2:
                pool.wait_ge(dve_ready, 1)
            for b in range(LEAD):
                mask(0, 0, b + 1)
                negate(0, 0, b)

            def slot(j, p, b, more):
                if more or b + LEAD + 1 < B:
                    mask(*at(j, p, b + LEAD + 1))
                if more and b == TURN - 1:
                    rstd_of(j + 1)
                if more or b + LEAD < B:
                    negate(*at(j, p, b + LEAD))
                if more and b == 4:
                    cosines(j + 1)
                if more and b == 3 and not (isinstance(j, int) and j + 2 > LAST):
                    gather(j + 2)

            schedule(pool, slot)

        @block.scalar
        def _(act):
            act.wait_ge(weights_in, LOADS)
            act.wait_ge(dve_consts, 1)

            def turned(j):
                act.wait_ge(s["turned_x"], j + 1)
                nc.scalar.activation(xT[:], front[:, 0], ACT.Copy).then_inc(s["xT_done"], 1)
                act.wait_ge(s["turned_c"], j + 1)
                nc.scalar.activation(cT[:], front[:, 1], ACT.Copy).then_inc(s["cT_done"], 1)

            def double(j):
                for n, one in enumerate((cT, xT)[:NS]):
                    act.wait_ge(s[("cT_done", "xT_done")[n]], j + 1)
                    last = nc.scalar.activation(twice[n][:], one[:].rearrange("p (b k) -> p b k", b=B).unsqueeze(2).broadcast_to([D, B, 2, S]), ACT.Copy)
                last.then_inc(s["twice_done"], 1)

            def keys_queries(j, p):
                act.wait_ge(s["turned_q" if rope else "q_mm"], j + 1)
                for g in range(2):
                    f = slice(g * S, g * S + S)
                    src = front[f, 0].rearrange("p (b q) -> p b q", b=B)
                    if rope:
                        last = nc.scalar.activation(qg[f, p, :, g], src, ACT.Copy)
                    else:
                        last = nc.scalar.activation(qg[f, p, :, g], src, ACT.Identity, scale=SCALE, bias=bq[f])
                last.then_inc(s["q_done"], 1)
                act.wait_ge(s["turned_k" if rope else "k_mm"], j + 1)
                if rope:
                    nc.scalar.activation(kT[:, p, 0], front[:, 1], ACT.Copy).then_inc(s["k_done"], 1)
                else:
                    nc.scalar.activation(kT[:, p, 0], front[:, 1], ACT.Identity, bias=bk[:]).then_inc(s["k_done"], 1)
                if own_keys:
                    act.wait_ge(s["own_k_mm"], j + 1)
                    nc.scalar.activation(kT[:, p, 1], front[:, 0], ACT.Identity, bias=bk[:]).then_inc(s["own_k_done"], 1)

            def squares(j):
                act.wait_ge(s["q_mm"], j + 1)
                nc.scalar.activation(qs[:, 0].rearrange("p n d -> p (n d)"), front[:, 0], ACT.Square).then_inc(s["q_sq"], 1)
                act.wait_ge(s["k_mm"], j + 1)
                nc.scalar.activation(qs[:, 1].rearrange("p n d -> p (n d)"), front[:, 1], ACT.Square).then_inc(s["k_sq"], 1)

            def roots(j):
                act.wait_ge(s["ssqeps_done"], j + 1)
                nc.scalar.activation(rr[:], ssq[:], ACT.Sqrt).then_inc(s["sqrt_done"], 1)

            def exps(j, p, b):
                act.wait_ge(s["shifted"], j * B + b + 1)
                nc.scalar.activation(e[:, b % RING], e[:, b % RING], ACT.Exp).then_inc(s["exp_done"], 1)

            def finish(j):
                act.wait_ge(s["fin_turned"], j + 1)
                nc.scalar.activation(aT[:], front[:, 0], ACT.Copy).then_inc(s["aT_done"], 1)

            turned(0)
            if rope:
                squares(0)
                double(0)
                roots(0)
                keys_queries(0, 0)
            else:
                keys_queries(0, 0)
                double(0)
            for b in range(AHEAD):
                exps(0, 0, b)

            def slot(j, p, b, more):
                n = j * B + b
                for src in range(NS):
                    act.wait_ge(s["turned_e"], n * NS + src + 1)
                    nc.scalar.activation(pt[:, b % 2, src].rearrange("p m q -> p (m q)"), turn[:, src], ACT.Copy).then_inc(s["pt_done"], 1)
                if more and b == TURN:
                    turned(j + 1)
                if more and rope and b == TURN + 1:
                    roots(j + 1)
                if more or b + AHEAD < B:
                    exps(*at(j, p, b + AHEAD))
                if more and b == TURN:
                    if rope:
                        squares(j + 1)
                    else:
                        keys_queries(j + 1, 1 - p)
                    double(j + 1)
                if more and rope and b == ROPE:
                    keys_queries(j + 1, 1 - p)
                if b == 0 and project and not at_start(j):
                    finish(j - 1)

            schedule(act, slot)
            if project:
                finish(LAST)

        @block.vector
        def _(dve):
            dve.wait_ge(weights_in, LOADS)
            if rope:
                nc.vector.tensor_tensor(tab[:], tab[:], wrow[:], ALU.mult).then_inc(dve_consts, 1)
            elif layer == 2:
                nc.vector.tensor_scalar(bq[:], bq[:], SCALE, None, ALU.mult).then_inc(dve_consts, 1)
                dve.wait_ge(dve_consts, 1)
                nc.vector.tensor_scalar(keep[:], m8[:].bitcast(U8), -1.0, 1.0, ALU.mult, ALU.add)
                nc.vector.tensor_scalar(neg[:], m8[:].bitcast(U8), -1e9, None, ALU.mult).then_inc(dve_ready, 1)
                dve.wait_ge(dve_ready, 1)
            else:
                nc.vector.tensor_scalar(bq[:], bq[:], SCALE, None, ALU.mult).then_inc(dve_consts, 1)
            dve.wait_ge(dve_consts, 1)
            dve.wait_ge(pool_consts, 5)

            def mean_variance(j, p):
                dve.wait_ge(x_loaded[p], 16 * ((j - p) // 2 + 1) if isinstance(j, int) else 8 * (j - p) + 16)
                if combined:
                    dve.wait_ge(y_in, 16 * NT * (j + 1))
                    if not isinstance(j, int) or j > 1:
                        dve.wait_ge(s["new_done"], j - 1)
                    for t in range(NT):
                        last = nc.vector.scalar_tensor_tensor(x_res[:, p, t], y[:, t], prob[:, bass.ds(j * NT + t, 1)], x_raw[:, t], ALU.mult, ALU.add)
                    last.then_inc(y_used, 1)
                    dve.wait_ge(y_used, j + 1)
                moments(nc, dve, x_res[:, p], NT, stats, parts, mean[:], power[:], s, j + 1)

            def norm(j, p):
                dve.wait_ge(s["rstd_done"], j + 1)
                for t in range(NT):
                    last = nc.vector.tensor_scalar(xn[:, t], x_res[:, p, t], mean[:, t:t + 1], rstd[:, t:t + 1], ALU.subtract, ALU.mult)
                last.then_inc(s["norm_done"], 1)

            def values(j, p, steps):
                for n in steps:
                    src, half = V_STEPS[n]
                    bank = front[:, n % 2].rearrange("p (b n a d) -> p b n a d", b=4, a=2, d=HD)
                    dve.wait_ge(s["v_mm"], j * len(V_STEPS) + n + 1)
                    for a in range(2):
                        f = slice(a * S, a * S + S)
                        for_heads = vx[f, p, src, half * 4:half * 4 + 4, :, a, :HD]
                        if rope:
                            last = nc.vector.tensor_copy(for_heads, bank[f, :, :, a])
                        else:
                            bias = bv[f].rearrange("p (n a d) -> p n a d", a=2, d=HD)[:, :, a].unsqueeze(1).broadcast_to([S, 4, 8, HD])
                            last = nc.vector.tensor_tensor(for_heads, bank[f, :, :, a], bias, ALU.add)
                    last.then_inc(s["v_done"], 1)

            def rms(j):
                dve.wait_ge(s["q_sq"], j + 1)
                dve.wait_ge(s["k_sq"], j + 1)
                nc.vector.tensor_reduce(ssq[:], qs[:], AX.X, ALU.add).then_inc(s["ssq_done"], 1)
                dve.wait_ge(s["ssq_done"], j + 1)
                nc.vector.tensor_scalar(ssq[:], ssq[:], 1.0 / HD, RMS_EPS, ALU.mult, ALU.add).then_inc(s["ssqeps_done"], 1)

            def scale(j):
                dve.wait_ge(s["sqrt_done"], j + 1)
                nc.vector.reciprocal(rr[:], rr[:]).then_inc(s["rr_done"], 1)
                dve.wait_ge(s["rr_done"], j + 1)
                for k in range(2):
                    last = nc.vector.tensor_tensor(qk[:, k], front[:, k].rearrange("p (n d) -> p n d", d=HD),
                                                   rr[:, k].unsqueeze(2).broadcast_to([D, NT * H, HD]), ALU.mult)
                last.then_inc(s["qk_scaled"], 1)
                dve.wait_ge(s["qk_scaled"], j + 1)
                half = HD // 2
                for k in range(2):
                    for lo, hi in ((0, half), (half, 0)):
                        last = nc.vector.tensor_tensor(qs[:, k, :, lo:lo + half], qk[:, k, :, hi:hi + half],
                                                       tab[:, 2 * k + 1, lo:lo + half].unsqueeze(1).broadcast_to([D, NT * H, half]), ALU.mult)
                last.then_inc(s["swapped"], 1)

            def turn_rope(j):
                dve.wait_ge(s["swapped"], j + 1)
                dve.wait_ge(s["cosed"], j + 1)
                nc.vector.tensor_tensor(qk[:], qk[:], qs[:], ALU.add).then_inc(s["roped"], 1)

            def before_softmax(j, p, b):
                if rope and b == 1:
                    mean_variance(j, p)

            def after_row(j, p, b):
                if not rope and b == TURN - 2:
                    mean_variance(j, p)
                if b == TURN - 1:
                    norm(j, p)
                if rope and b == TURN:
                    rms(j)
                if rope and b == TURN + 1:
                    scale(j)
                if rope and b == TURN + 2:
                    turn_rope(j)
                if b == VALUES:
                    values(j, p, range(0, NS))
                if b == VALUES + 1:
                    values(j, p, range(NS, 2 * NS))

            def keep_scores(j, p, b):
                n = j * B + b
                dve.wait_ge(s["scores_mm"], n + 1)
                nc.vector.tensor_tensor(e[:, b % RING, 0], sc[:, b % AHEAD, 0].rearrange("p (n k) -> p n k", n=8),
                                        keep[:].unsqueeze(1).broadcast_to([D, 8, S]), ALU.mult).then_inc(s["kept"], 1)

            def softmax(j, p, b):
                n = j * B + b
                r = b % RING
                if layer == 2:
                    dve.wait_ge(s["negated"], n + 1)
                    src = e[:, r, 0]
                    nc.vector.tensor_reduce(mx[:, b % 2], src, AX.X, ALU.max).then_inc(s["max_done"], 1)
                elif NS == 1:
                    dve.wait_ge(s["scores_mm"], n + 1)
                    src = sc[:, b % AHEAD, 0].rearrange("p (n k) -> p n k", n=8)
                    nc.vector.tensor_reduce(mx[:, b % 2], src, AX.X, ALU.max).then_inc(s["max_done"], 1)
                else:
                    dve.wait_ge(s["scores_mm"], n + 1)
                    src = sc[:, b % AHEAD].rearrange("p s (n k) -> p s n k", n=8)
                    nc.vector.tensor_reduce(mx[:, b % 2], src.rearrange("p s n k -> p n s k"), AX.XY, ALU.max).then_inc(s["max_done"], 1)
                dve.wait_ge(s["max_done"], n + 1)
                if NS == 1:
                    nc.vector.tensor_tensor(e[:, r, 0], src, mx[:, b % 2].unsqueeze(2).broadcast_to([D, 8, S]), ALU.subtract).then_inc(s["shifted"], 1)
                else:
                    nc.vector.tensor_tensor(e[:, r], src, mx[:, b % 2].unsqueeze(1).unsqueeze(3).broadcast_to([D, NS, 8, S]), ALU.subtract).then_inc(s["shifted"], 1)

            def finish(j, p):
                dve.wait_ge(s["fin_mm"], j + 1)
                if not isinstance(j, int) or j:
                    dve.wait_ge(saved, 16 * j)
                res = x_res[:, p].rearrange("p t f -> p (t f)")
                new = x_new[:].rearrange("p t f -> p (t f)")
                if layer == 2:
                    nc.vector.tensor_tensor(new, front[:, 1], res, ALU.add).then_inc(s["fin_added"], 1)
                    dve.wait_ge(s["fin_added"], j + 1)
                    nc.vector.tensor_tensor(x_new[:], x_new[:], bo[:].unsqueeze(1).broadcast_to([D, NT, D]), ALU.add).then_inc(s["new_done"], 1)
                else:
                    nc.vector.tensor_tensor(new, front[:, 1], res, ALU.add).then_inc(s["new_done"], 1)

            for b in range(B):
                before_softmax(0, 0, b)
                after_row(0, 0, b)
            if layer == 2:
                for b in range(LEAD):
                    keep_scores(0, 0, b)
            for b in range(AHEAD):
                softmax(0, 0, b)

            def slot(j, p, b, more):
                n = j * B + b
                if b == 1 and project and not at_start(j):
                    finish(j - 1, 1 - p)
                if more:
                    before_softmax(j + 1, 1 - p, b)
                if layer == 2 and (more or b + LEAD < B):
                    keep_scores(*at(j, p, b + LEAD))
                if more or b + AHEAD < B:
                    softmax(*at(j, p, b + AHEAD))
                dve.wait_ge(s["pv_mm"], n + 1)
                sums = pv[:, b % 2, :2 * 8 * (HD + 1)].rearrange("p (n d) -> p n d", d=HD + 1)
                nc.vector.reciprocal(rden[:, b % 2], sums[:, :, HD]).then_inc(s["rden_done"], 1)
                dve.wait_ge(s["rden_done"], n + 1)
                out = slice((b % 2) * S, (b % 2) * S + S)
                for g in range(2):
                    f = slice(g * S, g * S + S)
                    last = nc.vector.tensor_tensor(attn[out, p, b // 2, g * S:(g + 1) * S].rearrange("p (n d) -> p n d", d=HD),
                                                   sums[f, g * 8:(g + 1) * 8, :HD], rden[f, b % 2, g * 8:(g + 1) * 8].unsqueeze(2).broadcast_to([S, 8, HD]), ALU.mult)
                last.then_inc(s["normed"], 1)
                if more:
                    after_row(j + 1, 1 - p, b)
                if b == B - 1 and not project:
                    if not at_start(j):
                        dve.wait_ge(saved, 16 * j)
                    dve.wait_ge(s["normed"], (j + 1) * B)
                    nc.vector.tensor_tensor(x_new[:], attn[:, p], x_res[:, p], ALU.add).then_inc(s["new_done"], 1)

            schedule(dve, slot)
            if project:
                finish(LAST, 1)

        @block.tensor
        def _(pe):
            pe.wait_ge(weights_in, LOADS)
            pe.wait_ge(pool_consts, 5)

            def turn_inputs(j):
                pe.wait_ge(s["norm_done"], j + 1)
                if not at_start(j):
                    pe.wait_ge(s["v_done"], j * len(V_STEPS))
                if project and (not isinstance(j, int) or j > 1):
                    pe.wait_ge(s["new_done"], j - 1)
                for t in range(NT):
                    last = nc.tensor.transpose(front[:, 0, t * D:(t + 1) * D], xn[:, t], ident[:])
                last.then_inc(s["turned_x"], 1)
                pe.wait_ge(c_loaded, 16 * (j + 1))
                for t in range(NT):
                    last = nc.tensor.transpose(front[:, 1, t * D:(t + 1) * D], c_raw[:, t], ident[:])
                last.then_inc(s["turned_c"], 1)

            def keys_queries(j):
                if rope:
                    for (mm, done), a, wt, k in ((("q_mm", "xT_done"), xT, wq, 0), (("k_mm", "cT_done"), cT, wk, 1)):
                        pe.wait_ge(s[done], j + 1)
                        for t in range(NT):
                            last = nc.tensor.matmul(front[:, k, t * D:(t + 1) * D], a[:, t * D:(t + 1) * D], wt[:], start=True, stop=True)
                        last.then_inc(s[mm], 1)
                else:
                    pe.wait_ge(s["xT_done"], j + 1)
                    nc.tensor.matmul(front[:, 0], wq[:], xT[:], start=True, stop=True).then_inc(s["q_mm"], 1)
                    pe.wait_ge(s["cT_done"], j + 1)
                    nc.tensor.matmul(front[:, 1], wk[:], cT[:], start=True, stop=True).then_inc(s["k_mm"], 1)

            def own_keys_mm(j):
                pe.wait_ge(s["q_done"], j + 1)
                nc.tensor.matmul(front[:, 0], wk[:], xT[:], start=True, stop=True).then_inc(s["own_k_mm"], 1)

            def turn_roped(j):
                pe.wait_ge(s["roped"], j + 1)
                for k, name in enumerate(("turned_q", "turned_k")):
                    for t in range(NT):
                        last = nc.tensor.transpose(front[:, k, t * D:(t + 1) * D], qk[:, k, t * H:(t + 1) * H].rearrange("p n d -> p (n d)"), ident[:])
                    last.then_inc(s[name], 1)

            def values(j, steps):
                for n in steps:
                    src, half = V_STEPS[n]
                    if n < 2:
                        pe.wait_ge(s["twice_done"], j + 1)
                        pe.wait_ge(s["own_k_done" if own_keys and n == 0 else "k_done"], j + 1)
                    else:
                        pe.wait_ge(s["v_done"], j * len(V_STEPS) + n - 1)
                    for b in range(4):
                        feats = twice[src][:, half * 4 + b].rearrange("p a k -> p (a k)")
                        last = nc.tensor.matmul(front[:, n % 2, b * D:(b + 1) * D], feats, wv[:], start=True, stop=True)
                    last.then_inc(s["v_mm"], 1)

            def scores(j, p, b):
                n = j * B + b
                pe.wait_ge(s["q_done"], j + 1)
                pe.wait_ge(s["masked"], n + 1)
                if not isinstance(n, int) or n >= AHEAD:
                    pe.wait_ge(s["kept" if layer == 2 else "shifted"], n - AHEAD + 1)
                for src in range(NS):
                    last = nc.tensor.matmul(sc[:, b % AHEAD, src], qg[:, p, b].rearrange("p g q -> p (g q)"),
                                            kn[:, b % 2, src].rearrange("p n k -> p (n k)"), start=True, stop=True)
                last.then_inc(s["scores_mm"], 1)

            turn_inputs(0)
            keys_queries(0)
            if own_keys:
                own_keys_mm(0)
            if rope:
                turn_roped(0)
            values(0, range(0, NS))
            values(0, range(NS, 2 * NS))
            for b in range(LEAD):
                scores(0, 0, b)

            def turn_attn(j, p):
                pe.wait_ge(s["normed"], (j + 1) * B)
                for t in range(NT):
                    last = nc.tensor.transpose(front[:, 0, t * D:(t + 1) * D], attn[:, p, t], ident[:])
                last.then_inc(s["fin_turned"], 1)

            def finish(j):
                pe.wait_ge(s["aT_done"], j + 1)
                for t in range(NT):
                    last = nc.tensor.matmul(front[:, 1, t * D:(t + 1) * D], aT[:, t * D:(t + 1) * D], wo[:], start=True, stop=True)
                last.then_inc(s["fin_mm"], 1)

            def slot(j, p, b, more):
                n = j * B + b
                pe.wait_ge(s["exp_done"], n + 1)
                for src in range(NS):
                    if not at_start(n):
                        pe.wait_ge(s["pt_done"], n * NS)
                    for k in range(4):
                        last = nc.tensor.transpose(turn[:, src, k * D:(k + 1) * D], e[:, b % RING, src, 2 * k:2 * k + 2].rearrange("p n k -> p (n k)"), ident[:])
                    last.then_inc(s["turned_e"], 1)
                if not own_keys and (more or b + LEAD < B):
                    scores(*at(j, p, b + LEAD))
                if more and b == TURN:
                    turn_inputs(j + 1)
                if b == 0:
                    pe.wait_ge(s["v_done"], (j + 1) * len(V_STEPS))
                    if project and not at_start(j):
                        turn_attn(j - 1, 1 - p)
                if not isinstance(n, int) or n > 1:
                    pe.wait_ge(s["normed"], n - 1)
                out = pv[:, b % 2, :144].rearrange("p (g m x) -> p g m x", g=2, m=4)
                for src in range(NS):
                    pe.wait_ge(s["pt_done"], n * NS + src + 1)
                    for k in range(4):
                        values_of = vx[:, p, src, b].rearrange("p (g m) a d -> p g m (a d)", g=2)[:, :, k]
                        last = nc.tensor.matmul(out[:, :, k], pt[:, b % 2, src, k], values_of, start=(src == 0 and k == 0), stop=(src == NS - 1), skip_group_check=True)
                last.then_inc(s["pv_mm"], 1)
                if more and b == TURN:
                    keys_queries(j + 1)
                if own_keys and (more or b + LEAD < B):
                    scores(*at(j, p, b + LEAD))
                if more and own_keys and b == TURN:
                    own_keys_mm(j + 1)
                if more and rope and b == ROPE:
                    turn_roped(j + 1)
                if more and b in (VALUES, VALUES + 1):
                    values(j + 1, range((b - VALUES) * NS, (b - VALUES + 1) * NS))
                if b == 0 and project and not at_start(j):
                    finish(j - 1)

            schedule(pe, slot)
            if project:
                turn_attn(LAST, 1)
                finish(LAST)


E4 = 4


def layernorm_experts(nc, c, ph, x_in, w, x_out):
    U = 2
    with ExitStack() as ctx:
        m = Space(nc, ctx, ph)
        ident, ones = m.sb("ident", [D, D]), m.sb("ones", [D, D])
        gw, gb, falling = m.sb("gw", [D, E4]), m.sb("gb", [D, E4]), m.sb("falling", [D, E4])
        w1, w2 = m.sb("w1", [D, E4, D]), m.sb("w2", [D, E4, D])
        b1, g1, be1 = (m.sb(n, [D, E4]) for n in ("b1", "g1", "be1"))
        b2, g2, be2 = m.sb("b2", [D, E4, D]), m.sb("g2", [D, E4, D]), m.sb("be2", [E4, D])
        wmean = m.sb("wmean", [D, 4, E4])
        minus_half, euler = m.sb("minus_half", [D, NT]), m.sb("euler", [D, NT])
        x, xn, xT = m.sb("x", [D, U, NT, D]), m.sb("xn", [D, U, NT, D]), m.sb("xT", [D, U, GROUP])
        stats, parts = m.sb("stats", [D, U, NT, 6]), m.sb("parts", [D, U, 3, NT])
        mean, power, rstd = (m.sb(n, [D, U, NT]) for n in ("mean", "power", "rstd"))
        score, eq, hot1, hot2, share, left = (m.sb(n, [D, U, NT, E4]) for n in ("score", "eq", "hot1", "hot2", "share", "left"))
        top1, top2, pick, ratio, w_first, w_second = (m.sb(n, [D, U, NT]) for n in ("top1", "top2", "pick", "ratio", "w_first", "w_second"))
        sq, std, hid = (m.sb(n, [D, U, E4, GROUP]) for n in ("sq", "std", "hid"))
        y, ysq = m.sb("y", [D, U, NT, E4, D]), m.sb("ysq", [D, 2, E4 * D])
        ssq = m.sb("ssq", [D, U, NT, E4])
        shareT = m.sb("shareT", [E4, U, GROUP])
        mixed, x_new, x_sum = (m.sb(n, [D, U, NT, D]) for n in ("mixed", "x_new", "x_sum"))
        ln_eps = m.sb("ln_eps", [D, 1])
        bank = m.psum("bank", [D, U, 4, GROUP])

        loads = [(ident[:], c["ident"]), (ones[:], c["ones"]), (gw[:], w["gate_W"]), (gb[:], w["gate_b"].broadcast_to([D, E4])),
                 (falling[:], c["falling"][:, :E4]), (b1[:], w["b1T"]), (g1[:], w["g1T"]), (be1[:], w["be1T"]), (be2[:], w["be2"]),
                 (w1[:], w["W1"].rearrange("(e p) f -> p e f", e=E4)), (w2[:], w["W2"].rearrange("(e p) f -> p e f", e=E4)),
                 (b2[:].rearrange("p e f -> p (e f)"), w["b2"].broadcast_to([D, E4 * D])),
                 (g2[:].rearrange("p e f -> p (e f)"), w["g2"].broadcast_to([D, E4 * D]))]
        LOADS = 16 * len(loads)
        weights_in, pool_consts, mean_steps, b1_mm = (m.sem(n) for n in ("weights_in", "pool_consts", "mean_steps", "b1_mm"))
        x_loaded = [m.sem(f"x_loaded{u}") for u in range(U)]
        saved = [m.sem(f"saved{u}") for u in range(U)]
        s = {k: m.sem(k) for k in (
            "stats_done parts_done mean_done power_done rstd_done norm_done turned xT_done logits_mm score_done top1_done eq1_done "
            "eqw1_done pick1_done hot1_done left_done top2_done eq2_done eqw2_done pick2_done hot2_done diff_done ratio_done "
            "den_done first_done second_done share1_done share_done hid_mm sq_done var_mm std_done inv_done scaled_done hid_done "
            "y_mm y_done ysq_done ssq_done var2_done std2_done inv2_done factor_done weighed gained mixed_done share_turned "
            "shareT_done offset_mm sum_done sum2_done new_done").split()}
        block = ctx.enter_context(nc.Block())
        STEPS = GROUPS // U

        def pair_count(i, u, e):
            return i * (U * E4) + (e // 2) * (2 * U) + u * 2 + e % 2 + 1

        @block.sync
        def _(sp):
            for u in range(U):
                sp.dma_start(x[:, u], rows(x_in, u * GROUP)).then_inc(x_loaded[u], 16)
            for dst, src in loads:
                sp.dma_start(dst, src).then_inc(weights_in, 16)

            def body(i, last=False):
                for u in range(U):
                    if not last:
                        sp.wait_ge(s["mixed_done"], (i * U + u) * NT + NT)
                        sp.dma_start(x[:, u], rows(x_in, (i + 1) * U * GROUP + u * GROUP)).then_inc(x_loaded[u], 16)
                for u in range(U):
                    sp.wait_ge(s["new_done"], i * U + u + 1)
                    sp.dma_start(rows(x_out, i * U * GROUP + u * GROUP), x_new[:, u]).then_inc(saved[u], 16)

            turns(sp, STEPS, body, True)
            for u in range(U):
                sp.wait_ge(saved[u], 16 * STEPS)

        @block.gpsimd
        def _(pool):
            nc.gpsimd.memset(minus_half[:], -0.5).then_inc(pool_consts, 1)
            nc.gpsimd.memset(euler[:], float(np.e)).then_inc(pool_consts, 1)
            pool.wait_ge(pool_consts, 2)
            pool.wait_ge(weights_in, LOADS)
            def turn(i):
                for u in range(U):
                    k = i * U + u + 1
                    pool.wait_ge(s["power_done"], k)
                    nc.gpsimd.tensor_tensor(rstd[:, u], power[:, u], minus_half[:], ALU.pow).then_inc(s["rstd_done"], 1)
                for u in range(U):
                    k = i * U + u + 1
                    pool.wait_ge(s["diff_done"], k)
                    nc.gpsimd.tensor_tensor(ratio[:, u], euler[:], ratio[:, u], ALU.pow).then_inc(s["ratio_done"], 1)
                for u in range(U):
                    for t in range(NT):
                        k = (i * U + u) * NT + t + 1
                        if t == 0:
                            pool.wait_ge(s["factor_done"], i * U + u + 1)
                        nc.gpsimd.tensor_tensor(y[:, u, t], y[:, u, t], ssq[:, u, t].unsqueeze(2).broadcast_to([D, E4, D]), ALU.mult).then_inc(s["weighed"], 1)
                        pool.wait_ge(s["weighed"], k)
                        nc.gpsimd.tensor_tensor(y[:, u, t], y[:, u, t], g2[:], ALU.mult).then_inc(s["gained"], 1)

            turns(pool, STEPS, turn)

        @block.scalar
        def _(act):
            act.wait_ge(mean_steps, 4)
            def turn(i):
                for u in range(U):
                    act.wait_ge(s["turned"], i * U + u + 1)
                    nc.scalar.activation(xT[:, u], bank[:, u, 0], ACT.Copy).then_inc(s["xT_done"], 1)
                for pair in range(2):
                    both = (2 * pair, 2 * pair + 1)
                    for u in range(U):
                        for e in both:
                            act.wait_ge(s["hid_mm"], pair_count(i, u, e))
                            nc.scalar.activation(sq[:, u, e], bank[:, u, 2 + e % 2], ACT.Square, bias=b1[:, e:e + 1]).then_inc(s["sq_done"], 1)
                    for u in range(U):
                        for e in both:
                            act.wait_ge(s["var_mm"], pair_count(i, u, e))
                            nc.scalar.activation(std[:, u, e], bank[:, u, e % 2], ACT.Sqrt, scale=1.0 / D, bias=ln_eps[:]).then_inc(s["std_done"], 1)
                    for u in range(U):
                        for e in both:
                            act.wait_ge(s["scaled_done"], pair_count(i, u, e))
                            nc.scalar.activation(hid[:, u, e], sq[:, u, e], ACT.Relu, scale=g1[:, e:e + 1], bias=be1[:, e:e + 1]).then_inc(s["hid_done"], 1)
                for u in range(U):
                    for t in range(NT):
                        k = (i * U + u) * NT + t + 1
                        act.wait_ge(s["y_done"], k)
                        if u * NT + t >= 2 or not at_start(i):
                            act.wait_ge(s["ssq_done"], k - 2 if u * NT + t >= 2 else i * U * NT)
                        nc.scalar.activation(ysq[:, t % 2], y[:, u, t].rearrange("p e f -> p (e f)"), ACT.Square).then_inc(s["ysq_done"], 1)
                    act.wait_ge(s["var2_done"], i * U + u + 1)
                    nc.scalar.activation(ssq[:, u], ssq[:, u], ACT.Sqrt).then_inc(s["std2_done"], 1)
                    act.wait_ge(s["share_turned"], i * U + u + 1)
                    nc.scalar.activation(shareT[:, u], bank[:E4, u, 0], ACT.Copy).then_inc(s["shareT_done"], 1)

            turns(act, STEPS, turn)

        @block.vector
        def _(dve):
            dve.wait_ge(weights_in, LOADS)
            dve.wait_ge(pool_consts, 2)
            nc.vector.memset(ln_eps[:], LN_EPS)
            nc.vector.tensor_reduce(wmean[:, 0], w1[:], AX.X, ALU.add)
            nc.vector.tensor_reduce(wmean[:, 1], w2[:], AX.X, ALU.add)
            nc.vector.tensor_reduce(wmean[:, 2], b2[:], AX.X, ALU.add).then_inc(mean_steps, 1)
            dve.wait_ge(b1_mm, 1)
            nc.vector.tensor_copy(wmean[:, 3], bank[:, 0, 0, :E4]).then_inc(mean_steps, 1)
            dve.wait_ge(mean_steps, 2)
            nc.vector.tensor_scalar(wmean[:], wmean[:], 1.0 / D, None, ALU.mult).then_inc(mean_steps, 1)
            dve.wait_ge(mean_steps, 3)
            for a, k in ((w1, 0), (w2, 1), (b2, 2)):
                nc.vector.tensor_tensor(a[:], a[:], wmean[:, k].unsqueeze(2).broadcast_to([D, E4, D]), ALU.subtract)
            nc.vector.tensor_tensor(b1[:], b1[:], wmean[:, 3], ALU.subtract).then_inc(mean_steps, 1)
            dve.wait_ge(mean_steps, 4)
            def turn(i):
                for u in range(U):
                    dve.wait_ge(x_loaded[u], 16 * (i + 1))
                    moments(nc, dve, x[:, u], NT, stats[:, u], parts[:, u], mean[:, u], power[:, u], s, i * U + u + 1)
                for u in range(U):
                    dve.wait_ge(s["rstd_done"], i * U + u + 1)
                    for t in range(NT):
                        last = nc.vector.tensor_scalar(xn[:, u, t], x[:, u, t], mean[:, u, t:t + 1], rstd[:, u, t:t + 1], ALU.subtract, ALU.mult)
                    last.then_inc(s["norm_done"], 1)
                for u in range(U):
                    k = i * U + u + 1
                    per_tile = lambda a: a[:, u].unsqueeze(2).broadcast_to([D, NT, E4])
                    per_expert = lambda a: a.unsqueeze(1).broadcast_to([D, NT, E4])
                    dve.wait_ge(s["logits_mm"], k)
                    nc.vector.tensor_tensor(score[:, u], bank[:, u, 1, :NT * E4].rearrange("p (t e) -> p t e", t=NT), per_expert(gb[:]), ALU.add).then_inc(s["score_done"], 1)
                    dve.wait_ge(s["score_done"], k)
                    for n, (src, top, hot) in enumerate(((score, top1, hot1), (left, top2, hot2)), 1):
                        if n == 2:
                            nc.vector.scalar_tensor_tensor(left[:, u], hot1[:, u], -3.0e38, score[:, u], ALU.mult, ALU.add).then_inc(s["left_done"], 1)
                            dve.wait_ge(s["left_done"], k)
                        nc.vector.tensor_reduce(top[:, u], src[:, u], AX.X, ALU.max).then_inc(s[f"top{n}_done"], 1)
                        dve.wait_ge(s[f"top{n}_done"], k)
                        nc.vector.tensor_tensor(eq[:, u], src[:, u], per_tile(top), ALU.is_equal).then_inc(s[f"eq{n}_done"], 1)
                        dve.wait_ge(s[f"eq{n}_done"], k)
                        nc.vector.tensor_tensor(eq[:, u], eq[:, u], per_expert(falling[:]), ALU.mult).then_inc(s[f"eqw{n}_done"], 1)
                        dve.wait_ge(s[f"eqw{n}_done"], k)
                        nc.vector.tensor_reduce(pick[:, u], eq[:, u], AX.X, ALU.max).then_inc(s[f"pick{n}_done"], 1)
                        dve.wait_ge(s[f"pick{n}_done"], k)
                        nc.vector.tensor_tensor(hot[:, u], eq[:, u], per_tile(pick), ALU.is_equal).then_inc(s[f"hot{n}_done"], 1)
                        dve.wait_ge(s[f"hot{n}_done"], k)
                    nc.vector.tensor_tensor(ratio[:, u], top2[:, u], top1[:, u], ALU.subtract).then_inc(s["diff_done"], 1)
                    nc.vector.tensor_tensor(x_sum[:, u], x[:, u], xn[:, u], ALU.add).then_inc(s["sum_done"], 1)
                    dve.wait_ge(s["ratio_done"], k)
                    nc.vector.tensor_scalar(w_first[:, u], ratio[:, u], 1.0, None, ALU.add).then_inc(s["den_done"], 1)
                    dve.wait_ge(s["den_done"], k)
                    nc.vector.reciprocal(w_first[:, u], w_first[:, u]).then_inc(s["first_done"], 1)
                    dve.wait_ge(s["first_done"], k)
                    nc.vector.tensor_tensor(w_second[:, u], ratio[:, u], w_first[:, u], ALU.mult).then_inc(s["second_done"], 1)
                    dve.wait_ge(s["second_done"], k)
                    nc.vector.tensor_tensor(hot1[:, u], hot1[:, u], per_tile(w_first), ALU.mult)
                    nc.vector.tensor_tensor(hot2[:, u], hot2[:, u], per_tile(w_second), ALU.mult).then_inc(s["share1_done"], 1)
                    dve.wait_ge(s["share1_done"], k)
                    nc.vector.tensor_tensor(share[:, u], hot1[:, u], hot2[:, u], ALU.add).then_inc(s["share_done"], 1)
                for pair in range(2):
                    for u in range(U):
                        for e in (2 * pair, 2 * pair + 1):
                            n = pair_count(i, u, e)
                            dve.wait_ge(s["std_done"], n)
                            nc.vector.reciprocal(std[:, u, e], std[:, u, e]).then_inc(s["inv_done"], 1)
                            dve.wait_ge(s["inv_done"], n)
                            nc.vector.scalar_tensor_tensor(sq[:, u, e], bank[:, u, 2 + e % 2], b1[:, e:e + 1], std[:, u, e], ALU.add, ALU.mult).then_inc(s["scaled_done"], 1)
                for u in range(U):
                    k = i * U + u + 1
                    for t in range(NT):
                        n = (i * U + u) * NT + t + 1
                        dve.wait_ge(s["y_mm"], n)
                        nc.vector.tensor_tensor(y[:, u, t], bank[:, u, t].rearrange("p (e f) -> p e f", e=E4), b2[:], ALU.add).then_inc(s["y_done"], 1)
                        if t:
                            dve.wait_ge(s["ysq_done"], n - 1)
                            nc.vector.tensor_reduce(ssq[:, u, t - 1], ysq[:, (t - 1) % 2].rearrange("p (e f) -> p e f", e=E4), AX.X, ALU.add).then_inc(s["ssq_done"], 1)
                    dve.wait_ge(s["ysq_done"], n)
                    nc.vector.tensor_reduce(ssq[:, u, NT - 1], ysq[:, (NT - 1) % 2].rearrange("p (e f) -> p e f", e=E4), AX.X, ALU.add).then_inc(s["ssq_done"], 1)
                    dve.wait_ge(s["ssq_done"], n)
                    nc.vector.tensor_scalar(ssq[:, u], ssq[:, u], 1.0 / D, LN_EPS, ALU.mult, ALU.add).then_inc(s["var2_done"], 1)
                    dve.wait_ge(s["std2_done"], k)
                    nc.vector.reciprocal(ssq[:, u], ssq[:, u]).then_inc(s["inv2_done"], 1)
                    dve.wait_ge(s["inv2_done"], k)
                    nc.vector.tensor_tensor(ssq[:, u], ssq[:, u], share[:, u], ALU.mult).then_inc(s["factor_done"], 1)
                for u in range(U):
                    k = i * U + u + 1
                    for t in range(NT):
                        dve.wait_ge(s["gained"], (i * U + u) * NT + t + 1)
                        nc.vector.tensor_reduce(mixed[:, u, t], y[:, u, t].rearrange("p e f -> p f e"), AX.X, ALU.add).then_inc(s["mixed_done"], 1)
                    dve.wait_ge(s["mixed_done"], (i * U + u) * NT + NT)
                    nc.vector.tensor_tensor(mixed[:, u], mixed[:, u], x_sum[:, u], ALU.add).then_inc(s["sum2_done"], 1)
                    dve.wait_ge(s["sum2_done"], k)
                    dve.wait_ge(s["offset_mm"], k)
                    if not at_start(i):
                        dve.wait_ge(saved[u], 16 * i)
                    nc.vector.tensor_tensor(x_new[:, u].rearrange("p t f -> p (t f)"), bank[:, u, 1], mixed[:, u].rearrange("p t f -> p (t f)"), ALU.add).then_inc(s["new_done"], 1)

            turns(dve, STEPS, turn)

        @block.tensor
        def _(pe):
            pe.wait_ge(weights_in, LOADS)
            nc.tensor.matmul(bank[:, 0, 0, :E4], ones[:], b1[:], start=True, stop=True).then_inc(b1_mm, 1)
            pe.wait_ge(mean_steps, 4)
            def turn(i):
                for u in range(U):
                    pe.wait_ge(s["norm_done"], i * U + u + 1)
                    if not at_start(i):
                        pe.wait_ge(s["new_done"], i * U)
                    for t in range(NT):
                        last = nc.tensor.transpose(bank[:, u, 0, t * D:(t + 1) * D], xn[:, u, t], ident[:])
                    last.then_inc(s["turned"], 1)
                for u in range(U):
                    pe.wait_ge(s["xT_done"], i * U + u + 1)
                    for t in range(NT):
                        last = nc.tensor.matmul(bank[:, u, 1, t * E4:(t + 1) * E4], xT[:, u, t * D:(t + 1) * D], gw[:], start=True, stop=True)
                    last.then_inc(s["logits_mm"], 1)
                for pair in range(2):
                    both = (2 * pair, 2 * pair + 1)
                    for u in range(U):
                        for e in both:
                            if pair:
                                pe.wait_ge(s["scaled_done"], pair_count(i, u, e - 2))
                            nc.tensor.matmul(bank[:, u, 2 + e % 2], w1[:, e], xT[:, u], start=True, stop=True).then_inc(s["hid_mm"], 1)
                    for u in range(U):
                        for e in both:
                            pe.wait_ge(s["sq_done"], pair_count(i, u, e))
                            if pair:
                                pe.wait_ge(s["std_done"], pair_count(i, u, e - 2))
                            elif e == 1:
                                pe.wait_ge(s["score_done"], i * U + u + 1)
                            nc.tensor.matmul(bank[:, u, e % 2], ones[:], sq[:, u, e], start=True, stop=True).then_inc(s["var_mm"], 1)
                for u in range(U):
                    pe.wait_ge(s["hid_done"], pair_count(i, u, E4 - 1))
                    for t in range(NT):
                        for e in range(E4):
                            last = nc.tensor.matmul(bank[:, u, t, e * D:(e + 1) * D], hid[:, u, e, t * D:(t + 1) * D], w2[:, e], start=True, stop=True)
                        last.then_inc(s["y_mm"], 1)
                for u in range(U):
                    k = i * U + u + 1
                    pe.wait_ge(s["share_done"], k)
                    pe.wait_ge(s["y_done"], (i * U + u) * NT + NT)
                    for t in range(NT):
                        last = nc.tensor.transpose(bank[:E4, u, 0, t * D:(t + 1) * D], share[:, u, t], ident[:])
                    last.then_inc(s["share_turned"], 1)
                    pe.wait_ge(s["shareT_done"], k)
                    for t in range(NT):
                        last = nc.tensor.matmul(bank[:, u, 1, t * D:(t + 1) * D], shareT[:, u, t * D:(t + 1) * D], be2[:], start=True, stop=True)
                    last.then_inc(s["offset_mm"], 1)

            turns(pe, STEPS, turn)


def combine(nc, ph, x_in, ye, pos_in, x_out):
    RING = 4
    with ExitStack() as ctx:
        m = Space(nc, ctx, ph)
        pos = m.sb("pos", [D, TOKENS // D], I32)
        x, y, x_new = (m.sb(n, [D, RING, NT, D]) for n in ("x", "y", "x_new"))
        pos_loaded, added = m.sem("pos_loaded"), m.sem("added")
        x_loaded, gathered, saved = ([m.sem(f"{n}{r}") for r in range(RING)] for n in ("x_loaded", "gathered", "saved"))
        block = ctx.enter_context(nc.Block())

        @block.sync
        def _(sp):
            sp.dma_start(pos[:], pos_in).then_inc(pos_loaded, 16)
            for g in range(GROUPS):
                if g >= RING:
                    sp.wait_ge(added, g - RING + 1)
                sp.dma_start(x[:, g % RING], rows(x_in, g * GROUP)).then_inc(x_loaded[g % RING], 16)

        @block.gpsimd
        def _(pool):
            pool.wait_ge(pos_loaded, 16)
            for g in range(GROUPS):
                if g >= RING:
                    pool.wait_ge(added, g - RING + 1)
                for t in range(NT):
                    pool.indirect_dma_start(out=y[:, g % RING, t], out_offset=None, in_=ye,
                                            in_offset=bass.IndirectOffsetOnAxis(ap=pos[:, g * NT + t:g * NT + t + 1], axis=0)).then_inc(gathered[g % RING], 16)

        @block.vector
        def _(dve):
            for g in range(GROUPS):
                r, turn = g % RING, g // RING + 1
                dve.wait_ge(x_loaded[r], 16 * turn)
                dve.wait_ge(gathered[r], 16 * NT * turn)
                if turn > 1:
                    dve.wait_ge(saved[r], 16 * (turn - 1))
                nc.vector.tensor_tensor(x_new[:, r], y[:, r], x[:, r], ALU.add).then_inc(added, 1)

        @block.scalar
        def _(act):
            for g in range(GROUPS):
                act.wait_ge(added, g + 1)
                act.dma_start(rows(x_out, g * GROUP), x_new[:, g % RING]).then_inc(saved[g % RING], 16)
            for r in range(RING):
                act.wait_ge(saved[r], 16 * (GROUPS // RING))


def build(nc, t, x, out):
    def scratch(name, shape, dt=F32):
        return nc.dram_tensor(name, shape, dt).ap()

    x1, x2, x3, x4, x5, x6 = (scratch(f"x_{n}", (TOKENS, D)) for n in range(1, 7))
    xe, ye = scratch("expert_in", (XE_ROWS, D)), scratch("expert_out", (XE_ROWS, D))
    pos, prob, table = scratch("pos", (D, TOKENS // D), I32), scratch("prob", (D, TOKENS // D)), scratch("table", (1, SLOTS), I32)
    part = lambda prefix: {k[len(prefix):]: v for k, v in t.items() if k.startswith(prefix)}
    expert = lambda prefix: [t[prefix + k] for k in ("w1", "b1", "w2", "b2")]

    slot_attention(nc, t, x, t["ctx"], x1)
    route(nc, t, "route0", x1, "cosine", xe, pos, prob, table, True, True)
    experts(nc, t, "experts0", xe, table, expert("L0f_"), ye, True)

    w = part("L1a_")
    w["norm"] = (w["qn"], w["kn"])
    attention(nc, t, "att1", 1, x1, t["ctx"], w, x2, (ye, pos, prob))
    layernorm_experts(nc, t, "lnx1", x2, part("L1f_"), x3)

    attention(nc, t, "att2", 2, x3, t["ctx"], part("L2a_"), x4, None)
    route(nc, t, "route2", x4, (t["L2f_gw"], t["L2f_gb"]), xe, pos, prob, table, True, False)
    experts(nc, t, "experts2", xe, table, expert("L2f_"), ye, False)

    attention(nc, t, "att3", 3, x4, t["ctx"], part("L3a_"), x5, (ye, pos, prob))
    route(nc, t, "route3", x5, (t["L3f_gw"], t["L3f_gb"]), xe, pos, prob, table, False, False)
    experts(nc, t, "experts3", xe, table, expert("L3f_"), ye, False)
    combine(nc, "combine3", x5, ye, pos, out)


def rope_tables():
    out = np.zeros((D, 4, HD), np.float32)
    for k, (theta, scale) in enumerate(((32.0, HD ** -0.5), (1000.0, 1.0))):
        freqs = np.float32(theta) ** (-np.arange(0, HD, 2, dtype=np.float32) / HD)
        angle = np.arange(S, dtype=np.float32)[:, None] * freqs[None, :]
        cos, sin = np.cos(angle), np.sin(angle)
        out[:, 2 * k] = np.tile(np.concatenate([cos, cos], 1), (2, 1)) * scale
        out[:, 2 * k + 1] = np.tile(np.concatenate([-sin, sin], 1), (2, 1)) * scale
    return out


def constants():
    ar = np.arange
    return {
        "ident": np.eye(D, dtype=np.float32),
        "ones": np.ones((D, D), np.float32),
        "pair_ones": np.kron(np.eye(2, dtype=np.float32), np.ones((S, S), np.float32)),
        "pair_ident": np.tile(np.eye(S, dtype=np.float32), (2, 1)),
        "before": np.triu(np.ones((D, D), np.float32), 1),
        "falling": np.tile(ar(E, 0, -1, dtype=np.float32), (D, 1)),
        "steps": np.tile(ar(TOKENS // SLOT, dtype=np.float32) * SLOT, (D, 1)),
        "slot_no": np.tile(ar(SLOTS, dtype=np.float32), (D, 1)),
        "n_mask": (((ar(D) // HD) % 8)[:, None] == ar(8)[None]).astype(np.float32),
        "rope": rope_tables(),
        "zero_row": np.zeros((1, E), np.float32),
    }


def layout(a):
    col = lambda v: v.reshape(D, 1)
    row = lambda v: v.reshape(1, -1)
    chunks = lambda b: b.reshape(E, 4, D).transpose(0, 2, 1).reshape(E * D, 4)
    second = lambda w: w.reshape(E, 4, D, D).transpose(0, 2, 1, 3).reshape(E * D, 4 * D)
    t = {
        "ctx": a["ctx_1024"].reshape(TOKENS, D),
        "L0_Wk": a["L0_xattn_Wk"], "L0_Wq": a["L0_xattn_Wq"], "L0_Wv": a["L0_xattn_Wv"],
        "L0_wihT": a["L0_xattn_gru_wih"].T, "L0_whhT": a["L0_xattn_gru_whh"].T,
        "L0_bih": a["L0_xattn_gru_bih"].reshape(3, D).T, "L0_bhh": a["L0_xattn_gru_bhh"].reshape(3, D).T,
        "L0_w_slot": col(a["L0_xattn_slot_norm_w"]), "L0_w_in": col(a["L0_xattn_input_norm_w"]),
        "L0_w_redT": a["L0_ffn_w_red"].T, "L0_wg": a["L0_ffn_wg"],
        "L0f_w1": a["L0_ffn_w1"].reshape(E * D, -1), "L0f_b1": chunks(a["L0_ffn_b1"]),
        "L0f_w2": second(a["L0_ffn_w2"]), "L0f_b2": a["L0_ffn_b2"],
        "L1a_q": a["L1_xattn_Wq"].T, "L1a_k": a["L1_xattn_Wk"].T, "L1a_v": a["L1_xattn_Wv"].T, "L1a_o": a["L1_xattn_Wo"].T,
        "L1a_qn": row(a["L1_xattn_q_norm_w"]), "L1a_kn": row(a["L1_xattn_k_norm_w"]),
        "L1f_gate_W": a["L1_ffn_gate_W"], "L1f_gate_b": row(a["L1_ffn_gate_b"]),
        "L1f_W1": a["L1_ffn_W1"].reshape(E4 * D, D), "L1f_W2": a["L1_ffn_W2"].reshape(E4 * D, D),
        "L1f_b1T": a["L1_ffn_b1"].T, "L1f_g1T": a["L1_ffn_g1"].T, "L1f_be1T": a["L1_ffn_be1"].T,
        "L1f_b2": row(a["L1_ffn_b2"]), "L1f_g2": row(a["L1_ffn_g2"]), "L1f_be2": a["L1_ffn_be2"],
        "L2a_q": a["L2_xattn_W_q"], "L2a_k": a["L2_xattn_W_k"], "L2a_v": a["L2_xattn_W_v"], "L2a_o": a["L2_xattn_W_o"],
        "L2a_bq": col(a["L2_xattn_b_q"]), "L2a_bk": col(a["L2_xattn_b_k"]), "L2a_bv": row(a["L2_xattn_b_v"]),
        "L2a_bo": row(a["L2_xattn_b_o"]), "L2a_mask": np.ascontiguousarray(a["mask_SxS2_bk1"]).view(np.uint32),
        "L2f_gw": a["L2_ffn_router_W"], "L2f_gb": row(a["L2_ffn_router_b"]),
        "L2f_w1": a["L2_ffn_W1"].reshape(E * D, -1), "L2f_b1": chunks(a["L2_ffn_b1"]),
        "L2f_w2": second(a["L2_ffn_W2"]), "L2f_b2": a["L2_ffn_b2"],
        "L3a_q": a["L3_xattn_Wq"].T, "L3a_k": a["L3_xattn_Wk"].T, "L3a_v": a["L3_xattn_Wv"].T,
        "L3a_bq": col(a["L3_xattn_bq"]), "L3a_bk": col(a["L3_xattn_bk"]), "L3a_bv": row(a["L3_xattn_bv"]),
        "L3f_gw": a["L3_ffn_gate_w"].T, "L3f_gb": row(a["L3_ffn_gate_b"]),
        "L3f_w1": a["L3_ffn_w1"].transpose(0, 2, 1).reshape(E * D, -1), "L3f_b1": chunks(a["L3_ffn_b1"]),
        "L3f_w2": second(a["L3_ffn_w2"].transpose(0, 2, 1)), "L3f_b2": a["L3_ffn_b2"],
    }
    return {k: np.ascontiguousarray(v) for k, v in t.items()}


def kernel(**inputs):
    import concourse.bacc as bacc
    from concourse.bass_utils import run_bass_kernel_spmd

    a = {k: np.asarray(v) for k, v in inputs.items()}
    arrays = {"x": a["x"].reshape(TOKENS, D), **layout(a), **constants()}
    nc = bacc.Bacc("TRN2", target_bir_lowering=False, num_devices=1)
    t = {k: nc.dram_tensor(f"in_{k}", v.shape, mybir.dt.from_np(v.dtype), kind="ExternalInput").ap() for k, v in arrays.items()}
    out = nc.dram_tensor("out", (TOKENS, D), F32, kind="ExternalOutput").ap()
    build(nc, t, t["x"], out)
    r = run_bass_kernel_spmd(nc, [{f"in_{k}": v for k, v in arrays.items()}], core_ids=[0])
    return r.results[0]["out"].reshape(a["x"].shape)
```

```python
from contextlib import ExitStack

import numpy as np

import concourse.bass as bass
from concourse import mybir

F32 = mybir.dt.float32
I32 = mybir.dt.int32
U8 = mybir.dt.uint8
ALU = mybir.AluOpType
ACT = mybir.ActivationFunctionType
AX = mybir.AxisListType

D = 128
TOKENS = 8192
NT = 4
GROUP = NT * D
GROUPS = TOKENS // GROUP
S = 64
LN_EPS = 1e-5
RMS_EPS = 1e-6


def rows(dram, start, tiles=NT):
    return dram[bass.ds(start, tiles * D), :].rearrange("(t p) f -> p t f", p=D)


def at_start(i):
    return isinstance(i, int) and i == 0


def turns(eng, count, turn, last_apart=False):
    turn(0)
    with eng.Fori(1, count - 1 if last_apart else count) as i:
        turn(i)
    if last_apart:
        turn(count - 1, last=True)


class Space:

    def __init__(self, nc, ctx, phase):
        self.nc, self.ctx, self.phase, self.sems = nc, ctx, phase, []
        ctx.callback(self.clear)

    def clear(self):
        self.nc.clear_and_free_semaphores(self.sems)
        self.nc.all_engine_barrier()

    def sb(self, name, shape, dt=F32):
        return self.ctx.enter_context(self.nc.sbuf_tensor(f"{self.phase}_{name}", shape, dt))

    def psum(self, name, shape):
        return self.ctx.enter_context(self.nc.psum_tensor(f"{self.phase}_{name}", shape, F32))

    def sem(self, name):
        self.sems.append(self.nc.alloc_semaphore(f"{self.phase}_{name}"))
        return self.sems[-1]


def slot_attention(nc, c, x_in, ctx_in, x_out):
    U = 2
    ROUNDS = 3
    SCALE = float(D) ** -0.5
    with ExitStack() as ctx:
        m = Space(nc, ctx, "slots")
        wk, wq, wv = (m.sb(n, [D, D]) for n in ("wk", "wq", "wv"))
        wihT, whhT = m.sb("wihT", [D, 3 * D]), m.sb("whhT", [D, 3 * D])
        bih, bhh = m.sb("bih", [D, 3]), m.sb("bhh", [D, 3])
        w_slot, w_in = m.sb("w_slot", [D, 1]), m.sb("w_in", [D, 1])
        ident, ones, pair_ones = m.sb("ident", [D, D]), m.sb("ones", [D, D]), m.sb("pair_ones", [D, D])
        minus_half = m.sb("minus_half", [D, 2 * NT])
        keyT = m.sb("keyT", [D, D])
        val3 = m.sb("val3", [D, 3 * D])
        k_scale = m.sb("k_scale", [D, 1])
        half_b = m.sb("half_b", [D, 3])
        x_raw, c_raw = m.sb("x_raw", [D, U, NT, D]), m.sb("c_raw", [D, U, NT, D])
        stats, mv, mean = m.sb("stats", [D, U, 2 * NT, 6]), m.sb("mv", [D, U, 3, 2 * NT]), m.sb("mean", [D, U, 2 * NT])
        halves, quarters, per_row, eps = (m.sb(n, [D, 2 * NT]) for n in ("halves", "quarters", "per_row", "eps"))
        power, rstd = m.sb("power", [D, U, 2 * NT]), m.sb("rstd", [D, U, 2 * NT])
        xn, cn = m.sb("xn", [D, U, NT, D]), m.sb("cn", [D, U, NT, D])
        h, cT, kT = (m.sb(n, [D, U, GROUP]) for n in ("h", "cT", "kT"))
        v3 = m.sb("v3", [D, U, NT, 3 * D])
        sq = m.sb("sq", [D, U, GROUP])
        ms, rs = m.sb("ms", [D, U, NT]), m.sb("rs", [D, U, NT])
        r_diag, r_row = m.sb("r_diag", [D, U, NT, S]), m.sb("r_row", [D, U, NT * S])
        pair_ident = m.sb("pair_ident", [D, S])
        mx, total = m.sb("mx", [D, U, NT]), m.sb("total", [D, U, NT])
        expo, attn, colr = (m.sb(n, [D, U, NT, S]) for n in ("expo", "attn", "colr"))
        attn_bd = m.sb("attn_bd", [D, U, NT, 2, S])
        tr, tz, z, z_rest, zh, hn, n_in, n = (m.sb(k, [D, U, GROUP]) for k in ("tr", "tz", "z", "z_rest", "zh", "hn", "n_in", "n"))
        half = m.sb("half", [D, 1])
        x_res, x_new = m.sb("x_res", [D, U, NT, D]), m.sb("x_new", [D, U, NT, D])
        bank = m.psum("bank", [D, U, 4, GROUP])

        weights_in = m.sem("weights_in")
        pool_consts, dve_consts = m.sem("pool_consts"), m.sem("dve_consts")
        prep_mm, prep_set = m.sem("prep_mm"), m.sem("prep_set")
        raw_in = [m.sem(f"raw_in{u}") for u in range(U)]
        res_in = [m.sem(f"res_in{u}") for u in range(U)]
        out_done = [m.sem(f"out_done{u}") for u in range(U)]
        names = (
            "stats_done sums_done quartered squared power_raw power_done rstd_done norm_done turned_x turned_c hT_done cT_done "
            "keys_mm kT_done v3_mm v3_done sq_done ssq_mm ms_done rs_done r_diag_done r_row_mm r_row_done scores_mm scaled max_done shifted "
            "exp_done total_done inv_done attn_done colsum_mm coleps_done colr_done attn_bd_done hn_mm r_mm n_mm z_mm "
            "r_done z_done hn_done tz_done z_rest_done tn1_done n_in_done n_done zh_done upd_done h_done hback_mm new_done"
        ).split()
        s = {k: m.sem(k) for k in names}
        block = ctx.enter_context(nc.Block())

        LOADS = 13

        @block.sync
        def _(sp):
            for dst, src in ((wk, c["L0_Wk"]), (wq, c["L0_Wq"]), (wv, c["L0_Wv"]), (wihT, c["L0_wihT"]),
                             (whhT, c["L0_whhT"]), (bih, c["L0_bih"]), (bhh, c["L0_bhh"]), (w_slot, c["L0_w_slot"]),
                             (w_in, c["L0_w_in"]), (ident, c["ident"]), (ones, c["ones"]), (pair_ones, c["pair_ones"]), (pair_ident, c["pair_ident"])):
                sp.dma_start(dst[:], src).then_inc(weights_in, 16)
            for u in range(U):
                sp.dma_start(x_raw[:, u], rows(x_in, u * GROUP)).then_inc(raw_in[u], 16)
                sp.dma_start(c_raw[:, u], rows(ctx_in, u * GROUP)).then_inc(raw_in[u], 16)

            def body(i, last=False):
                if not last:
                    for u in range(U):
                        sp.wait_ge(s["norm_done"], i * U + u + 1)
                        sp.dma_start(x_raw[:, u], rows(x_in, (i + 1) * U * GROUP + u * GROUP)).then_inc(raw_in[u], 16)
                        sp.dma_start(c_raw[:, u], rows(ctx_in, (i + 1) * U * GROUP + u * GROUP)).then_inc(raw_in[u], 16)
                for u in range(U):
                    if not at_start(i):
                        sp.wait_ge(s["new_done"], i * U)
                    sp.dma_start(x_res[:, u], rows(x_in, i * U * GROUP + u * GROUP)).then_inc(res_in[u], 16)
                for u in range(U):
                    sp.wait_ge(s["new_done"], i * U + u + 1)
                    sp.dma_start(rows(x_out, i * U * GROUP + u * GROUP), x_new[:, u]).then_inc(out_done[u], 16)

            turns(sp, GROUPS // U, body, True)
            for u in range(U):
                sp.wait_ge(out_done[u], 16 * (GROUPS // U))

        @block.gpsimd
        def _(pool):
            nc.gpsimd.memset(minus_half[:], -0.5).then_inc(pool_consts, 1)
            nc.gpsimd.memset(attn_bd[:], 0.0).then_inc(pool_consts, 1)
            for dst, value in ((halves[:], 0.5), (quarters[:], 0.25), (per_row[:], 1.0 / D), (eps[:, :NT], LN_EPS), (eps[:, NT:], RMS_EPS)):
                nc.gpsimd.memset(dst, value).then_inc(pool_consts, 1)
            pool.wait_ge(pool_consts, 7)

            def roots(i):
                for u in range(U):
                    k = i * U + u + 1
                    pool.wait_ge(s["stats_done"], k)
                    st = stats[:, u]
                    nc.gpsimd.tensor_tensor(mv[:, u, 0], st[:, :, 1], st[:, :, 4], ALU.add)
                    nc.gpsimd.tensor_tensor(mv[:, u, 1], st[:, :, 1], st[:, :, 4], ALU.subtract)
                    nc.gpsimd.tensor_tensor(mv[:, u, 2], st[:, :, 2], st[:, :, 5], ALU.add).then_inc(s["sums_done"], 1)
                    pool.wait_ge(s["sums_done"], k)
                    nc.gpsimd.tensor_tensor(mean[:, u], mv[:, u, 0], halves[:], ALU.mult)
                    nc.gpsimd.tensor_tensor(mv[:, u, 0], mv[:, u, 0], mv[:, u, 0], ALU.mult)
                    nc.gpsimd.tensor_tensor(mv[:, u, 1], mv[:, u, 1], mv[:, u, 1], ALU.mult)
                    nc.gpsimd.tensor_tensor(mv[:, u, 2], mv[:, u, 2], per_row[:], ALU.mult).then_inc(s["squared"], 1)
                    pool.wait_ge(s["squared"], k)
                    nc.gpsimd.tensor_tensor(mv[:, u, 1, NT:], mv[:, u, 1, NT:], mv[:, u, 0, NT:], ALU.add)
                    nc.gpsimd.tensor_tensor(mv[:, u, 2], mv[:, u, 2], eps[:], ALU.add).then_inc(s["power_raw"], 1)
                    pool.wait_ge(s["power_raw"], k)
                    nc.gpsimd.tensor_tensor(mv[:, u, 1], mv[:, u, 1], quarters[:], ALU.mult).then_inc(s["quartered"], 1)
                    pool.wait_ge(s["quartered"], k)
                    nc.gpsimd.tensor_tensor(power[:, u], mv[:, u, 1], mv[:, u, 2], ALU.add).then_inc(s["power_done"], 1)
                    pool.wait_ge(s["power_done"], k)
                    nc.gpsimd.tensor_tensor(rstd[:, u], power[:, u], minus_half[:], ALU.pow).then_inc(s["rstd_done"], 1)

            def turn(i, last=False):
                for r in range(ROUNDS):
                    for u in range(U):
                        k = (i * ROUNDS + r) * U + u + 1
                        pool.wait_ge(s["ms_done"], k)
                        nc.gpsimd.tensor_tensor(rs[:, u], ms[:, u], minus_half[:, :NT], ALU.pow).then_inc(s["rs_done"], 1)
                    if r == 1 and not last:
                        roots(i + 1)
                    for u in range(U):
                        k = (i * ROUNDS + r) * U + u + 1
                        pool.wait_ge(s["z_done"], k)
                        nc.gpsimd.tensor_tensor(zh[:, u], z[:, u], h[:, u], ALU.mult).then_inc(s["zh_done"], 1)

            roots(0)
            turns(pool, GROUPS // U, turn, True)

        @block.scalar
        def _(act):
            act.wait_ge(prep_mm, 1)
            act.wait_ge(weights_in, 16 * LOADS)
            nc.scalar.activation(keyT[:], bank[:, 0, 0, :D], ACT.Copy, scale=w_in[:]).then_inc(prep_set, 1)
            nc.scalar.activation(val3[:], bank[:, 0, 1, :3 * D], ACT.Copy, scale=w_in[:]).then_inc(prep_set, 1)
            act.wait_ge(dve_consts, 3)
            def square(i, r, u):
                k = (i * ROUNDS + r) * U + u + 1
                if r == 0:
                    act.wait_ge(s["hT_done"], i * U + u + 1)
                else:
                    act.wait_ge(s["h_done"], k - U)
                nc.scalar.activation(sq[:, u], h[:, u], ACT.Square).then_inc(s["sq_done"], 1)

            def turn(i):
                for u in range(U):
                    act.wait_ge(s["turned_c"], i * U + u + 1)
                    nc.scalar.activation(cT[:, u], bank[:, u, 1], ACT.Copy).then_inc(s["cT_done"], 1)
                for u in range(U):
                    act.wait_ge(s["turned_x"], i * U + u + 1)
                    nc.scalar.activation(h[:, u], bank[:, u, 0], ACT.Copy).then_inc(s["hT_done"], 1)
                for u in range(U):
                    square(i, 0, u)
                for u in range(U):
                    k = i * U + u + 1
                    act.wait_ge(s["keys_mm"], k)
                    nc.scalar.activation(kT[:, u], bank[:, u, 2], ACT.Copy, scale=k_scale[:]).then_inc(s["kT_done"], 1)
                for u in range(U):
                    for t, b in enumerate((3, 2, 3, 2)):
                        act.wait_ge(s["v3_mm"], (i * U + u) * NT + t + 1)
                        nc.scalar.activation(v3[:, u, t], bank[:, u, b, :3 * D], ACT.Copy).then_inc(s["v3_done"], 1)
                for r in range(ROUNDS):
                    for u in range(U):
                        if r:
                            square(i, r, u)
                    for u in range(U):
                        k = (i * ROUNDS + r) * U + u + 1
                        act.wait_ge(s["r_row_mm"], k)
                        nc.scalar.activation(r_row[:, u], bank[:, u, 0, :NT * S], ACT.Copy).then_inc(s["r_row_done"], 1)
                    for u in range(U):
                        act.wait_ge(s["hn_mm"], (i * ROUNDS + r) * U + u + 1)
                        nc.scalar.activation(hn[:, u], bank[:, u, 3], ACT.Identity, scale=0.5, bias=half_b[:, 2:3]).then_inc(s["hn_done"], 1)
                    for u in range(U):
                        k = (i * ROUNDS + r) * U + u + 1
                        act.wait_ge(s["shifted"], k)
                        nc.scalar.activation(expo[:, u], expo[:, u], ACT.Exp).then_inc(s["exp_done"], 1)
                    for u in range(U):
                        k = (i * ROUNDS + r) * U + u + 1
                        act.wait_ge(s["r_mm"], k)
                        nc.scalar.activation(tr[:, u], bank[:, u, 0], ACT.Tanh, scale=0.5, bias=half_b[:, 0:1]).then_inc(s["r_done"], 1)
                        act.wait_ge(s["z_mm"], k)
                        nc.scalar.activation(tz[:, u], bank[:, u, 1], ACT.Tanh, scale=0.5, bias=half_b[:, 1:2]).then_inc(s["tz_done"], 1)
                        act.wait_ge(s["tz_done"], k)
                        nc.scalar.activation(z[:, u], tz[:, u], ACT.Identity, scale=0.5, bias=half[:]).then_inc(s["z_done"], 1)
                        nc.scalar.activation(z_rest[:, u], tz[:, u], ACT.Identity, scale=-0.5, bias=half[:]).then_inc(s["z_rest_done"], 1)
                        act.wait_ge(s["n_in_done"], k)
                        nc.scalar.activation(n[:, u], n_in[:, u], ACT.Tanh, bias=bih[:, 2:3]).then_inc(s["n_done"], 1)

            turns(act, GROUPS // U, turn)

        @block.vector
        def _(dve):
            dve.wait_ge(weights_in, 16 * LOADS)
            nc.vector.memset(half[:], 0.5)
            nc.vector.tensor_scalar(k_scale[:], w_slot[:], SCALE, None, ALU.mult).then_inc(dve_consts, 1)
            nc.vector.tensor_tensor(half_b[:, 0:2], bih[:, 0:2], bhh[:, 0:2], ALU.add).then_inc(dve_consts, 1)
            nc.vector.tensor_scalar(half_b[:, 2:3], bhh[:, 2:3], 0.5, None, ALU.mult)
            dve.wait_ge(dve_consts, 2)
            nc.vector.tensor_scalar(half_b[:, 0:2], half_b[:, 0:2], 0.5, None, ALU.mult).then_inc(dve_consts, 1)
            def statistics(i):
                for u in range(U):
                    dve.wait_ge(raw_in[u], 32 * (i + 1))
                    for t in range(NT):
                        nc.vector.bn_stats(stats[:, u, t], x_raw[:, u, t])
                        last = nc.vector.bn_stats(stats[:, u, NT + t], c_raw[:, u, t])
                    last.then_inc(s["stats_done"], 1)

            def normalise(i):
                for u in range(U):
                    dve.wait_ge(s["rstd_done"], i * U + u + 1)
                    for t in range(NT):
                        nc.vector.tensor_scalar(xn[:, u, t], x_raw[:, u, t], mean[:, u, t:t + 1], rstd[:, u, t:t + 1], ALU.subtract, ALU.mult)
                        last = nc.vector.tensor_scalar(cn[:, u, t], c_raw[:, u, t], rstd[:, u, NT + t:NT + t + 1], None, ALU.mult)
                    last.then_inc(s["norm_done"], 1)

            def turn(i, last=False):
                more = not last
                for r in range(ROUNDS):
                    if r == 1 and more:
                        statistics(i + 1)
                    if r == 2 and more:
                        normalise(i + 1)
                    count = lambda u: (i * ROUNDS + r) * U + u + 1
                    for u in range(U):
                        dve.wait_ge(s["ssq_mm"], count(u))
                        nc.vector.tensor_scalar(ms[:, u], bank[:, u, 0, :NT], 1.0 / D, RMS_EPS, ALU.mult, ALU.add).then_inc(s["ms_done"], 1)
                    for u in range(U):
                        dve.wait_ge(s["rs_done"], count(u))
                        nc.vector.tensor_tensor(r_diag[:, u], pair_ident[:].unsqueeze(1).broadcast_to([D, NT, S]),
                                                rs[:, u].unsqueeze(2).broadcast_to([D, NT, S]), ALU.mult).then_inc(s["r_diag_done"], 1)
                    for u in range(U):
                        dve.wait_ge(s["scores_mm"], count(u))
                        dve.wait_ge(s["r_row_done"], count(u))
                        for b in range(2):
                            p = slice(S * b, S * b + S)
                            own = bank[p, u, 1].rearrange("p (t b q) -> p t b q", t=NT, b=2)[:, :, b]
                            last = nc.vector.tensor_tensor(expo[p, u], own, r_row[p, u].rearrange("p (t q) -> p t q", t=NT), ALU.mult)
                        last.then_inc(s["scaled"], 1)
                        dve.wait_ge(s["scaled"], count(u))
                        nc.vector.tensor_reduce(mx[:, u], expo[:, u], AX.X, ALU.max).then_inc(s["max_done"], 1)
                        dve.wait_ge(s["max_done"], count(u))
                        nc.vector.tensor_tensor(expo[:, u], expo[:, u], mx[:, u].unsqueeze(2).broadcast_to([D, NT, S]),
                                                ALU.subtract).then_inc(s["shifted"], 1)
                    for u in range(U):
                        dve.wait_ge(s["exp_done"], count(u))
                        nc.vector.tensor_reduce(total[:, u], expo[:, u], AX.X, ALU.add).then_inc(s["total_done"], 1)
                        dve.wait_ge(s["total_done"], count(u))
                        nc.vector.reciprocal(total[:, u], total[:, u]).then_inc(s["inv_done"], 1)
                        dve.wait_ge(s["inv_done"], count(u))
                        nc.vector.tensor_tensor(attn[:, u], expo[:, u], total[:, u].unsqueeze(2).broadcast_to([D, NT, S]),
                                                ALU.mult).then_inc(s["attn_done"], 1)
                    for u in range(U):
                        dve.wait_ge(s["colsum_mm"], count(u))
                        nc.vector.tensor_scalar(colr[:, u], bank[:, u, 2, :NT * S], RMS_EPS, None, ALU.add).then_inc(s["coleps_done"], 1)
                        dve.wait_ge(s["coleps_done"], count(u))
                        nc.vector.reciprocal(colr[:, u], colr[:, u]).then_inc(s["colr_done"], 1)
                        dve.wait_ge(s["colr_done"], count(u))
                        for b in range(2):
                            p = slice(S * b, S * b + S)
                            last = nc.vector.tensor_tensor(attn_bd[p, u, :, b], attn[p, u], colr[p, u], ALU.mult)
                        last.then_inc(s["attn_bd_done"], 1)
                    for u in range(U):
                        dve.wait_ge(s["hn_done"], count(u))
                        dve.wait_ge(s["r_done"], count(u))
                        nc.vector.scalar_tensor_tensor(n_in[:, u], tr[:, u], 1.0, hn[:, u], ALU.add, ALU.mult).then_inc(s["tn1_done"], 1)
                        dve.wait_ge(s["tn1_done"], count(u))
                        dve.wait_ge(s["n_mm"], count(u))
                        nc.vector.tensor_tensor(n_in[:, u], n_in[:, u], bank[:, u, 2], ALU.add).then_inc(s["n_in_done"], 1)
                        dve.wait_ge(s["n_done"], count(u))
                        dve.wait_ge(s["z_rest_done"], count(u))
                        nc.vector.tensor_tensor(n[:, u], z_rest[:, u], n[:, u], ALU.mult).then_inc(s["upd_done"], 1)
                        dve.wait_ge(s["upd_done"], count(u))
                        dve.wait_ge(s["zh_done"], count(u))
                        nc.vector.tensor_tensor(h[:, u], n[:, u], zh[:, u], ALU.add).then_inc(s["h_done"], 1)
                for u in range(U):
                    k = i * U + u + 1
                    dve.wait_ge(s["hback_mm"], k)
                    dve.wait_ge(res_in[u], 16 * (i + 1))
                    if not at_start(i):
                        dve.wait_ge(out_done[u], 16 * i)
                    nc.vector.tensor_tensor(x_new[:, u], bank[:, u, 0], x_res[:, u].rearrange("p t f -> p (t f)"), ALU.add).then_inc(s["new_done"], 1)

            statistics(0)
            normalise(0)
            turns(dve, GROUPS // U, turn, True)

        @block.tensor
        def _(pe):
            pe.wait_ge(weights_in, 16 * LOADS)
            nc.tensor.matmul(bank[:, 0, 0, :D], wk[:], wq[:], start=True, stop=True)
            nc.tensor.matmul(bank[:, 0, 1, :3 * D], wv[:], wihT[:], start=True, stop=True).then_inc(prep_mm, 1)
            pe.wait_ge(prep_set, 2)
            pe.wait_ge(pool_consts, 7)

            def hidden_n(u):
                nc.tensor.matmul(bank[:, u, 3], whhT[:, 2 * D:], h[:, u], start=True, stop=True).then_inc(s["hn_mm"], 1)

            def open_round(i, r):
                for u in range(U):
                    pe.wait_ge(s["sq_done"], (i * ROUNDS + r) * U + u + 1)
                    for t in range(NT):
                        last = nc.tensor.matmul(bank[:, u, 0, t:t + 1], sq[:, u, t * D:(t + 1) * D], ones[:, :1], start=True, stop=True)
                    last.then_inc(s["ssq_mm"], 1)
                    if r == 0:
                        pe.wait_ge(s["kT_done"], i * U + u + 1)
                    for t in range(NT):
                        c_ = slice(t * D, (t + 1) * D)
                        last = nc.tensor.matmul(bank[:, u, 1, c_], kT[:, u, c_], h[:, u, c_], start=True, stop=True)
                    last.then_inc(s["scores_mm"], 1)
                    if r:
                        hidden_n(u)

            def turn(i):
                for u in range(U):
                    pe.wait_ge(s["norm_done"], i * U + u + 1)
                    for t in range(NT):
                        last = nc.tensor.transpose(bank[:, u, 1, t * D:(t + 1) * D], cn[:, u, t], ident[:])
                    last.then_inc(s["turned_c"], 1)
                for u in range(U):
                    if not at_start(i):
                        pe.wait_ge(s["new_done"], (i - 1) * U + u + 1)
                    for t in range(NT):
                        last = nc.tensor.transpose(bank[:, u, 0, t * D:(t + 1) * D], xn[:, u, t], ident[:])
                    last.then_inc(s["turned_x"], 1)
                for u in range(U):
                    pe.wait_ge(s["cT_done"], i * U + u + 1)
                    nc.tensor.matmul(bank[:, u, 2], keyT[:], cT[:, u], start=True, stop=True).then_inc(s["keys_mm"], 1)
                open_round(i, 0)
                for u in range(U):
                    for t, b in enumerate((3, 2, 3, 2)):
                        if t > 1:
                            pe.wait_ge(s["v3_done"], (i * U + u) * NT + t - 1)
                        nc.tensor.matmul(bank[:, u, b, :3 * D], cT[:, u, t * D:(t + 1) * D], val3[:], start=True, stop=True).then_inc(s["v3_mm"], 1)
                for r in range(ROUNDS):
                    count = lambda u: (i * ROUNDS + r) * U + u + 1
                    if r:
                        open_round(i, r)
                    else:
                        for u in range(U):
                            pe.wait_ge(s["v3_done"], (i * U + u) * NT + NT)
                            hidden_n(u)
                    for u in range(U):
                        pe.wait_ge(s["r_diag_done"], count(u))
                        nc.tensor.matmul(bank[:, u, 0, :NT * S], pair_ones[:], r_diag[:, u], start=True, stop=True).then_inc(s["r_row_mm"], 1)
                    for u in range(U):
                        pe.wait_ge(s["scaled"], count(u))
                        nc.tensor.matmul(bank[:, u, 0], whhT[:, :D], h[:, u], start=True, stop=False)
                        nc.tensor.matmul(bank[:, u, 1], whhT[:, D:2 * D], h[:, u], start=True, stop=False)
                    for u in range(U):
                        pe.wait_ge(s["attn_done"], count(u))
                        nc.tensor.matmul(bank[:, u, 2, :NT * S], pair_ones[:], attn[:, u], start=True, stop=True).then_inc(s["colsum_mm"], 1)
                    for u in range(U):
                        pe.wait_ge(s["attn_bd_done"], count(u))
                        for g, name in ((0, "r_mm"), (2, "n_mm"), (1, "z_mm")):
                            for t in range(NT):
                                last = nc.tensor.matmul(bank[:, u, g, t * D:(t + 1) * D], v3[:, u, t, g * D:(g + 1) * D], attn_bd[:, u, t],
                                                        start=(g == 2), stop=(g == 2 or t == NT - 1))
                            last.then_inc(s[name], 1)
                for u in range(U):
                    pe.wait_ge(s["h_done"], (i * ROUNDS + ROUNDS - 1) * U + u + 1)
                    for t in range(NT):
                        last = nc.tensor.transpose(bank[:, u, 0, t * D:(t + 1) * D], h[:, u, t * D:(t + 1) * D], ident[:])
                    last.then_inc(s["hback_mm"], 1)

            turns(pe, GROUPS // U, turn)


E = 8
R_TILES = 8
R_STEPS = TOKENS // (R_TILES * D)
SLOT_TILES = 2
SLOT = SLOT_TILES * D
SLOTS = TOKENS // SLOT + E
TABLE_STEPS = 12
EXPERT_ROWS = TOKENS + SLOT
IDLE = E * EXPERT_ROWS
XE_ROWS = IDLE + E * SLOT
FILLS = 2 * E
XE_COLS = D + 1
YE_ROWS = TOKENS + FILLS * SLOT


def moments(nc, dve, raw, tiles, stats, parts, mean, power, s, k):
    for t in range(tiles):
        last = nc.vector.bn_stats(stats[:, t], raw[:, t])
    last.then_inc(s["stats_done"], 1)
    dve.wait_ge(s["stats_done"], k)
    nc.vector.tensor_tensor(parts[:, 0], stats[:, :, 1], stats[:, :, 4], ALU.add)
    nc.vector.tensor_tensor(parts[:, 1], stats[:, :, 1], stats[:, :, 4], ALU.subtract)
    nc.vector.tensor_tensor(parts[:, 2], stats[:, :, 2], stats[:, :, 5], ALU.add).then_inc(s["parts_done"], 1)
    dve.wait_ge(s["parts_done"], k)
    nc.vector.tensor_scalar(mean, parts[:, 0], 0.5, None, ALU.mult)
    nc.vector.tensor_tensor(parts[:, 1], parts[:, 1], parts[:, 1], ALU.mult)
    nc.vector.tensor_scalar(parts[:, 2], parts[:, 2], 1.0 / D, LN_EPS, ALU.mult, ALU.add).then_inc(s["mean_done"], 1)
    dve.wait_ge(s["mean_done"], k)
    nc.vector.scalar_tensor_tensor(power, parts[:, 1], 0.25, parts[:, 2], ALU.mult, ALU.add).then_inc(s["power_done"], 1)


def route(nc, c, ph, x_in, gate, xe, prob_out, table_out, weighted):
    with ExitStack() as ctx:
        m = Space(nc, ctx, ph)
        T, N = R_TILES, TOKENS // D
        ident, ones, before = m.sb("ident", [D, D]), m.sb("ones", [D, D]), m.sb("before", [D, D])
        gw, gb = m.sb("gw", [D, E]), m.sb("gb", [D, E])
        falling, restart = m.sb("falling", [D, E]), m.sb("restart", [D, E, T])
        idle = m.sb("idle", [D, FILLS, SLOT_TILES, XE_COLS])
        token_no = m.sb("token_no", [D, N + FILLS * SLOT_TILES], I32)
        raw, xn, xnT = m.sb("raw", [D, 2, T, D]), m.sb("xn", [D, N, XE_COLS]), m.sb("xnT", [D, 2, T * D])
        stats, parts = m.sb("stats", [D, 2, T, 6]), m.sb("parts", [D, 2, 3, T])
        mean, power, std, rstd = (m.sb(n, [D, N]) for n in ("mean", "power", "std", "rstd"))
        logit, hot, eq, expo, rank = (m.sb(n, [D, N, E]) for n in ("logit", "hot", "eq", "expo", "rank"))
        top, pick, prob, esum, posf, basef = (m.sb(n, [D, N]) for n in ("top", "pick", "prob", "esum", "posf", "basef"))
        tot, incl, base = (m.sb(n, [D, R_STEPS, E, T]) for n in ("tot", "incl", "base"))
        carry = m.sb("carry", [D, R_STEPS + 1, E])
        pos = m.sb("pos", [D, N], I32)
        steps, slot_no = m.sb("steps", [D, TOKENS // SLOT]), m.sb("slot_no", [D, SLOTS])
        over, need = m.sb("over", [D, E, TOKENS // SLOT]), m.sb("need", [D, E])
        cum, jump, count, end = m.sb("cum", [D, E]), m.sb("jump", [D, E]), m.sb("count", [D, E]), m.sb("end", [D, E], I32)
        past, tabf, tab = m.sb("past", [D, 2, SLOTS, E]), m.sb("tabf", [D, 2, SLOTS]), m.sb("tab", [D, 2, SLOTS], I32)
        pT = m.psum("pT", [D, 4, 4 * D])
        pL, pR, pS, pW = (m.psum(n, [D, 512]) for n in ("pL", "pR", "pS", "pW"))

        weights_in, pool_consts, gate_done = m.sem("weights_in"), m.sem("pool_consts"), m.sem("gate_done")
        gates, scattered, saved = m.sem("gate_steps"), m.sem("scattered"), m.sem("saved")
        raw_in = [m.sem(f"raw_in{u}") for u in range(2)]
        s = {k: m.sem(k) for k in (
            "stats_done parts_done mean_done power_done std_done rstd_done norm_done turned xnT_done logits_mm logit_done top_done "
            "eq_done eqw_done pick_done hot_done shifted exp_done esum_done prob_done ranks_mm tot_done incl_done base0_done "
            "base_done rank_done own_rank_done posf_done numbered carry_done table_step pos_done").split()}
        LOADS = 10
        if gate == "cosine":
            w_redT, wg, wgT = m.sb("w_redT", [16, D]), m.sb("wg", [E, 16]), m.sb("wgT", [16, E])
            wsq, wnorm, half8 = m.sb("wsq", [E, 16]), m.sb("wnorm", [E, 1]), m.sb("half8", [E, 1])
            LOADS = 11
        block = ctx.enter_context(nc.Block())

        @block.sync
        def _(sp):
            for i in range(2):
                sp.dma_start(raw[:, i], rows(x_in, i * T * D, T)).then_inc(raw_in[i], 16)
            own = ((w_redT[:], c["L0_w_redT"]), (wg[:], c["L0_wg"])) if gate == "cosine" else ((gw[:], gate[0]),)
            for dst, src in own + ((ident[:], c["ident"]), (ones[:], c["ones"]), (before[:], c["before"]), (falling[:], c["falling"]),
                                   (steps[:], c["steps"]), (slot_no[:], c["slot_no"]), (token_no[:], c["token_no"]), (carry[:, 0], c["expert_row"])):
                sp.dma_start(dst, src).then_inc(weights_in, 16)
            bias = c["zero_row"][0:1, :E] if gate == "cosine" else gate[1]
            sp.dma_start(gb[:], bias.broadcast_to([D, E])).then_inc(weights_in, 16)
            for i in range(2, R_STEPS):
                sp.wait_ge(s["norm_done"], i - 1)
                sp.dma_start(raw[:, i % 2], rows(x_in, i * T * D, T)).then_inc(raw_in[i % 2], 16)
            sp.wait_ge(s["numbered"], 2)
            sp.dma_start(rows(xe, IDLE, E * SLOT_TILES), idle[:, E:].rearrange("p s t f -> p (s t) f")).then_inc(saved, 16)
            sp.wait_ge(s["table_step"], 1)
            for e in range(E):
                behind = sp.value_load(end[0:1, e:e + 1], min_val=0, max_val=XE_ROWS - SLOT)
                sp.dma_start(rows(xe, behind, SLOT_TILES), idle[:, e]).then_inc(saved, 16)
            sp.wait_ge(s["table_step"], TABLE_STEPS)
            sp.dma_start(table_out, tab[0:1].rearrange("p a n -> p (a n)")).then_inc(saved, 16)
            if weighted:
                sp.wait_ge(s["prob_done"], 1)
                sp.dma_start(prob_out, prob[:]).then_inc(saved, 16)
            sp.wait_ge(saved, 16 * (E + (3 if weighted else 2)))

        @block.gpsimd
        def _(pool):
            nc.gpsimd.memset(idle[:], 0.0).then_inc(pool_consts, 1)
            nc.gpsimd.memset(restart[:], 1.0).then_inc(pool_consts, 1)
            pool.wait_ge(pool_consts, 2)
            nc.gpsimd.memset(restart[:, :, 0:1], 0.0).then_inc(pool_consts, 1)
            if gate == "cosine":
                nc.gpsimd.memset(half8[:], 0.5).then_inc(pool_consts, 1)
                pool.wait_ge(pool_consts, 4)
                pool.wait_ge(gates, 1)
                nc.gpsimd.tensor_tensor(wnorm[:], wnorm[:], half8[:], ALU.pow).then_inc(gates, 1)

            def scatter(i):
                pool.wait_ge(s["pos_done"], i + 1)
                pool.wait_ge(s["norm_done"], i + 1)
                pool.wait_ge(s["numbered"], 1)
                for t in range(i * T, (i + 1) * T):
                    pool.indirect_dma_start(out=xe, out_offset=bass.IndirectOffsetOnAxis(ap=pos[:, t:t + 1], axis=0),
                                            in_=xn[:, t], in_offset=None).then_inc(scattered, 16)

            for i in range(R_STEPS):
                scatter(i)
            pool.wait_ge(scattered, 16 * N)

        @block.scalar
        def _(act):
            if gate == "cosine":
                act.wait_ge(weights_in, 16 * LOADS)
                nc.scalar.activation(wsq[:], wg[:], ACT.Square, accum_out=wnorm[:]).then_inc(gates, 1)

            def roots(i):
                own = slice(i * T, (i + 1) * T)
                act.wait_ge(s["power_done"], i + 1)
                nc.scalar.activation(std[:, own], power[:, own], ACT.Sqrt).then_inc(s["std_done"], 1)

            roots(0)
            for i in range(R_STEPS):
                for g in range(T // 4):
                    act.wait_ge(s["turned"], i * (T // 4) + g + 1)
                    nc.scalar.activation(xnT[:, i % 2, g * 4 * D:(g + 1) * 4 * D], pT[:, g], ACT.Copy).then_inc(s["xnT_done"], 1)
                if i < R_STEPS - 1:
                    roots(i + 1)
            if weighted:
                act.wait_ge(s["shifted"], R_STEPS)
                nc.scalar.activation(expo[:], expo[:], ACT.Exp).then_inc(s["exp_done"], 1)

        @block.vector
        def _(dve):
            def mean_variance(i):
                own = slice(i * T, (i + 1) * T)
                dve.wait_ge(raw_in[i % 2], 16 * (i // 2 + 1))
                moments(nc, dve, raw[:, i % 2], T, stats[:, i % 2], parts[:, i % 2], mean[:, own], power[:, own], s, i + 1)

            mean_variance(0)
            dve.wait_ge(weights_in, 16 * LOADS)
            if gate == "cosine":
                dve.wait_ge(gates, 2)
                nc.vector.tensor_scalar(wnorm[:], wnorm[:], 1e-4, None, ALU.max).then_inc(gates, 1)
                dve.wait_ge(gates, 3)
                nc.vector.reciprocal(wnorm[:], wnorm[:]).then_inc(gates, 1)
                dve.wait_ge(gates, 4)
                nc.vector.tensor_scalar(wg[:], wg[:], wnorm[:], None, ALU.mult).then_inc(gates, 1)
                dve.wait_ge(gates, 6)
                nc.vector.tensor_copy(wgT[:], pW[:16, :E]).then_inc(gates, 1)
                dve.wait_ge(gates, 8)
                nc.vector.tensor_copy(gw[:], pW[:, 16:16 + E]).then_inc(gate_done, 1)
            dve.wait_ge(pool_consts, 3)
            nc.vector.tensor_copy(xn[:, :, D].bitcast(I32), token_no[:, :N]).then_inc(s["numbered"], 1)
            nc.vector.tensor_copy(idle[:, :, :, D].bitcast(I32), token_no[:, N:].rearrange("p (s t) -> p s t", s=FILLS)).then_inc(s["numbered"], 1)

            def normalise(i):
                own = slice(i * T, (i + 1) * T)
                dve.wait_ge(s["std_done"], i + 1)
                nc.vector.reciprocal(rstd[:, own], std[:, own]).then_inc(s["rstd_done"], 1)
                dve.wait_ge(s["rstd_done"], i + 1)
                for t in range(T):
                    a = i * T + t
                    last = nc.vector.tensor_scalar(xn[:, a, :D], raw[:, i % 2, t], mean[:, a:a + 1], rstd[:, a:a + 1], ALU.subtract, ALU.mult)
                last.then_inc(s["norm_done"], 1)

            def choose(i):
                own = slice(i * T, (i + 1) * T)
                per_tile = lambda a: a.unsqueeze(2).broadcast_to([D, T, E])
                per_expert = lambda a: a.unsqueeze(1).broadcast_to([D, T, E])
                k = i + 1
                dve.wait_ge(s["logits_mm"], k)
                nc.vector.tensor_tensor(logit[:, own], pL[:, :T * E].rearrange("p (t e) -> p t e", t=T), per_expert(gb[:]), ALU.add).then_inc(s["logit_done"], 1)
                dve.wait_ge(s["logit_done"], k)
                nc.vector.tensor_reduce(top[:, own], logit[:, own], AX.X, ALU.max).then_inc(s["top_done"], 1)
                dve.wait_ge(s["top_done"], k)
                nc.vector.tensor_tensor(eq[:, own], logit[:, own], per_tile(top[:, own]), ALU.is_equal).then_inc(s["eq_done"], 1)
                if weighted:
                    nc.vector.tensor_tensor(expo[:, own], logit[:, own], per_tile(top[:, own]), ALU.subtract).then_inc(s["shifted"], 1)
                dve.wait_ge(s["eq_done"], k)
                nc.vector.tensor_tensor(eq[:, own], eq[:, own], per_expert(falling[:]), ALU.mult).then_inc(s["eqw_done"], 1)
                dve.wait_ge(s["eqw_done"], k)
                nc.vector.tensor_reduce(pick[:, own], eq[:, own], AX.X, ALU.max).then_inc(s["pick_done"], 1)
                dve.wait_ge(s["pick_done"], k)
                nc.vector.tensor_tensor(hot[:, own], eq[:, own], per_tile(pick[:, own]), ALU.is_equal).then_inc(s["hot_done"], 1)

            def number(i):
                own = slice(i * T, (i + 1) * T)
                k = i + 1
                dve.wait_ge(s["ranks_mm"], k)
                nc.vector.tensor_copy(tot[:, i], pS[:, :T * E].rearrange("p (t e) -> p e t", t=T)).then_inc(s["tot_done"], 1)
                dve.wait_ge(s["tot_done"], k)
                flat = lambda a: a.rearrange("p e t -> p (e t)")
                nc.vector.tensor_tensor_scan(flat(incl[:, i]), flat(restart[:]), flat(tot[:, i]), 0.0, ALU.mult, ALU.add).then_inc(s["incl_done"], 1)
                dve.wait_ge(s["incl_done"], k)
                nc.vector.tensor_tensor(base[:, i], incl[:, i], tot[:, i], ALU.subtract).then_inc(s["base0_done"], 1)
                if i:
                    dve.wait_ge(s["carry_done"], i)
                nc.vector.tensor_tensor(carry[:, i + 1], carry[:, i], incl[:, i, :, T - 1], ALU.add).then_inc(s["carry_done"], 1)
                dve.wait_ge(s["base0_done"], k)
                nc.vector.tensor_tensor(base[:, i], base[:, i], carry[:, i].unsqueeze(2).broadcast_to([D, E, T]), ALU.add).then_inc(s["base_done"], 1)
                dve.wait_ge(s["base_done"], k)
                nc.vector.tensor_tensor(rank[:, own], pR[:, :T * E].rearrange("p (t e) -> p t e", t=T),
                                        base[:, i].rearrange("p e t -> p t e"), ALU.add).then_inc(s["rank_done"], 1)
                dve.wait_ge(s["rank_done"], k)
                nc.vector.tensor_tensor(rank[:, own], rank[:, own], hot[:, own], ALU.mult).then_inc(s["own_rank_done"], 1)
                dve.wait_ge(s["own_rank_done"], k)
                nc.vector.tensor_reduce(posf[:, own], rank[:, own], AX.X, ALU.add).then_inc(s["posf_done"], 1)
                dve.wait_ge(s["posf_done"], k)
                nc.vector.tensor_copy(pos[:, own], posf[:, own]).then_inc(s["pos_done"], 1)

            normalise(0)
            for i in range(R_STEPS):
                if i < R_STEPS - 1:
                    mean_variance(i + 1)
                choose(i)
                if i < R_STEPS - 1:
                    normalise(i + 1)
                number(i)
            NS = TOKENS // SLOT
            steps_done = [0]

            def step(ins):
                steps_done[0] += 1
                ins.then_inc(s["table_step"], 1)
                dve.wait_ge(s["table_step"], steps_done[0])

            per_slot = lambda a: a[:].unsqueeze(1).broadcast_to([D, SLOTS, E])
            dve.wait_ge(s["carry_done"], R_STEPS)
            step(nc.vector.tensor_copy(end[:], carry[:, R_STEPS]))
            step(nc.vector.tensor_tensor(count[:], carry[:, R_STEPS], carry[:, 0], ALU.subtract))
            step(nc.vector.tensor_tensor(over[:], count[:].unsqueeze(2).broadcast_to([D, E, NS]), steps[:].unsqueeze(1).broadcast_to([D, E, NS]), ALU.is_gt))
            step(nc.vector.tensor_reduce(need[:], over[:], AX.X, ALU.add))
            step(nc.vector.tensor_tensor_scan(cum[:], ones[:, :E], need[:], 0.0, ALU.mult, ALU.add))
            step(nc.vector.tensor_scalar(jump[:], need[:], -float(SLOT), float(EXPERT_ROWS), ALU.mult, ALU.add))
            step(nc.vector.tensor_tensor(past[:, 0], slot_no[:].unsqueeze(2).broadcast_to([D, SLOTS, E]), per_slot(cum), ALU.is_ge))
            step(nc.vector.tensor_tensor(past[:, 1], past[:, 0], per_slot(jump), ALU.mult))
            step(nc.vector.tensor_reduce(tabf[:], past[:], AX.X, ALU.add))
            step(nc.vector.tensor_scalar(tabf[:, 0], tabf[:, 0], float(E - 1), None, ALU.min))
            step(nc.vector.scalar_tensor_tensor(tabf[:, 1], slot_no[:], float(SLOT), tabf[:, 1], ALU.mult, ALU.add))
            step(nc.vector.tensor_copy(tab[:], tabf[:]))
            if weighted:
                dve.wait_ge(s["exp_done"], 1)
                nc.vector.tensor_reduce(esum[:], expo[:], AX.X, ALU.add).then_inc(s["esum_done"], 1)
                dve.wait_ge(s["esum_done"], 1)
                nc.vector.reciprocal(prob[:], esum[:]).then_inc(s["prob_done"], 1)

        @block.tensor
        def _(pe):
            pe.wait_ge(weights_in, 16 * LOADS)
            if gate == "cosine":
                pe.wait_ge(gates, 5)
                nc.tensor.transpose(pW[:16, :E], wg[:], ident[:E, :E]).then_inc(gates, 1)
                pe.wait_ge(gates, 7)
                nc.tensor.matmul(pW[:, 16:16 + E], w_redT[:], wgT[:], start=True, stop=True).then_inc(gates, 1)
                pe.wait_ge(gate_done, 1)

            def logits(i):
                pe.wait_ge(s["norm_done"], i + 1)
                for g in range(T // 4):
                    if i:
                        pe.wait_ge(s["xnT_done"], (i - 1) * (T // 4) + g + 1)
                    for t in range(4):
                        last = nc.tensor.transpose(pT[:, g, t * D:(t + 1) * D], xn[:, i * T + g * 4 + t, :D], ident[:])
                    last.then_inc(s["turned"], 1)
                if i:
                    pe.wait_ge(s["logit_done"], i)
                for g in range(T // 4):
                    pe.wait_ge(s["xnT_done"], i * (T // 4) + g + 1)
                    for t in range(4 * g, 4 * g + 4):
                        last = nc.tensor.matmul(pL[:, t * E:(t + 1) * E], xnT[:, i % 2, t * D:(t + 1) * D], gw[:], start=True, stop=True)
                last.then_inc(s["logits_mm"], 1)

            def ranks(i):
                pe.wait_ge(s["hot_done"], i + 1)
                if i:
                    pe.wait_ge(s["rank_done"], i)
                hot_all = hot[:, i * T:(i + 1) * T].rearrange("p t e -> p (t e)")
                nc.tensor.matmul(pR[:, :T * E], before[:], hot_all, start=True, stop=True)
                nc.tensor.matmul(pS[:, :T * E], ones[:], hot_all, start=True, stop=True).then_inc(s["ranks_mm"], 1)

            for i in range(R_STEPS):
                logits(i)
                ranks(i)


def experts(nc, c, ph, xe, table_in, w, ye, gelu):
    RING = 4
    U = 2
    F = 4
    TURNS = SLOTS // RING
    with ExitStack() as ctx:
        m = Space(nc, ctx, ph)
        ident, tab = m.sb("ident", [D, D]), m.sb("tab", [1, 2 * SLOTS], I32)
        w1, w2 = m.sb("w1", [D, RING, F * D]), m.sb("w2", [D, RING, F * D])
        b1, b2 = m.sb("b1", [D, RING, F]), m.sb("b2", [D, RING, D])
        x, xT = m.sb("x", [D, RING, SLOT_TILES, XE_COLS]), m.sb("xT", [D, U, SLOT])
        token = m.sb("token", [D, RING, SLOT_TILES], I32)
        h, y = m.sb("h", [D, U, F, SLOT]), m.sb("y", [D, RING, SLOT_TILES, D])
        pX, pH, pY = m.psum("pX", [D, U, 512]), m.psum("pH", [D, U, F, SLOT]), m.psum("pY", [D, U, 512])
        setup_in, tab_in, store_turn = m.sem("setup_in"), m.sem("tab_in"), m.sem("store_turn")
        x_loaded, w1_in, w2_in, saved = ([m.sem(f"{n}{r}") for r in range(RING)] for n in ("x_loaded", "w1_in", "w2_in", "saved"))
        s = {k: m.sem(k) for k in "turned xT_done hidden_mm act_done y_mm y_done".split()}
        block = ctx.enter_context(nc.Block())

        @block.sync
        def _(sp):
            sp.dma_start(tab[:], table_in).then_inc(tab_in, 16)
            sp.dma_start(ident[:], c["ident"]).then_inc(setup_in, 16)
            sp.wait_ge(tab_in, 16)

            def turn(i):
                for r in range(RING):
                    k = i * RING + r
                    e = sp.value_load(tab[0:1, bass.ds(k, 1)], min_val=0, max_val=E - 1)
                    first_row = sp.value_load(tab[0:1, bass.ds(k + SLOTS, 1)], min_val=0, max_val=XE_ROWS - SLOT)
                    if not at_start(i):
                        sp.wait_ge(s["y_done"], k - RING + 1)
                    sp.dma_start(x[:, r], rows(xe, first_row, SLOT_TILES)).then_inc(x_loaded[r], 16)
                    sp.dma_start(w1[:, r], w[0][bass.ds(e * D, D), :]).then_inc(w1_in[r], 16)
                    sp.dma_start(b1[:, r], w[1][bass.ds(e * D, D), :]).then_inc(w1_in[r], 16)
                    sp.dma_start(w2[:, r], w[2][bass.ds(e * D, D), :]).then_inc(w2_in[r], 16)
                    sp.dma_start(b2[:, r], w[3][bass.ds(e, 1), :].broadcast_to([D, D])).then_inc(w2_in[r], 16)

            turns(sp, TURNS, turn)

        @block.gpsimd
        def _(pool):
            def turn(i):
                for r in range(RING):
                    pool.wait_ge(s["y_done"], i * RING + r + 1)
                    pool.sem_inc(store_turn, 1)
                    for t in range(SLOT_TILES):
                        pool.indirect_dma_start(out=ye, out_offset=bass.IndirectOffsetOnAxis(ap=token[:, r, t:t + 1], axis=0),
                                                in_=y[:, r, t], in_offset=None).then_inc(saved[r], 16)

            turns(pool, TURNS, turn)
            for r in range(RING):
                pool.wait_ge(saved[r], 16 * SLOT_TILES * TURNS)

        @block.scalar
        def _(act):
            def copy_turned(k, u):
                act.wait_ge(s["turned"], k + 1)
                nc.scalar.activation(xT[:, u], pX[:, u, :SLOT], ACT.Copy).then_inc(s["xT_done"], 1)

            def turn(i, last=False):
                for r in range(RING):
                    k, u = i * RING + r, r % 2
                    act.wait_ge(w1_in[r], 32 * (i + 1))
                    for f in range(F):
                        act.wait_ge(s["hidden_mm"], k * F + (f | 1) + 1)
                        if f == 0 and not (last and r == RING - 1):
                            copy_turned(k + 1, 1 - u)
                        if gelu:
                            nc.scalar.activation(h[:, u, f], pH[:, u, f], ACT.Gelu, bias=b1[:, r, f:f + 1]).then_inc(s["act_done"], 1)
                        else:
                            nc.scalar.activation(h[:, u, f], pH[:, u, f], ACT.Relu, bias=b1[:, r, f:f + 1]).then_inc(s["act_done"], 1)

            copy_turned(0, 0)
            turns(act, TURNS, turn, True)

        @block.vector
        def _(dve):
            def turn(i):
                for r in range(RING):
                    k = i * RING + r
                    dve.wait_ge(x_loaded[r], 16 * (i + 1))
                    dve.wait_ge(w2_in[r], 32 * (i + 1))
                    dve.wait_ge(s["y_mm"], k + 1)
                    if not at_start(i):
                        dve.wait_ge(saved[r], 16 * SLOT_TILES * i)
                    nc.vector.tensor_copy(token[:, r], x[:, r, :, D].bitcast(I32))
                    nc.vector.tensor_tensor(y[:, r], pY[:, r % 2, :SLOT].rearrange("p (t f) -> p t f", t=SLOT_TILES),
                                            b2[:, r].unsqueeze(1).broadcast_to([D, SLOT_TILES, D]), ALU.add).then_inc(s["y_done"], 1)

            turns(dve, TURNS, turn)

        @block.tensor
        def _(pe):
            pe.wait_ge(setup_in, 16)

            def turn_rows(i, r):
                k = i * RING + r
                pe.wait_ge(x_loaded[r], 16 * (i + 1))
                if not (at_start(i) and r < 2):
                    pe.wait_ge(s["xT_done"], k - 1)
                for t in range(SLOT_TILES):
                    last = nc.tensor.transpose(pX[:, r % 2, t * D:(t + 1) * D], x[:, r, t, :D], ident[:])
                last.then_inc(s["turned"], 1)

            def hidden(i, r):
                k, u = i * RING + r, r % 2
                pe.wait_ge(w1_in[r], 32 * (i + 1))
                pe.wait_ge(s["xT_done"], k + 1)
                for f in range(F):
                    if not (at_start(i) and r < 2):
                        pe.wait_ge(s["act_done"], (k - 2) * F + (f | 1) + 1)
                    nc.tensor.matmul(pH[:, u, f], w1[:, r, f * D:(f + 1) * D], xT[:, u], start=True, stop=True).then_inc(s["hidden_mm"], 1)

            def second(i, r):
                k, u = i * RING + r, r % 2
                pe.wait_ge(w2_in[r], 32 * (i + 1))
                if not (at_start(i) and r < 2):
                    pe.wait_ge(s["y_done"], k - 1)
                for t in range(SLOT_TILES):
                    for f in range(F):
                        pe.wait_ge(s["act_done"], k * F + f + 1)
                        last = nc.tensor.matmul(pY[:, u, t * D:(t + 1) * D], h[:, u, f, t * D:(t + 1) * D], w2[:, r, f * D:(f + 1) * D],
                                                start=(f == 0), stop=(f == F - 1))
                last.then_inc(s["y_mm"], 1)

            def turn(i, last=False):
                for r in range(RING):
                    if r < RING - 1:
                        turn_rows(i, r + 1)
                    elif not last:
                        turn_rows(i + 1, 0)
                    hidden(i, r)
                    if r:
                        second(i, r - 1)
                    elif not at_start(i):
                        second(i - 1, RING - 1)

            turn_rows(0, 0)
            turns(pe, TURNS, turn, True)
            second(TURNS - 1, RING - 1)


H = 16
HD = D // H
B = GROUP // S


def attention(nc, c, ph, layer, x_in, ctx_in, w, x_out, combined):
    own_keys = layer == 3
    NS = 2 if own_keys else 1
    LEAD = 3 if layer == 2 else 2
    AHEAD = 1 if own_keys else 2
    RING = 2 * AHEAD
    SCALE = float(HD) ** -0.5
    rope = layer == 1
    project = layer != 3
    TURN = 3 if layer == 2 else 2
    ROPE = TURN + 3
    VALUES = 6 if rope else 5
    with ExitStack() as ctx:
        m = Space(nc, ctx, ph)
        ident, n_mask = m.sb("ident", [D, D]), m.sb("n_mask", [D, 8])
        wq, wk, wv = (m.sb(n, [D, D]) for n in ("wq", "wk", "wv"))
        minus_half = m.sb("minus_half", [D, NT])
        x_res, c_raw, xn = m.sb("x_res", [D, 2, NT, D]), m.sb("c_raw", [D, NT, D]), m.sb("xn", [D, NT, D])
        stats, parts = m.sb("stats", [D, NT, 6]), m.sb("parts", [D, 3, NT])
        mean, power, rstd = (m.sb(n, [D, NT]) for n in ("mean", "power", "rstd"))
        xT, cT = m.sb("xT", [D, GROUP]), m.sb("cT", [D, GROUP])
        twice = [m.sb(f"twice{n}", [D, B, 2, S]) for n in range(NS)]
        qg = m.sb("qg", [D, 2, B, 2, S])
        kT = m.sb("kT", [D, 2, NS, GROUP])
        kn = m.sb("kn", [D, 2, NS, 8, S])
        vx = m.sb("vx", [D, 2, NS, B, 8, 2, HD + 1])
        e = m.sb("e", [D, RING, NS, 8, S])
        mx, rden = m.sb("mx", [D, 2, 8]), m.sb("rden", [D, 2, H])
        pt = m.sb("pt", [D, 2, NS, 4, D])
        attn, x_new = m.sb("attn", [D, 2, NT, D]), m.sb("x_new", [D, NT, D])
        front = m.psum("front", [D, 2, GROUP])
        sc = m.psum("sc", [D, AHEAD, NS, 8 * S])
        turn = m.psum("turn", [D, NS, GROUP])
        pv = m.psum("pv", [D, 2, 512])

        loads = [(ident[:], c["ident"]), (n_mask[:], c["n_mask"]), (wq[:], w["q"]), (wk[:], w["k"]), (wv[:], w["v"])]
        if project:
            wo, aT = m.sb("wo", [D, D]), m.sb("aT", [D, GROUP])
            loads += [(wo[:], w["o"])]
        if not rope:
            bq, bk, bv = m.sb("bq", [D, 1]), m.sb("bk", [D, 1]), m.sb("bv", [D, D])
            loads += [(bq[:], w["bq"]), (bk[:], w["bk"]), (bv[:], w["bv"].broadcast_to([D, D]))]
        if layer == 2:
            bo, m8 = m.sb("bo", [D, D]), m.sb("m8", [D, S // 4], mybir.dt.uint32)
            keep, neg = m.sb("keep", [D, S]), m.sb("neg", [D, S])
            loads += [(bo[:], w["bo"].broadcast_to([D, D])), (m8[:S], w["mask"]), (m8[S:], w["mask"])]
        if rope:
            tab, wrow = m.sb("tab", [D, 4, HD]), m.sb("wrow", [D, 4, HD])
            qk, qs, qc = (m.sb(n, [D, 2, NT * H, HD]) for n in ("qk", "qs", "qc"))
            ssq, rr = m.sb("ssq", [D, 2, NT * H]), m.sb("rr", [D, 2, NT * H])
            loads += [(tab[:], c["rope"])]
            for k, v in enumerate(w["norm"]):
                loads += [(wrow[:, 2 * k], v.broadcast_to([D, HD]))]
                loads += [(wrow[:, 2 * k + 1, a:a + HD // 2], v[:, HD // 2 - a:HD - a].broadcast_to([D, HD // 2])) for a in (0, HD // 2)]
        if combined:
            prob = m.sb("prob", [D, TOKENS // D])
            y, x_raw = m.sb("y", [D, NT, D]), m.sb("x_raw", [D, NT, D])
            loads += [(prob[:], combined[1])]
            xc = m.sb("xc", [D, NT, D]) if rope else None
            y_in, y_used = m.sem("y_in"), m.sem("y_used")
        LOADS = 16 * len(loads)

        weights_in, pool_consts, dve_consts, dve_ready = (m.sem(n) for n in ("weights_in", "pool_consts", "dve_consts", "dve_ready"))
        x_loaded = [m.sem(f"x_loaded{p}") for p in range(2)]
        c_loaded, saved = m.sem("c_loaded"), m.sem("saved")
        s = {k: m.sem(k) for k in (
            "stats_done parts_done mean_done power_done rstd_done norm_done turned_x turned_c xT_done cT_done twice_done "
            "q_mm k_mm q_done k_done own_k_mm own_k_done v_mm v_done masked scores_mm kept negated max_done shifted exp_done "
            "turned_e pt_done pv_mm rden_done normed fin_turned aT_done fin_mm fin_added new_done "
            "res_done q_sq k_sq ssq_done ssqeps_done sqrt_done rr_done qk_scaled swapped cosed roped turned_q turned_k").split()}
        block = ctx.enter_context(nc.Block())
        LAST = GROUPS - 1
        V_STEPS = [(src, half) for half in range(2) for src in range(NS)]

        def at(j, p, b):
            return (j, p, b) if b < B else (j + 1, 1 - p, b - B)

        def schedule(eng, slot):
            for p in range(2):
                for b in range(B):
                    slot(p, p, b, True)
            with eng.Fori(1, GROUPS // 2 - 1) as i:
                for p in range(2):
                    for b in range(B):
                        slot(i * 2 + p, p, b, True)
            for p in range(2):
                for b in range(B):
                    slot(LAST - 1 + p, p, b, p == 0)

        @block.sync
        def _(sp):
            for dst, src in loads:
                sp.dma_start(dst, src).then_inc(weights_in, 16)

            def load(j, p):
                sp.dma_start(x_raw[:] if combined else x_res[:, p], rows(x_in, j * GROUP)).then_inc(x_loaded[p], 16)
                if combined:
                    sp.dma_start(y[:], rows(combined[0], j * GROUP)).then_inc(y_in, 16)
                if not at_start(j):
                    sp.wait_ge(s["turned_c"], j)
                sp.dma_start(c_raw[:], rows(ctx_in, j * GROUP)).then_inc(c_loaded, 16)

            def store(j):
                sp.wait_ge(s["new_done"], j + 1)
                sp.dma_start(rows(x_out, j * GROUP), x_new[:]).then_inc(saved, 16)

            load(0, 0)

            def slot(j, p, b, more):
                if b == 0 and more and combined:
                    sp.wait_ge(y_used, j + 1)
                    load(j + 1, 1 - p)
                if b == 1 and project and not at_start(j):
                    store(j - 1)
                if b == 1 and more and not combined:
                    load(j + 1, 1 - p)
                if b == B - 1 and not project:
                    store(j)

            schedule(sp, slot)
            if project:
                store(LAST)
            sp.wait_ge(saved, 16 * GROUPS)

        @block.gpsimd
        def _(pool):
            nc.gpsimd.memset(minus_half[:], -0.5).then_inc(pool_consts, 1)
            nc.gpsimd.memset(qg[:], 0.0).then_inc(pool_consts, 1)
            nc.gpsimd.memset(vx[:], 0.0).then_inc(pool_consts, 1)
            pool.wait_ge(pool_consts, 3)
            for a in range(2):
                nc.gpsimd.memset(vx[a * S:a * S + S, :, :, :, :, a, HD:].rearrange("p x s b n o -> p (x s b n) o"), 1.0).then_inc(pool_consts, 1)
            pool.wait_ge(weights_in, LOADS)
            pool.wait_ge(pool_consts, 5)

            def rstd_of(j):
                pool.wait_ge(s["power_done"], j + 1)
                nc.gpsimd.tensor_tensor(rstd[:], power[:], minus_half[:], ALU.pow).then_inc(s["rstd_done"], 1)

            def cosines(j):
                if rope:
                    pool.wait_ge(s["qk_scaled"], j + 1)
                    for k in range(2):
                        last = nc.gpsimd.tensor_tensor(qc[:, k], qk[:, k], tab[:, 2 * k].unsqueeze(1).broadcast_to([D, NT * H, HD]), ALU.mult)
                    last.then_inc(s["cosed"], 1)

            def mask(j, p, b):
                n = j * B + b
                pool.wait_ge(s["own_k_done" if own_keys else "k_done"], j + 1)
                if not isinstance(n, int) or n > 1:
                    pool.wait_ge(s["scores_mm"], n - 1)
                for src in range(NS):
                    last = nc.gpsimd.tensor_tensor(kn[:, b % 2, src], kT[:, p, src, b * S:(b + 1) * S].unsqueeze(1).broadcast_to([D, 8, S]),
                                                   n_mask[:].unsqueeze(2).broadcast_to([D, 8, S]), ALU.mult)
                last.then_inc(s["masked"], 1)

            def negate(j, p, b):
                if layer == 2:
                    pool.wait_ge(s["kept"], j * B + b + 1)
                    nc.gpsimd.tensor_tensor(e[:, b % RING, 0], e[:, b % RING, 0], neg[:].unsqueeze(1).broadcast_to([D, 8, S]), ALU.add).then_inc(s["negated"], 1)

            rstd_of(0)
            cosines(0)
            mask(0, 0, 0)
            if layer == 2:
                pool.wait_ge(dve_ready, 1)
            for b in range(LEAD):
                mask(0, 0, b + 1)
                negate(0, 0, b)

            def slot(j, p, b, more):
                if more or b + LEAD + 1 < B:
                    mask(*at(j, p, b + LEAD + 1))
                if more and b == TURN + 2:
                    cosines(j + 1)
                if more and b == TURN - 1:
                    rstd_of(j + 1)
                if more or b + LEAD < B:
                    negate(*at(j, p, b + LEAD))

            schedule(pool, slot)

        @block.scalar
        def _(act):
            act.wait_ge(weights_in, LOADS)
            act.wait_ge(dve_consts, 1)

            def turned(j):
                act.wait_ge(s["turned_x"], j + 1)
                nc.scalar.activation(xT[:], front[:, 0], ACT.Copy).then_inc(s["xT_done"], 1)
                act.wait_ge(s["turned_c"], j + 1)
                nc.scalar.activation(cT[:], front[:, 1], ACT.Copy).then_inc(s["cT_done"], 1)

            def double(j):
                for n, one in enumerate((cT, xT)[:NS]):
                    act.wait_ge(s[("cT_done", "xT_done")[n]], j + 1)
                    last = nc.scalar.activation(twice[n][:], one[:].rearrange("p (b k) -> p b k", b=B).unsqueeze(2).broadcast_to([D, B, 2, S]), ACT.Copy)
                last.then_inc(s["twice_done"], 1)

            def keys(j, p):
                act.wait_ge(s["turned_k" if rope else "k_mm"], j + 1)
                if rope:
                    nc.scalar.activation(kT[:, p, 0], front[:, 1], ACT.Copy).then_inc(s["k_done"], 1)
                else:
                    nc.scalar.activation(kT[:, p, 0], front[:, 1], ACT.Identity, bias=bk[:]).then_inc(s["k_done"], 1)

            def queries(j, p):
                act.wait_ge(s["turned_q" if rope else "q_mm"], j + 1)
                for g in range(2):
                    f = slice(g * S, g * S + S)
                    src = front[f, 0].rearrange("p (b q) -> p b q", b=B)
                    if rope:
                        last = nc.scalar.activation(qg[f, p, :, g], src, ACT.Copy)
                    else:
                        last = nc.scalar.activation(qg[f, p, :, g], src, ACT.Identity, scale=SCALE, bias=bq[f])
                last.then_inc(s["q_done"], 1)

            def keys_queries(j, p):
                if rope:
                    keys(j, p)
                queries(j, p)
                if not rope:
                    keys(j, p)
                if own_keys:
                    act.wait_ge(s["own_k_mm"], j + 1)
                    nc.scalar.activation(kT[:, p, 1], front[:, 0], ACT.Identity, bias=bk[:]).then_inc(s["own_k_done"], 1)

            def squares(j):
                act.wait_ge(s["q_mm"], j + 1)
                nc.scalar.activation(qs[:, 0].rearrange("p n d -> p (n d)"), front[:, 0], ACT.Square).then_inc(s["q_sq"], 1)
                act.wait_ge(s["k_mm"], j + 1)
                nc.scalar.activation(qs[:, 1].rearrange("p n d -> p (n d)"), front[:, 1], ACT.Square).then_inc(s["k_sq"], 1)

            def roots(j):
                act.wait_ge(s["ssqeps_done"], j + 1)
                nc.scalar.activation(rr[:], ssq[:], ACT.Sqrt).then_inc(s["sqrt_done"], 1)

            def exps(j, p, b):
                act.wait_ge(s["shifted"], j * B + b + 1)
                nc.scalar.activation(e[:, b % RING], e[:, b % RING], ACT.Exp).then_inc(s["exp_done"], 1)

            def residual(j, p):
                act.wait_ge(y_used, j + 1)
                if not isinstance(j, int) or j > 1:
                    act.wait_ge(s["new_done"], j - 1)
                nc.scalar.activation(x_res[:, p], xc[:], ACT.Copy).then_inc(s["res_done"], 1)

            def finish(j):
                act.wait_ge(s["fin_turned"], j + 1)
                nc.scalar.activation(aT[:], front[:, 0], ACT.Copy).then_inc(s["aT_done"], 1)

            turned(0)
            if rope:
                residual(0, 0)
                squares(0)
                double(0)
                roots(0)
                keys_queries(0, 0)
            else:
                keys_queries(0, 0)
                double(0)
            for b in range(AHEAD):
                exps(0, 0, b)

            def slot(j, p, b, more):
                n = j * B + b
                for src in range(NS):
                    act.wait_ge(s["turned_e"], n * NS + src + 1)
                    nc.scalar.activation(pt[:, b % 2, src].rearrange("p m q -> p (m q)"), turn[:, src], ACT.Copy).then_inc(s["pt_done"], 1)
                if more and b == TURN:
                    turned(j + 1)
                if more and rope and b == TURN + 1:
                    roots(j + 1)
                if more or b + AHEAD < B:
                    exps(*at(j, p, b + AHEAD))
                if more and b == TURN:
                    if rope:
                        squares(j + 1)
                        residual(j + 1, 1 - p)
                    else:
                        keys_queries(j + 1, 1 - p)
                    double(j + 1)
                if more and rope and b == ROPE:
                    keys_queries(j + 1, 1 - p)
                if b == 0 and project and not at_start(j):
                    finish(j - 1)

            schedule(act, slot)
            if project:
                finish(LAST)

        @block.vector
        def _(dve):
            dve.wait_ge(weights_in, LOADS)
            if rope:
                nc.vector.tensor_tensor(tab[:], tab[:], wrow[:], ALU.mult).then_inc(dve_consts, 1)
            elif layer == 2:
                nc.vector.tensor_scalar(bq[:], bq[:], SCALE, None, ALU.mult).then_inc(dve_consts, 1)
                dve.wait_ge(dve_consts, 1)
                nc.vector.tensor_scalar(keep[:], m8[:].bitcast(U8), -1.0, 1.0, ALU.mult, ALU.add)
                nc.vector.tensor_scalar(neg[:], m8[:].bitcast(U8), -1e9, None, ALU.mult).then_inc(dve_ready, 1)
                dve.wait_ge(dve_ready, 1)
            else:
                nc.vector.tensor_scalar(bq[:], bq[:], SCALE, None, ALU.mult).then_inc(dve_consts, 1)
            dve.wait_ge(dve_consts, 1)
            dve.wait_ge(pool_consts, 5)

            def mean_variance(j, p):
                x = xc[:] if rope else x_res[:, p]
                dve.wait_ge(x_loaded[p], 16 * ((j - p) // 2 + 1) if isinstance(j, int) else 8 * (j - p) + 16)
                if combined:
                    dve.wait_ge(y_in, 16 * (j + 1))
                    if rope and not at_start(j):
                        dve.wait_ge(s["res_done"], j)
                    elif not rope and (not isinstance(j, int) or j > 1):
                        dve.wait_ge(s["new_done"], j - 1)
                    for t in range(NT):
                        last = nc.vector.scalar_tensor_tensor(x[:, t], y[:, t], prob[:, bass.ds(j * NT + t, 1)], x_raw[:, t], ALU.mult, ALU.add)
                    last.then_inc(y_used, 1)
                    dve.wait_ge(y_used, j + 1)
                moments(nc, dve, x, NT, stats, parts, mean[:], power[:], s, j + 1)

            def norm(j, p):
                x = xc[:] if rope else x_res[:, p]
                dve.wait_ge(s["rstd_done"], j + 1)
                for t in range(NT):
                    last = nc.vector.tensor_scalar(xn[:, t], x[:, t], mean[:, t:t + 1], rstd[:, t:t + 1], ALU.subtract, ALU.mult)
                last.then_inc(s["norm_done"], 1)

            def values(j, p, steps):
                for n in steps:
                    src, half = V_STEPS[n]
                    bank = front[:, n % 2].rearrange("p (b n a d) -> p b n a d", b=4, a=2, d=HD)
                    dve.wait_ge(s["v_mm"], j * len(V_STEPS) + n + 1)
                    for a in range(2):
                        f = slice(a * S, a * S + S)
                        for_heads = vx[f, p, src, half * 4:half * 4 + 4, :, a, :HD]
                        if rope:
                            last = nc.vector.tensor_copy(for_heads, bank[f, :, :, a])
                        else:
                            bias = bv[f].rearrange("p (n a d) -> p n a d", a=2, d=HD)[:, :, a].unsqueeze(1).broadcast_to([S, 4, 8, HD])
                            last = nc.vector.tensor_tensor(for_heads, bank[f, :, :, a], bias, ALU.add)
                    last.then_inc(s["v_done"], 1)

            def rms(j):
                dve.wait_ge(s["q_sq"], j + 1)
                dve.wait_ge(s["k_sq"], j + 1)
                nc.vector.tensor_reduce(ssq[:], qs[:], AX.X, ALU.add).then_inc(s["ssq_done"], 1)
                dve.wait_ge(s["ssq_done"], j + 1)
                nc.vector.tensor_scalar(ssq[:], ssq[:], 1.0 / HD, RMS_EPS, ALU.mult, ALU.add).then_inc(s["ssqeps_done"], 1)

            def scale(j):
                dve.wait_ge(s["sqrt_done"], j + 1)
                nc.vector.reciprocal(rr[:], rr[:]).then_inc(s["rr_done"], 1)
                dve.wait_ge(s["rr_done"], j + 1)
                for k in range(2):
                    last = nc.vector.tensor_tensor(qk[:, k], front[:, k].rearrange("p (n d) -> p n d", d=HD),
                                                   rr[:, k].unsqueeze(2).broadcast_to([D, NT * H, HD]), ALU.mult)
                last.then_inc(s["qk_scaled"], 1)
                dve.wait_ge(s["qk_scaled"], j + 1)
                half = HD // 2
                for k in range(2):
                    for lo, hi in ((0, half), (half, 0)):
                        last = nc.vector.tensor_tensor(qs[:, k, :, lo:lo + half], qk[:, k, :, hi:hi + half],
                                                       tab[:, 2 * k + 1, lo:lo + half].unsqueeze(1).broadcast_to([D, NT * H, half]), ALU.mult)
                last.then_inc(s["swapped"], 1)

            def turn_rope(j):
                dve.wait_ge(s["swapped"], j + 1)
                dve.wait_ge(s["cosed"], j + 1)
                nc.vector.tensor_tensor(qk[:], qc[:], qs[:], ALU.add).then_inc(s["roped"], 1)

            def after_row(j, p, b):
                if b == TURN - 2:
                    mean_variance(j, p)
                if b == TURN - 1:
                    norm(j, p)
                if rope and b == TURN:
                    rms(j)
                if rope and b == TURN + 1:
                    scale(j)
                if rope and b == TURN + 2:
                    turn_rope(j)
                if b == VALUES:
                    values(j, p, range(0, NS))
                if b == VALUES + 1:
                    values(j, p, range(NS, 2 * NS))

            def keep_scores(j, p, b):
                n = j * B + b
                dve.wait_ge(s["scores_mm"], n + 1)
                nc.vector.tensor_tensor(e[:, b % RING, 0], sc[:, b % AHEAD, 0].rearrange("p (n k) -> p n k", n=8),
                                        keep[:].unsqueeze(1).broadcast_to([D, 8, S]), ALU.mult).then_inc(s["kept"], 1)

            def softmax(j, p, b):
                n = j * B + b
                r = b % RING
                if layer == 2:
                    dve.wait_ge(s["negated"], n + 1)
                    src = e[:, r, 0]
                    nc.vector.tensor_reduce(mx[:, b % 2], src, AX.X, ALU.max).then_inc(s["max_done"], 1)
                elif NS == 1:
                    dve.wait_ge(s["scores_mm"], n + 1)
                    src = sc[:, b % AHEAD, 0].rearrange("p (n k) -> p n k", n=8)
                    nc.vector.tensor_reduce(mx[:, b % 2], src, AX.X, ALU.max).then_inc(s["max_done"], 1)
                else:
                    dve.wait_ge(s["scores_mm"], n + 1)
                    src = sc[:, b % AHEAD].rearrange("p s (n k) -> p s n k", n=8)
                    nc.vector.tensor_reduce(mx[:, b % 2], src.rearrange("p s n k -> p n s k"), AX.XY, ALU.max).then_inc(s["max_done"], 1)
                dve.wait_ge(s["max_done"], n + 1)
                if NS == 1:
                    nc.vector.tensor_tensor(e[:, r, 0], src, mx[:, b % 2].unsqueeze(2).broadcast_to([D, 8, S]), ALU.subtract).then_inc(s["shifted"], 1)
                else:
                    nc.vector.tensor_tensor(e[:, r], src, mx[:, b % 2].unsqueeze(1).unsqueeze(3).broadcast_to([D, NS, 8, S]), ALU.subtract).then_inc(s["shifted"], 1)

            def finish(j, p):
                dve.wait_ge(s["fin_mm"], j + 1)
                if rope:
                    dve.wait_ge(s["res_done"], j + 1)
                if not isinstance(j, int) or j:
                    dve.wait_ge(saved, 16 * j)
                res = x_res[:, p].rearrange("p t f -> p (t f)")
                new = x_new[:].rearrange("p t f -> p (t f)")
                if layer == 2:
                    nc.vector.tensor_tensor(new, front[:, 1], res, ALU.add).then_inc(s["fin_added"], 1)
                    dve.wait_ge(s["fin_added"], j + 1)
                    nc.vector.tensor_tensor(x_new[:], x_new[:], bo[:].unsqueeze(1).broadcast_to([D, NT, D]), ALU.add).then_inc(s["new_done"], 1)
                else:
                    nc.vector.tensor_tensor(new, front[:, 1], res, ALU.add).then_inc(s["new_done"], 1)

            for b in range(B):
                after_row(0, 0, b)
            if layer == 2:
                for b in range(LEAD):
                    keep_scores(0, 0, b)
            for b in range(AHEAD):
                softmax(0, 0, b)

            def slot(j, p, b, more):
                n = j * B + b
                if b == 1 and layer == 2 and not at_start(j):
                    finish(j - 1, 1 - p)
                if layer == 2 and (more or b + LEAD < B):
                    keep_scores(*at(j, p, b + LEAD))
                if more or b + AHEAD < B:
                    softmax(*at(j, p, b + AHEAD))
                if b == 1 and rope and not at_start(j):
                    finish(j - 1, 1 - p)
                dve.wait_ge(s["pv_mm"], n + 1)
                sums = pv[:, b % 2, :2 * 8 * (HD + 1)].rearrange("p (n d) -> p n d", d=HD + 1)
                nc.vector.reciprocal(rden[:, b % 2], sums[:, :, HD]).then_inc(s["rden_done"], 1)
                dve.wait_ge(s["rden_done"], n + 1)
                out = slice((b % 2) * S, (b % 2) * S + S)
                for g in range(2):
                    f = slice(g * S, g * S + S)
                    last = nc.vector.tensor_tensor(attn[out, p, b // 2, g * S:(g + 1) * S].rearrange("p (n d) -> p n d", d=HD),
                                                   sums[f, g * 8:(g + 1) * 8, :HD], rden[f, b % 2, g * 8:(g + 1) * 8].unsqueeze(2).broadcast_to([S, 8, HD]), ALU.mult)
                last.then_inc(s["normed"], 1)
                if more:
                    after_row(j + 1, 1 - p, b)
                if b == B - 1 and not project:
                    if not at_start(j):
                        dve.wait_ge(saved, 16 * j)
                    dve.wait_ge(s["normed"], (j + 1) * B)
                    nc.vector.tensor_tensor(x_new[:], attn[:, p], x_res[:, p], ALU.add).then_inc(s["new_done"], 1)

            schedule(dve, slot)
            if project:
                finish(LAST, 1)

        @block.tensor
        def _(pe):
            pe.wait_ge(weights_in, LOADS)
            pe.wait_ge(pool_consts, 5)

            def turn_inputs(j):
                pe.wait_ge(s["norm_done"], j + 1)
                if not at_start(j):
                    pe.wait_ge(s["v_done"], j * len(V_STEPS))
                if project and (not isinstance(j, int) or j > 1):
                    pe.wait_ge(s["new_done"], j - 1)
                for t in range(NT):
                    last = nc.tensor.transpose(front[:, 0, t * D:(t + 1) * D], xn[:, t], ident[:])
                last.then_inc(s["turned_x"], 1)
                pe.wait_ge(c_loaded, 16 * (j + 1))
                for t in range(NT):
                    last = nc.tensor.transpose(front[:, 1, t * D:(t + 1) * D], c_raw[:, t], ident[:])
                last.then_inc(s["turned_c"], 1)

            def keys_queries(j):
                if rope:
                    for (mm, done), a, wt, k in ((("q_mm", "xT_done"), xT, wq, 0), (("k_mm", "cT_done"), cT, wk, 1)):
                        pe.wait_ge(s[done], j + 1)
                        for t in range(NT):
                            last = nc.tensor.matmul(front[:, k, t * D:(t + 1) * D], a[:, t * D:(t + 1) * D], wt[:], start=True, stop=True)
                        last.then_inc(s[mm], 1)
                else:
                    pe.wait_ge(s["xT_done"], j + 1)
                    nc.tensor.matmul(front[:, 0], wq[:], xT[:], start=True, stop=True).then_inc(s["q_mm"], 1)
                    pe.wait_ge(s["cT_done"], j + 1)
                    nc.tensor.matmul(front[:, 1], wk[:], cT[:], start=True, stop=True).then_inc(s["k_mm"], 1)

            def own_keys_mm(j):
                pe.wait_ge(s["q_done"], j + 1)
                nc.tensor.matmul(front[:, 0], wk[:], xT[:], start=True, stop=True).then_inc(s["own_k_mm"], 1)

            def turn_roped(j):
                pe.wait_ge(s["roped"], j + 1)
                for k, name in ((1, "turned_k"), (0, "turned_q")):
                    for t in range(NT):
                        last = nc.tensor.transpose(front[:, k, t * D:(t + 1) * D], qk[:, k, t * H:(t + 1) * H].rearrange("p n d -> p (n d)"), ident[:])
                    last.then_inc(s[name], 1)

            def values(j, steps):
                for n in steps:
                    src, half = V_STEPS[n]
                    if n < 2:
                        pe.wait_ge(s["twice_done"], j + 1)
                        pe.wait_ge(s["q_done"], j + 1)
                        pe.wait_ge(s["own_k_done" if own_keys and n == 0 else "k_done"], j + 1)
                    else:
                        pe.wait_ge(s["v_done"], j * len(V_STEPS) + n - 1)
                    for b in range(4):
                        feats = twice[src][:, half * 4 + b].rearrange("p a k -> p (a k)")
                        last = nc.tensor.matmul(front[:, n % 2, b * D:(b + 1) * D], feats, wv[:], start=True, stop=True)
                    last.then_inc(s["v_mm"], 1)

            def scores(j, p, b):
                n = j * B + b
                pe.wait_ge(s["q_done"], j + 1)
                pe.wait_ge(s["masked"], n + 1)
                if not isinstance(n, int) or n >= AHEAD:
                    pe.wait_ge(s["kept" if layer == 2 else "shifted"], n - AHEAD + 1)
                for src in range(NS):
                    last = nc.tensor.matmul(sc[:, b % AHEAD, src], qg[:, p, b].rearrange("p g q -> p (g q)"),
                                            kn[:, b % 2, src].rearrange("p n k -> p (n k)"), start=True, stop=True)
                last.then_inc(s["scores_mm"], 1)

            turn_inputs(0)
            keys_queries(0)
            if own_keys:
                own_keys_mm(0)
            if rope:
                turn_roped(0)
            values(0, range(0, NS))
            values(0, range(NS, 2 * NS))
            for b in range(LEAD):
                scores(0, 0, b)

            def turn_attn(j, p):
                pe.wait_ge(s["normed"], (j + 1) * B)
                for t in range(NT):
                    last = nc.tensor.transpose(front[:, 0, t * D:(t + 1) * D], attn[:, p, t], ident[:])
                last.then_inc(s["fin_turned"], 1)

            def finish(j):
                pe.wait_ge(s["aT_done"], j + 1)
                for t in range(NT):
                    last = nc.tensor.matmul(front[:, 1, t * D:(t + 1) * D], aT[:, t * D:(t + 1) * D], wo[:], start=True, stop=True)
                last.then_inc(s["fin_mm"], 1)

            def slot(j, p, b, more):
                n = j * B + b
                pe.wait_ge(s["exp_done"], n + 1)
                for src in range(NS):
                    if not at_start(n):
                        pe.wait_ge(s["pt_done"], n * NS)
                    for k in range(4):
                        last = nc.tensor.transpose(turn[:, src, k * D:(k + 1) * D], e[:, b % RING, src, 2 * k:2 * k + 2].rearrange("p n k -> p (n k)"), ident[:])
                    last.then_inc(s["turned_e"], 1)
                if not own_keys and (more or b + LEAD < B):
                    scores(*at(j, p, b + LEAD))
                if more and b == TURN:
                    turn_inputs(j + 1)
                if b == 0:
                    pe.wait_ge(s["v_done"], (j + 1) * len(V_STEPS))
                    if project and not at_start(j):
                        turn_attn(j - 1, 1 - p)
                if more and rope and b == ROPE:
                    turn_roped(j + 1)
                if not isinstance(n, int) or n > 1:
                    pe.wait_ge(s["normed"], n - 1)
                out = pv[:, b % 2, :144].rearrange("p (g m x) -> p g m x", g=2, m=4)
                for src in range(NS):
                    pe.wait_ge(s["pt_done"], n * NS + src + 1)
                    for k in range(4):
                        values_of = vx[:, p, src, b].rearrange("p (g m) a d -> p g m (a d)", g=2)[:, :, k]
                        last = nc.tensor.matmul(out[:, :, k], pt[:, b % 2, src, k], values_of, start=(src == 0 and k == 0), stop=(src == NS - 1), skip_group_check=True)
                last.then_inc(s["pv_mm"], 1)
                if more and b == TURN:
                    keys_queries(j + 1)
                if own_keys and (more or b + LEAD < B):
                    scores(*at(j, p, b + LEAD))
                if more and own_keys and b == TURN:
                    own_keys_mm(j + 1)
                if more and b in (VALUES, VALUES + 1):
                    values(j + 1, range((b - VALUES) * NS, (b - VALUES + 1) * NS))
                if b == 0 and project and not at_start(j):
                    finish(j - 1)

            schedule(pe, slot)
            if project:
                turn_attn(LAST, 1)
                finish(LAST)


E4 = 4


def layernorm_experts(nc, c, ph, x_in, w, x_out):
    U = 2
    with ExitStack() as ctx:
        m = Space(nc, ctx, ph)
        ident, ones = m.sb("ident", [D, D]), m.sb("ones", [D, D])
        gw, gb, falling = m.sb("gw", [D, E4]), m.sb("gb", [D, E4]), m.sb("falling", [D, E4])
        w1, w2 = m.sb("w1", [D, E4, D]), m.sb("w2", [D, E4, D])
        b1, g1, be1 = (m.sb(n, [D, E4]) for n in ("b1", "g1", "be1"))
        b2, g2, be2 = m.sb("b2", [D, E4, D]), m.sb("g2", [D, E4, D]), m.sb("be2", [E4, D])
        wmean = m.sb("wmean", [D, 4, E4])
        minus_half, euler = m.sb("minus_half", [D, NT]), m.sb("euler", [D, NT])
        x, xn, xT = m.sb("x", [D, U, NT, D]), m.sb("xn", [D, U, NT, D]), m.sb("xT", [D, U, GROUP])
        stats, parts = m.sb("stats", [D, U, NT, 6]), m.sb("parts", [D, U, 3, NT])
        mean, power, rstd = (m.sb(n, [D, U, NT]) for n in ("mean", "power", "rstd"))
        score, eq, hot1, hot2, left = (m.sb(n, [D, U, NT, E4]) for n in ("score", "eq", "hot1", "hot2", "left"))
        share = m.sb("share", [D, 2, U, NT, E4])
        top1, top2, pick, ratio, w_first, w_second = (m.sb(n, [D, U, NT]) for n in ("top1", "top2", "pick", "ratio", "w_first", "w_second"))
        hb, sq, hid = (m.sb(n, [D, U, E4, GROUP]) for n in ("hb", "sq", "hid"))
        root, inv, diag = m.sb("root", [D, U, E4, NT]), m.sb("inv", [D, U, E4, NT]), m.sb("diag", [D, U, E4, NT, D])
        y, ysq = m.sb("y", [D, U, NT, E4, D]), m.sb("ysq", [D, U, E4 * D])
        ssq = m.sb("ssq", [D, U, NT, E4])
        shareT = m.sb("shareT", [E4, U, GROUP])
        mixed, x_new = (m.sb(n, [D, U, NT, D]) for n in ("mixed", "x_new"))
        x_sum = m.sb("x_sum", [D, 2, U, NT, D])
        ln_eps = m.sb("ln_eps", [D, 1])
        bank = m.psum("bank", [D, U, 4, GROUP])

        loads = [(ident[:], c["ident"]), (ones[:], c["ones"]), (gw[:], w["gate_W"]), (gb[:], w["gate_b"].broadcast_to([D, E4])),
                 (falling[:], c["falling"][:, :E4]), (b1[:], w["b1T"]), (g1[:], w["g1T"]), (be1[:], w["be1T"]), (be2[:], w["be2"]),
                 (w1[:], w["W1"].rearrange("(e p) f -> p e f", e=E4)), (w2[:], w["W2"].rearrange("(e p) f -> p e f", e=E4)),
                 (b2[:].rearrange("p e f -> p (e f)"), w["b2"].broadcast_to([D, E4 * D])),
                 (g2[:].rearrange("p e f -> p (e f)"), w["g2"].broadcast_to([D, E4 * D]))]
        LOADS = 16 * len(loads)
        weights_in, pool_consts, mean_steps, b1_mm = (m.sem(n) for n in ("weights_in", "pool_consts", "mean_steps", "b1_mm"))
        x_loaded = [m.sem(f"x_loaded{u}") for u in range(U)]
        saved = [m.sem(f"saved{u}") for u in range(U)]
        s = {k: m.sem(k) for k in (
            "stats_done parts_done mean_done power_done rstd_done norm_done turned xT_done logits_mm score_done top1_done eq1_done "
            "eqw1_done pick1_done hot1_done left_done top2_done eq2_done eqw2_done pick2_done hot2_done diff_done ratio_done "
            "den_done first_done second_done share1_done share_done hid_mm sq_done var_mm root_done inv_done diag_done row_mm scaled_done hid_done "
            "y_mm y_done ysq_done ssq_done var2_done std2_done inv2_done factor_done weighed gained mixed_done share_turned "
            "shareT_done offset_mm sum_done sum2_done new_done").split()}
        block = ctx.enter_context(nc.Block())
        STEPS = GROUPS // U
        VAR = 64

        def nth(i, a, u):
            return i * (E4 * U) + a * U + u + 1

        def schedule(eng, hidden, gate, tail):
            def turn(i, last=False):
                for q in range(2):
                    step = i * 2 + q
                    more = not (last and q)
                    hidden(step, q, more)
                    if more:
                        gate(step + 1, 1 - q)
                    tail(step, q, more)

            turns(eng, STEPS // 2, turn, True)

        @block.sync
        def _(sp):
            for u in range(U):
                sp.dma_start(x[:, u], rows(x_in, u * GROUP)).then_inc(x_loaded[u], 16)
            for dst, src in loads:
                sp.dma_start(dst, src).then_inc(weights_in, 16)

            def load(i):
                for u in range(U):
                    sp.wait_ge(s["sum_done"], (i - 1) * U + u + 1)
                    sp.dma_start(x[:, u], rows(x_in, i * U * GROUP + u * GROUP)).then_inc(x_loaded[u], 16)

            def store(i):
                for u in range(U):
                    sp.wait_ge(s["new_done"], i * U + u + 1)
                    sp.dma_start(rows(x_out, i * U * GROUP + u * GROUP), x_new[:, u]).then_inc(saved[u], 16)

            def hidden(i, q, more):
                if not at_start(i):
                    store(i - 1)

            def gate(i, q):
                if not isinstance(i, int) or i < STEPS - 1:
                    load(i + 1)

            def tail(i, q, more):
                pass

            load(1)
            schedule(sp, hidden, gate, tail)
            store(STEPS - 1)
            for u in range(U):
                sp.wait_ge(saved[u], 16 * STEPS)

        @block.gpsimd
        def _(pool):
            nc.gpsimd.memset(minus_half[:], -0.5).then_inc(pool_consts, 1)
            nc.gpsimd.memset(euler[:], float(np.e)).then_inc(pool_consts, 1)
            pool.wait_ge(pool_consts, 2)
            pool.wait_ge(weights_in, LOADS)

            def roots(i):
                for u in range(U):
                    pool.wait_ge(s["power_done"], i * U + u + 1)
                    nc.gpsimd.tensor_tensor(rstd[:, u], power[:, u], minus_half[:], ALU.pow).then_inc(s["rstd_done"], 1)

            def gains(i):
                for u in range(U):
                    for t in range(NT):
                        pool.wait_ge(s["weighed"], (i * U + u) * NT + t + 1)
                        nc.gpsimd.tensor_tensor(y[:, u, t], y[:, u, t], g2[:], ALU.mult).then_inc(s["gained"], 1)

            def hidden(i, q, more):
                if more:
                    roots(i + 1)
                if not at_start(i):
                    gains(i - 1)
                for e in range(E4):
                    for u in range(U):
                        pool.wait_ge(s["inv_done"], i * U + u + 1)
                        if not at_start(i):
                            pool.wait_ge(s["row_mm"], nth(i - 1, e, u))
                        nc.gpsimd.tensor_tensor(diag[:, u, e], ident[:].unsqueeze(1).broadcast_to([D, NT, D]),
                                                inv[:, u, e].unsqueeze(2).broadcast_to([D, NT, D]), ALU.mult).then_inc(s["diag_done"], 1)

            def gate(i, q):
                for u in range(U):
                    pool.wait_ge(s["diff_done"], i * U + u + 1)
                    nc.gpsimd.tensor_tensor(ratio[:, u], euler[:], ratio[:, u], ALU.pow).then_inc(s["ratio_done"], 1)

            def tail(i, q, more):
                pass

            roots(0)
            gate(0, 0)
            schedule(pool, hidden, gate, tail)
            gains(STEPS - 1)

        @block.scalar
        def _(act):
            act.wait_ge(mean_steps, 4)

            def gate(i, q):
                for u in range(U):
                    act.wait_ge(s["turned"], i * U + u + 1)
                    nc.scalar.activation(xT[:, u], bank[:, u, 0], ACT.Copy).then_inc(s["xT_done"], 1)

            def weigh(i, n):
                u, t = n // NT, n % NT
                act.wait_ge(s["factor_done"], i * U + u + 1)
                for e in range(E4):
                    last = nc.scalar.activation(y[:, u, t, e], y[:, u, t, e], ACT.Copy, scale=ssq[:, u, t, e:e + 1])
                last.then_inc(s["weighed"], 1)

            def hidden(i, q, more):
                for e in range(E4):
                    for u in range(U):
                        act.wait_ge(s["hid_mm"], nth(i, e, u))
                        nc.scalar.activation(hb[:, u, e], bank[:, u, 2 + e % 2], ACT.Identity, bias=b1[:, e:e + 1])
                        nc.scalar.activation(sq[:, u, e], bank[:, u, 2 + e % 2], ACT.Square, bias=b1[:, e:e + 1]).then_inc(s["sq_done"], 1)
                        if not at_start(i):
                            weigh(i - 1, e * U + u)
                for u in range(U):
                    act.wait_ge(s["var_mm"], nth(i, E4 - 1, u))
                    nc.scalar.activation(root[:, u].rearrange("p e t -> p (e t)"), bank[:, u, 1, VAR:VAR + E4 * NT], ACT.Sqrt, scale=1.0 / D, bias=ln_eps[:]).then_inc(s["root_done"], 1)
                for e in range(E4):
                    for u in range(U):
                        act.wait_ge(s["scaled_done"], nth(i, e, u))
                        nc.scalar.activation(hid[:, u, e], sq[:, u, e], ACT.Relu, scale=g1[:, e:e + 1], bias=be1[:, e:e + 1]).then_inc(s["hid_done"], 1)

            def tail(i, q, more):
                for t in range(NT):
                    for u in range(U):
                        act.wait_ge(s["y_done"], nth(i, t, u))
                        if t or not at_start(i):
                            act.wait_ge(s["ssq_done"], nth(i, t, u) - U)
                        nc.scalar.activation(ysq[:, u], y[:, u, t].rearrange("p e f -> p (e f)"), ACT.Square).then_inc(s["ysq_done"], 1)
                for u in range(U):
                    act.wait_ge(s["share_turned"], i * U + u + 1)
                    nc.scalar.activation(shareT[:, u], bank[:E4, u, 1], ACT.Copy).then_inc(s["shareT_done"], 1)
                for u in range(U):
                    act.wait_ge(s["var2_done"], i * U + u + 1)
                    nc.scalar.activation(ssq[:, u], ssq[:, u], ACT.Sqrt).then_inc(s["std2_done"], 1)

            gate(0, 0)
            schedule(act, hidden, gate, tail)
            for n in range(U * NT):
                weigh(STEPS - 1, n)

        @block.vector
        def _(dve):
            dve.wait_ge(weights_in, LOADS)
            dve.wait_ge(pool_consts, 2)
            nc.vector.memset(ln_eps[:], LN_EPS)
            nc.vector.tensor_reduce(wmean[:, 0], w1[:], AX.X, ALU.add)
            nc.vector.tensor_reduce(wmean[:, 1], w2[:], AX.X, ALU.add)
            nc.vector.tensor_reduce(wmean[:, 2], b2[:], AX.X, ALU.add).then_inc(mean_steps, 1)
            dve.wait_ge(b1_mm, 1)
            nc.vector.tensor_copy(wmean[:, 3], bank[:, 0, 0, :E4]).then_inc(mean_steps, 1)
            dve.wait_ge(mean_steps, 2)
            nc.vector.tensor_scalar(wmean[:], wmean[:], 1.0 / D, None, ALU.mult).then_inc(mean_steps, 1)
            dve.wait_ge(mean_steps, 3)
            for a, k in ((w1, 0), (w2, 1), (b2, 2)):
                nc.vector.tensor_tensor(a[:], a[:], wmean[:, k].unsqueeze(2).broadcast_to([D, E4, D]), ALU.subtract)
            nc.vector.tensor_tensor(b1[:], b1[:], wmean[:, 3], ALU.subtract).then_inc(mean_steps, 1)
            dve.wait_ge(mean_steps, 4)
            def norm(i):
                for u in range(U):
                    dve.wait_ge(x_loaded[u], 16 * (i + 1))
                    moments(nc, dve, x[:, u], NT, stats[:, u], parts[:, u], mean[:, u], power[:, u], s, i * U + u + 1)
                for u in range(U):
                    dve.wait_ge(s["rstd_done"], i * U + u + 1)
                    for t in range(NT):
                        last = nc.vector.tensor_scalar(xn[:, u, t], x[:, u, t], mean[:, u, t:t + 1], rstd[:, u, t:t + 1], ALU.subtract, ALU.mult)
                    last.then_inc(s["norm_done"], 1)

            def gate(i, q):
                for u in range(U):
                    k = i * U + u + 1
                    per_tile = lambda a: a[:, u].unsqueeze(2).broadcast_to([D, NT, E4])
                    per_expert = lambda a: a.unsqueeze(1).broadcast_to([D, NT, E4])
                    dve.wait_ge(s["logits_mm"], k)
                    nc.vector.tensor_tensor(score[:, u], bank[:, u, 1, :NT * E4].rearrange("p (t e) -> p t e", t=NT), per_expert(gb[:]), ALU.add).then_inc(s["score_done"], 1)
                    dve.wait_ge(s["score_done"], k)
                    for n, (src, top, hot) in enumerate(((score, top1, hot1), (left, top2, hot2)), 1):
                        if n == 2:
                            nc.vector.scalar_tensor_tensor(left[:, u], hot1[:, u], -3.0e38, score[:, u], ALU.mult, ALU.add).then_inc(s["left_done"], 1)
                            dve.wait_ge(s["left_done"], k)
                        nc.vector.tensor_reduce(top[:, u], src[:, u], AX.X, ALU.max).then_inc(s[f"top{n}_done"], 1)
                        dve.wait_ge(s[f"top{n}_done"], k)
                        nc.vector.tensor_tensor(eq[:, u], src[:, u], per_tile(top), ALU.is_equal).then_inc(s[f"eq{n}_done"], 1)
                        dve.wait_ge(s[f"eq{n}_done"], k)
                        nc.vector.tensor_tensor(eq[:, u], eq[:, u], per_expert(falling[:]), ALU.mult).then_inc(s[f"eqw{n}_done"], 1)
                        dve.wait_ge(s[f"eqw{n}_done"], k)
                        nc.vector.tensor_reduce(pick[:, u], eq[:, u], AX.X, ALU.max).then_inc(s[f"pick{n}_done"], 1)
                        dve.wait_ge(s[f"pick{n}_done"], k)
                        nc.vector.tensor_tensor(hot[:, u], eq[:, u], per_tile(pick), ALU.is_equal).then_inc(s[f"hot{n}_done"], 1)
                        dve.wait_ge(s[f"hot{n}_done"], k)
                    nc.vector.tensor_tensor(ratio[:, u], top2[:, u], top1[:, u], ALU.subtract).then_inc(s["diff_done"], 1)
                    nc.vector.tensor_tensor(x_sum[:, q, u], x[:, u], xn[:, u], ALU.add).then_inc(s["sum_done"], 1)
                    dve.wait_ge(s["ratio_done"], k)
                    nc.vector.tensor_scalar(w_first[:, u], ratio[:, u], 1.0, None, ALU.add).then_inc(s["den_done"], 1)
                    dve.wait_ge(s["den_done"], k)
                    nc.vector.reciprocal(w_first[:, u], w_first[:, u]).then_inc(s["first_done"], 1)
                    dve.wait_ge(s["first_done"], k)
                    nc.vector.tensor_tensor(w_second[:, u], ratio[:, u], w_first[:, u], ALU.mult).then_inc(s["second_done"], 1)
                    dve.wait_ge(s["second_done"], k)
                    nc.vector.tensor_tensor(hot1[:, u], hot1[:, u], per_tile(w_first), ALU.mult)
                    nc.vector.tensor_tensor(hot2[:, u], hot2[:, u], per_tile(w_second), ALU.mult).then_inc(s["share1_done"], 1)
                    dve.wait_ge(s["share1_done"], k)
                    nc.vector.tensor_tensor(share[:, q, u], hot1[:, u], hot2[:, u], ALU.add).then_inc(s["share_done"], 1)

            def hidden(i, q, more):
                if more:
                    norm(i + 1)
                if not at_start(i):
                    mix(i - 1, 1 - q)
                for u in range(U):
                    dve.wait_ge(s["root_done"], i * U + u + 1)
                    nc.vector.reciprocal(inv[:, u], root[:, u]).then_inc(s["inv_done"], 1)
                for e in range(E4):
                    for u in range(U):
                        dve.wait_ge(s["row_mm"], nth(i, e, u))
                        nc.vector.tensor_tensor(sq[:, u, e], bank[:, u, e % 2], hb[:, u, e], ALU.mult).then_inc(s["scaled_done"], 1)

            def sum_squares(i, t, u):
                dve.wait_ge(s["ysq_done"], nth(i, t, u))
                nc.vector.tensor_reduce(ssq[:, u, t], ysq[:, u].rearrange("p (e f) -> p e f", e=E4), AX.X, ALU.add).then_inc(s["ssq_done"], 1)

            def tail(i, q, more):
                for t in range(NT):
                    for u in range(U):
                        dve.wait_ge(s["y_mm"], nth(i, t, u))
                        nc.vector.tensor_tensor(y[:, u, t], bank[:, u, 2 + t % 2].rearrange("p (e f) -> p e f", e=E4), b2[:], ALU.add).then_inc(s["y_done"], 1)
                    if t:
                        for u in range(U):
                            sum_squares(i, t - 1, u)
                for u in range(U):
                    sum_squares(i, NT - 1, u)
                for u in range(U):
                    dve.wait_ge(s["ssq_done"], nth(i, NT - 1, u))
                    nc.vector.tensor_scalar(ssq[:, u], ssq[:, u], 1.0 / D, LN_EPS, ALU.mult, ALU.add).then_inc(s["var2_done"], 1)
                for u in range(U):
                    k = i * U + u + 1
                    dve.wait_ge(s["std2_done"], k)
                    nc.vector.reciprocal(ssq[:, u], ssq[:, u]).then_inc(s["inv2_done"], 1)
                    dve.wait_ge(s["inv2_done"], k)
                    nc.vector.tensor_tensor(ssq[:, u], ssq[:, u], share[:, q, u], ALU.mult).then_inc(s["factor_done"], 1)

            def mix(i, q):
                for u in range(U):
                    k = i * U + u + 1
                    for t in range(NT):
                        dve.wait_ge(s["gained"], (i * U + u) * NT + t + 1)
                        nc.vector.tensor_reduce(mixed[:, u, t], y[:, u, t].rearrange("p e f -> p f e"), AX.X, ALU.add).then_inc(s["mixed_done"], 1)
                    dve.wait_ge(s["mixed_done"], (i * U + u) * NT + NT)
                    nc.vector.tensor_tensor(mixed[:, u], mixed[:, u], x_sum[:, q, u], ALU.add).then_inc(s["sum2_done"], 1)
                    dve.wait_ge(s["sum2_done"], k)
                    dve.wait_ge(s["offset_mm"], k)
                    if not at_start(i):
                        dve.wait_ge(saved[u], 16 * i)
                    nc.vector.tensor_tensor(x_new[:, u].rearrange("p t f -> p (t f)"), bank[:, u, 0], mixed[:, u].rearrange("p t f -> p (t f)"), ALU.add).then_inc(s["new_done"], 1)

            norm(0)
            gate(0, 0)
            schedule(dve, hidden, gate, tail)
            mix(STEPS - 1, 1)

        @block.tensor
        def _(pe):
            pe.wait_ge(weights_in, LOADS)
            nc.tensor.matmul(bank[:, 0, 0, :E4], ones[:], b1[:], start=True, stop=True).then_inc(b1_mm, 1)
            pe.wait_ge(mean_steps, 4)

            def gate(i, q):
                for u in range(U):
                    pe.wait_ge(s["norm_done"], i * U + u + 1)
                    if not at_start(i):
                        pe.wait_ge(s["scaled_done"], nth(i - 1, 2, u))
                    for t in range(NT):
                        last = nc.tensor.transpose(bank[:, u, 0, t * D:(t + 1) * D], xn[:, u, t], ident[:])
                    last.then_inc(s["turned"], 1)
                for u in range(U):
                    pe.wait_ge(s["xT_done"], i * U + u + 1)
                    if not at_start(i):
                        pe.wait_ge(s["scaled_done"], nth(i - 1, 3, u))
                    for t in range(NT):
                        last = nc.tensor.matmul(bank[:, u, 1, t * E4:(t + 1) * E4], xT[:, u, t * D:(t + 1) * D], gw[:], start=True, stop=True)
                    last.then_inc(s["logits_mm"], 1)

            def hidden_product(i, e):
                for u in range(U):
                    if e > 1:
                        pe.wait_ge(s["sq_done"], nth(i, e - 2, u))
                    elif not at_start(i):
                        pe.wait_ge(s["y_done"], nth(i - 1, NT - 2 + e, u))
                    nc.tensor.matmul(bank[:, u, 2 + e % 2], w1[:, e], xT[:, u], start=True, stop=True).then_inc(s["hid_mm"], 1)

            def variances(i, e):
                for u in range(U):
                    pe.wait_ge(s["sq_done"], nth(i, e, u))
                    if e == 0:
                        pe.wait_ge(s["score_done"], i * U + u + 1)
                        if not at_start(i):
                            pe.wait_ge(s["shareT_done"], (i - 1) * U + u + 1)
                    for t in range(NT):
                        last = nc.tensor.matmul(bank[:, u, 1, VAR + e * NT + t:VAR + e * NT + t + 1], sq[:, u, e, t * D:(t + 1) * D], ones[:, :1], start=True, stop=True)
                    last.then_inc(s["var_mm"], 1)

            def hidden(i, q, more):
                hidden_product(i, 0)
                for e in range(E4):
                    if e + 1 < E4:
                        hidden_product(i, e + 1)
                    variances(i, e)
                for e in range(E4):
                    for u in range(U):
                        pe.wait_ge(s["diag_done"], nth(i, e, u))
                        if e > 1:
                            pe.wait_ge(s["scaled_done"], nth(i, e - 2, u))
                        elif e == 0 and not at_start(i):
                            pe.wait_ge(s["new_done"], (i - 1) * U + u + 1)
                        nc.tensor.matmul(bank[:, u, e % 2], ones[:], diag[:, u, e].rearrange("p t k -> p (t k)"), start=True, stop=True).then_inc(s["row_mm"], 1)

            def tail(i, q, more):
                for t in range(NT):
                    for u in range(U):
                        if t == 0:
                            pe.wait_ge(s["hid_done"], nth(i, E4 - 1, u))
                        elif t > 1:
                            pe.wait_ge(s["y_done"], nth(i, t - 2, u))
                        for e in range(E4):
                            last = nc.tensor.matmul(bank[:, u, 2 + t % 2, e * D:(e + 1) * D], hid[:, u, e, t * D:(t + 1) * D], w2[:, e], start=True, stop=True)
                        last.then_inc(s["y_mm"], 1)
                for u in range(U):
                    k = i * U + u + 1
                    pe.wait_ge(s["share_done"], k)
                    if more:
                        pe.wait_ge(s["score_done"], k + U)
                    for t in range(NT):
                        last = nc.tensor.transpose(bank[:E4, u, 1, t * D:(t + 1) * D], share[:, q, u, t], ident[:])
                    last.then_inc(s["share_turned"], 1)
                for u in range(U):
                    k = i * U + u + 1
                    pe.wait_ge(s["shareT_done"], k)
                    for t in range(NT):
                        last = nc.tensor.matmul(bank[:, u, 0, t * D:(t + 1) * D], shareT[:, u, t * D:(t + 1) * D], be2[:], start=True, stop=True)
                    last.then_inc(s["offset_mm"], 1)

            gate(0, 0)
            schedule(pe, hidden, gate, tail)


def combine(nc, ph, x_in, ye, x_out):
    RING = 4
    with ExitStack() as ctx:
        m = Space(nc, ctx, ph)
        x, y = (m.sb(n, [D, RING, NT, D]) for n in ("x", "y"))
        added = m.sem("added")
        loaded, saved = ([m.sem(f"{n}{r}") for r in range(RING)] for n in ("loaded", "saved"))
        block = ctx.enter_context(nc.Block())
        TURNS = GROUPS // RING

        @block.sync
        def _(sp):
            def turn(i):
                for r in range(RING):
                    if not at_start(i):
                        sp.wait_ge(saved[r], 16 * i)
                    sp.dma_start(x[:, r], rows(x_in, (i * RING + r) * GROUP)).then_inc(loaded[r], 16)
                    sp.dma_start(y[:, r], rows(ye, (i * RING + r) * GROUP)).then_inc(loaded[r], 16)

            turns(sp, TURNS, turn)

        @block.vector
        def _(dve):
            def turn(i):
                for r in range(RING):
                    dve.wait_ge(loaded[r], 32 * (i + 1))
                    nc.vector.tensor_tensor(x[:, r], y[:, r], x[:, r], ALU.add).then_inc(added, 1)

            turns(dve, TURNS, turn)

        @block.scalar
        def _(act):
            def turn(i):
                for r in range(RING):
                    act.wait_ge(added, i * RING + r + 1)
                    act.dma_start(rows(x_out, (i * RING + r) * GROUP), x[:, r]).then_inc(saved[r], 16)

            turns(act, TURNS, turn)
            for r in range(RING):
                act.wait_ge(saved[r], 16 * TURNS)


def build(nc, t, x, out):
    def scratch(name, shape, dt=F32):
        return nc.dram_tensor(name, shape, dt).ap()

    x1, x2, x3, x4, x5, x6 = (scratch(f"x_{n}", (TOKENS, D)) for n in range(1, 7))
    xe, ye = scratch("expert_in", (XE_ROWS, XE_COLS)), scratch("expert_out", (YE_ROWS, D))
    prob, table = scratch("prob", (D, TOKENS // D)), scratch("table", (1, 2 * SLOTS), I32)
    part = lambda prefix: {k[len(prefix):]: v for k, v in t.items() if k.startswith(prefix)}
    expert = lambda prefix: [t[prefix + k] for k in ("w1", "b1", "w2", "b2")]

    slot_attention(nc, t, x, t["ctx"], x1)
    route(nc, t, "route0", x1, "cosine", xe, prob, table, True)
    experts(nc, t, "experts0", xe, table, expert("L0f_"), ye, True)

    w = part("L1a_")
    w["norm"] = (w["qn"], w["kn"])
    attention(nc, t, "att1", 1, x1, t["ctx"], w, x2, (ye, prob))
    layernorm_experts(nc, t, "lnx1", x2, part("L1f_"), x3)

    attention(nc, t, "att2", 2, x3, t["ctx"], part("L2a_"), x4, None)
    route(nc, t, "route2", x4, (t["L2f_gw"], t["L2f_gb"]), xe, prob, table, True)
    experts(nc, t, "experts2", xe, table, expert("L2f_"), ye, False)

    attention(nc, t, "att3", 3, x4, t["ctx"], part("L3a_"), x5, (ye, prob))
    route(nc, t, "route3", x5, (t["L3f_gw"], t["L3f_gb"]), xe, prob, table, False)
    experts(nc, t, "experts3", xe, table, expert("L3f_"), ye, False)
    combine(nc, "combine3", x5, ye, out)


def rope_tables():
    out = np.zeros((D, 4, HD), np.float32)
    for k, (theta, scale) in enumerate(((32.0, HD ** -0.5), (1000.0, 1.0))):
        freqs = np.float32(theta) ** (-np.arange(0, HD, 2, dtype=np.float32) / HD)
        angle = np.arange(S, dtype=np.float32)[:, None] * freqs[None, :]
        cos, sin = np.cos(angle), np.sin(angle)
        out[:, 2 * k] = np.tile(np.concatenate([cos, cos], 1), (2, 1)) * scale
        out[:, 2 * k + 1] = np.tile(np.concatenate([-sin, sin], 1), (2, 1)) * scale
    return out


def constants():
    ar = np.arange
    return {
        "ident": np.eye(D, dtype=np.float32),
        "ones": np.ones((D, D), np.float32),
        "pair_ones": np.kron(np.eye(2, dtype=np.float32), np.ones((S, S), np.float32)),
        "pair_ident": np.tile(np.eye(S, dtype=np.float32), (2, 1)),
        "before": np.triu(np.ones((D, D), np.float32), 1),
        "falling": np.tile(ar(E, 0, -1, dtype=np.float32), (D, 1)),
        "steps": np.tile(ar(TOKENS // SLOT, dtype=np.float32) * SLOT, (D, 1)),
        "token_no": (np.arange(TOKENS // D + FILLS * SLOT_TILES)[None] * D + np.arange(D)[:, None]).astype(np.int32),
        "expert_row": np.tile(ar(E, dtype=np.float32) * EXPERT_ROWS, (D, 1)),
        "slot_no": np.tile(ar(SLOTS, dtype=np.float32), (D, 1)),
        "n_mask": (((ar(D) // HD) % 8)[:, None] == ar(8)[None]).astype(np.float32),
        "rope": rope_tables(),
        "zero_row": np.zeros((1, E), np.float32),
    }


def layout(a):
    col = lambda v: v.reshape(D, 1)
    row = lambda v: v.reshape(1, -1)
    chunks = lambda b: b.reshape(E, 4, D).transpose(0, 2, 1).reshape(E * D, 4)
    second = lambda w: w.reshape(E, 4, D, D).transpose(0, 2, 1, 3).reshape(E * D, 4 * D)
    t = {
        "ctx": a["ctx_1024"].reshape(TOKENS, D),
        "L0_Wk": a["L0_xattn_Wk"], "L0_Wq": a["L0_xattn_Wq"], "L0_Wv": a["L0_xattn_Wv"],
        "L0_wihT": a["L0_xattn_gru_wih"].T, "L0_whhT": a["L0_xattn_gru_whh"].T,
        "L0_bih": a["L0_xattn_gru_bih"].reshape(3, D).T, "L0_bhh": a["L0_xattn_gru_bhh"].reshape(3, D).T,
        "L0_w_slot": col(a["L0_xattn_slot_norm_w"]), "L0_w_in": col(a["L0_xattn_input_norm_w"]),
        "L0_w_redT": a["L0_ffn_w_red"].T, "L0_wg": a["L0_ffn_wg"],
        "L0f_w1": a["L0_ffn_w1"].reshape(E * D, -1), "L0f_b1": chunks(a["L0_ffn_b1"]),
        "L0f_w2": second(a["L0_ffn_w2"]), "L0f_b2": a["L0_ffn_b2"],
        "L1a_q": a["L1_xattn_Wq"].T, "L1a_k": a["L1_xattn_Wk"].T, "L1a_v": a["L1_xattn_Wv"].T, "L1a_o": a["L1_xattn_Wo"].T,
        "L1a_qn": row(a["L1_xattn_q_norm_w"]), "L1a_kn": row(a["L1_xattn_k_norm_w"]),
        "L1f_gate_W": a["L1_ffn_gate_W"], "L1f_gate_b": row(a["L1_ffn_gate_b"]),
        "L1f_W1": a["L1_ffn_W1"].reshape(E4 * D, D), "L1f_W2": a["L1_ffn_W2"].reshape(E4 * D, D),
        "L1f_b1T": a["L1_ffn_b1"].T, "L1f_g1T": a["L1_ffn_g1"].T, "L1f_be1T": a["L1_ffn_be1"].T,
        "L1f_b2": row(a["L1_ffn_b2"]), "L1f_g2": row(a["L1_ffn_g2"]), "L1f_be2": a["L1_ffn_be2"],
        "L2a_q": a["L2_xattn_W_q"], "L2a_k": a["L2_xattn_W_k"], "L2a_v": a["L2_xattn_W_v"], "L2a_o": a["L2_xattn_W_o"],
        "L2a_bq": col(a["L2_xattn_b_q"]), "L2a_bk": col(a["L2_xattn_b_k"]), "L2a_bv": row(a["L2_xattn_b_v"]),
        "L2a_bo": row(a["L2_xattn_b_o"]), "L2a_mask": np.ascontiguousarray(a["mask_SxS2_bk1"]).view(np.uint32),
        "L2f_gw": a["L2_ffn_router_W"], "L2f_gb": row(a["L2_ffn_router_b"]),
        "L2f_w1": a["L2_ffn_W1"].reshape(E * D, -1), "L2f_b1": chunks(a["L2_ffn_b1"]),
        "L2f_w2": second(a["L2_ffn_W2"]), "L2f_b2": a["L2_ffn_b2"],
        "L3a_q": a["L3_xattn_Wq"].T, "L3a_k": a["L3_xattn_Wk"].T, "L3a_v": a["L3_xattn_Wv"].T,
        "L3a_bq": col(a["L3_xattn_bq"]), "L3a_bk": col(a["L3_xattn_bk"]), "L3a_bv": row(a["L3_xattn_bv"]),
        "L3f_gw": a["L3_ffn_gate_w"].T, "L3f_gb": row(a["L3_ffn_gate_b"]),
        "L3f_w1": a["L3_ffn_w1"].transpose(0, 2, 1).reshape(E * D, -1), "L3f_b1": chunks(a["L3_ffn_b1"]),
        "L3f_w2": second(a["L3_ffn_w2"].transpose(0, 2, 1)), "L3f_b2": a["L3_ffn_b2"],
    }
    return {k: np.ascontiguousarray(v) for k, v in t.items()}


def kernel(**inputs):
    import concourse.bacc as bacc
    from concourse.bass_utils import run_bass_kernel_spmd

    a = {k: np.asarray(v) for k, v in inputs.items()}
    arrays = {"x": a["x"].reshape(TOKENS, D), **layout(a), **constants()}
    nc = bacc.Bacc("TRN2", target_bir_lowering=False, num_devices=1)
    t = {k: nc.dram_tensor(f"in_{k}", v.shape, mybir.dt.from_np(v.dtype), kind="ExternalInput").ap() for k, v in arrays.items()}
    out = nc.dram_tensor("out", (TOKENS, D), F32, kind="ExternalOutput").ap()
    build(nc, t, t["x"], out)
    r = run_bass_kernel_spmd(nc, [{f"in_{k}": v for k, v in arrays.items()}], core_ids=[0])
    return r.results[0]["out"].reshape(a["x"].shape)
```
